# Optimizing a Trainium2 kernel written in Bass

```python
import numpy as np
import jax
import jax.numpy as jnp

def _softmax(x, axis=-1):
    return jax.nn.softmax(x, axis=axis)
def _gelu(x):
    return jax.nn.gelu(x, approximate=True)
def _silu(x):
    return jax.nn.silu(x)
def _sigmoid(x):
    return jax.nn.sigmoid(x)
def _layernorm(x, axis=-1, eps=1e-5):
    m = jnp.mean(x, axis=axis, keepdims=True)
    v = jnp.var(x, axis=axis, keepdims=True)
    return (x - m) / jnp.sqrt(v + eps)
def _scatter_add(tgt, idx, src, axis=0):
    return tgt.at[idx].add(src)
def _segment_sum(src, seg, n):
    return jax.ops.segment_sum(src, seg, n)

kernel_name = 'mk_metaformer_d1_conv_nchw256_95ed28'

def setup_inputs(seed: int = 0):
    np.random.seed(seed)
    _w = jnp.asarray
    def _rec_inputs():
        import jax
        import jax.numpy as jnp
        _gk = jax.random.key(seed)
        x = -0.0006537 + 1.001 * jax.random.normal(jax.random.fold_in(_gk, 1), (1, 256, 96, 96), jnp.float32)
        return x
    x = _rec_inputs()
    def _L0_conv_setup():
        import jax, jax.numpy as jnp
        import numpy as np
        CUTOFF = 0.05

        def _freq_filter(x_chw, filter_type):
            x = jax.lax.stop_gradient(x_chw)
            C, H, W = x.shape
            a = jnp.abs(x)
            mn = a.min(axis=(1, 2), keepdims=True)
            ptp = a.max(axis=(1, 2), keepdims=True) - mn
            q = jnp.floor(255.0 * (a - mn) / ptp)
            f = jnp.fft.fftshift(jnp.fft.fft2(q), axes=(-2, -1))
            crow, ccol = (H // 2, W // 2)
            dr, dc = (int(CUTOFF * crow), int(CUTOFF * ccol))
            m = jnp.zeros((H, W), dtype=q.dtype)
            m = m.at[crow - dr:crow + dr, ccol - dc:ccol + dc].set(1.0)
            if filter_type == 'low_pass':
                m = 1.0 - m
            out = jnp.abs(jnp.fft.ifft2(jnp.fft.ifftshift(f * m, axes=(-2, -1))))
            return out.astype(x_chw.dtype)

        def _conv1x1(x, w, b):
            return jnp.einsum('oc,bchw->bohw', w, x) + b[None, :, None, None]
        key = jax.random.key(seed)
        ks = jax.random.split(key, 7)
        B, C, H, W = (1, 256, 96, 96)
        fuse = jax.random.normal(ks[0], (B, C, H, W), dtype=jnp.float32)
        s = 1.0 / np.sqrt(C)
        Wq = jax.random.normal(ks[1], (C, C), dtype=jnp.float32) * s
        bq = jax.random.normal(ks[2], (C,), dtype=jnp.float32) * 0.01
        Wk = jax.random.normal(ks[3], (C, C), dtype=jnp.float32) * s
        bk = jax.random.normal(ks[4], (C,), dtype=jnp.float32) * 0.01
        Wv = jax.random.normal(ks[5], (C, C), dtype=jnp.float32) * s
        bv = jax.random.normal(ks[6], (C,), dtype=jnp.float32) * 0.01
        return {'fuse': fuse, 'Wq': Wq, 'bq': bq, 'Wk': Wk, 'bk': bk, 'Wv': Wv, 'bv': bv}
    _L0_conv_all = _L0_conv_setup()
    _L0_conv_in = {k: v for k, v in _L0_conv_all.items() if k in ('Wq', 'bq', 'Wk', 'bk', 'Wv', 'bv', )}
    del _L0_conv_all

    def _L0_ffn_setup():
        import jax, jax.numpy as jnp
        import numpy as np
        B, S, D = (8, 4096, 256)
        H = 4 * D
        CAPACITY = 0.5
        key = jax.random.key(seed)
        ks = jax.random.split(key, 6)
        x = jax.random.normal(ks[0], (B, S, D), dtype=jnp.float32)
        attention_mask = jnp.zeros((B, 1, 1, S), dtype=jnp.float32)
        wr = jax.random.normal(ks[1], (D, 1), dtype=jnp.float32) * 0.02
        br = jnp.zeros((1,), dtype=jnp.float32)
        w1 = jax.random.normal(ks[2], (D, H), dtype=jnp.float32) * 0.02
        b1 = jnp.zeros((H,), dtype=jnp.float32)
        w2 = jax.random.normal(ks[3], (H, D), dtype=jnp.float32) * 0.02
        b2 = jnp.zeros((D,), dtype=jnp.float32)
        return {'x': x, 'attention_mask': attention_mask, 'wr': wr, 'br': br, 'w1': w1, 'b1': b1, 'w2': w2, 'b2': b2}
    _L0_ffn_all = _L0_ffn_setup()
    _L0_ffn_in = {k: v for k, v in _L0_ffn_all.items() if k in ('attention_mask', 'wr', 'br', 'w1', 'b1', 'w2', 'b2', )}
    del _L0_ffn_all

    return {
        "x": x,
        "L0_conv_Wq": _L0_conv_in["Wq"],
        "L0_conv_bq": _L0_conv_in["bq"],
        "L0_conv_Wk": _L0_conv_in["Wk"],
        "L0_conv_bk": _L0_conv_in["bk"],
        "L0_conv_Wv": _L0_conv_in["Wv"],
        "L0_conv_bv": _L0_conv_in["bv"],
        "L0_ffn_attention_mask": _L0_ffn_in["attention_mask"],
        "L0_ffn_wr": _L0_ffn_in["wr"],
        "L0_ffn_br": _L0_ffn_in["br"],
        "L0_ffn_w1": _L0_ffn_in["w1"],
        "L0_ffn_b1": _L0_ffn_in["b1"],
        "L0_ffn_w2": _L0_ffn_in["w2"],
        "L0_ffn_b2": _L0_ffn_in["b2"],
    }

def reference(x, L0_conv_Wq, L0_conv_bq, L0_conv_Wk, L0_conv_bk, L0_conv_Wv, L0_conv_bv, L0_ffn_attention_mask, L0_ffn_wr, L0_ffn_br, L0_ffn_w1, L0_ffn_b1, L0_ffn_w2, L0_ffn_b2):
    import jax
    import jax.numpy as jnp
    def _L0_conv_ref(fuse, Wq, bq, Wk, bk, Wv, bv):
        import jax, jax.numpy as jnp
        import numpy as np
        CUTOFF = 0.05

        def _freq_filter(x_chw, filter_type):
            x = jax.lax.stop_gradient(x_chw)
            C, H, W = x.shape
            a = jnp.abs(x)
            mn = a.min(axis=(1, 2), keepdims=True)
            ptp = a.max(axis=(1, 2), keepdims=True) - mn
            q = jnp.floor(255.0 * (a - mn) / ptp)
            f = jnp.fft.fftshift(jnp.fft.fft2(q), axes=(-2, -1))
            crow, ccol = (H // 2, W // 2)
            dr, dc = (int(CUTOFF * crow), int(CUTOFF * ccol))
            m = jnp.zeros((H, W), dtype=q.dtype)
            m = m.at[crow - dr:crow + dr, ccol - dc:ccol + dc].set(1.0)
            if filter_type == 'low_pass':
                m = 1.0 - m
            out = jnp.abs(jnp.fft.ifft2(jnp.fft.ifftshift(f * m, axes=(-2, -1))))
            return out.astype(x_chw.dtype)

        def _conv1x1(x, w, b):
            return jnp.einsum('oc,bchw->bohw', w, x) + b[None, :, None, None]
        B, C, H, W = fuse.shape
        scale = 1.0 / C ** 0.5
        FQ = jnp.broadcast_to(_freq_filter(fuse[0], 'high_pass'), fuse.shape)
        FK = jnp.broadcast_to(_freq_filter(fuse[0], 'low_pass'), fuse.shape)
        fuse_Query = _conv1x1(FQ, Wq, bq).reshape(B, C, H * W)
        fuse_Q_mask = fuse_Query.reshape(B * H, C * W)
        fuse_Query_t = jnp.transpose(fuse_Query, (0, 2, 1))
        fuse_Key = _conv1x1(FK, Wk, bk).reshape(B, C, H * W)
        Fuse_Q_mask = jnp.max(fuse_Q_mask, axis=0, keepdims=True)
        mask_KQ = jnp.einsum('bnc,bcm->bnm', fuse_Query_t, fuse_Key) * scale
        mask_KQ = jax.nn.softmax(mask_KQ, axis=0)
        mask_KQ = jnp.max(mask_KQ, axis=1)
        mask_KQ = mask_KQ.reshape(-1, W)
        mask_KQ = jnp.max(mask_KQ, axis=-1, keepdims=True)
        mask = (mask_KQ @ Fuse_Q_mask).reshape(B, C, H, W)
        fuse_Value = _conv1x1(fuse, Wv, bv)
        return fuse_Value + fuse_Value * mask

    def _L0_ffn_ref(x, attention_mask, wr, br, w1, b1, w2, b2):
        import jax, jax.numpy as jnp
        import numpy as np
        B, S, D = (8, 4096, 256)
        H = 4 * D
        CAPACITY = 0.5
        b, s, d = x.shape
        weights = (jnp.einsum('bsd,do->bso', x, wr) + br)[..., 0]
        k = max(1, int(CAPACITY * s))
        kk = k - 1 if k > 1 else 1
        _, idx = jax.lax.top_k(weights, k)
        sel_idx = idx[:, :kk]
        sel = jnp.take_along_axis(x, sel_idx[:, :, None], axis=1)
        h = jax.nn.gelu(jnp.einsum('bkd,dh->bkh', sel, w1) + b1)
        y = jnp.einsum('bkh,hd->bkd', h, w2) + b2
        w_sel = jnp.take_along_axis(weights, sel_idx, axis=1)
        y = y * w_sel[..., None]
        batch_idx = jnp.arange(b)[:, None]
        processed = jnp.zeros_like(x).at[batch_idx, sel_idx].set(y)
        return processed + x

    def _gn(v, G=32, eps=1e-5):
        B_, C_, H_, W_ = v.shape
        g = v.reshape(B_, G, C_ // G, H_, W_)
        m = jnp.mean(g, axis=(2, 3, 4), keepdims=True)
        s = jnp.var(g, axis=(2, 3, 4), keepdims=True)
        return ((g - m) / jnp.sqrt(s + eps)).reshape(v.shape)

    def _ln_c(v, eps=1e-6):
        m = jnp.mean(v, axis=1, keepdims=True)
        s = jnp.var(v, axis=1, keepdims=True)
        return (v - m) / jnp.sqrt(s + eps)

    def _ln_t(v, eps=1e-5):
        m = jnp.mean(v, axis=-1, keepdims=True)
        s = jnp.var(v, axis=-1, keepdims=True)
        return (v - m) / jnp.sqrt(s + eps)

    def _to_tokens(v):
        B_, C_, H_, W_ = v.shape
        return v.reshape(B_, C_, H_ * W_).transpose(0, 2, 1)
    def _from_tokens(t, like):
        B_, C_, H_, W_ = like.shape
        return t.transpose(0, 2, 1).reshape(B_, C_, H_, W_)

    x = x + _L0_conv_ref(_ln_c(x), L0_conv_Wq, L0_conv_bq, L0_conv_Wk, L0_conv_bk, L0_conv_Wv, L0_conv_bv)
    t = _to_tokens(x)
    t = t + _L0_ffn_ref(_ln_t(t), L0_ffn_attention_mask, L0_ffn_wr, L0_ffn_br, L0_ffn_w1, L0_ffn_b1, L0_ffn_w2, L0_ffn_b2)
    x = _from_tokens(t, x)
    return x


_drawn_inputs = setup_inputs


def setup_inputs(seed=0):
    import zlib

    import numpy as np

    out = dict(_drawn_inputs(seed))
    spreads = {'L0_ffn_b1': (0.0, 0.8), 'L0_ffn_b2': (0.0, 0.8)}
    factors = {'L0_conv_bq': 8.0,
     'L0_conv_bv': 5.402,
     'L0_ffn_wr': 8.0,
     'L0_ffn_w1': 8.0,
     'L0_ffn_w2': 8.0}
    for name, (base, spread) in spreads.items():
        noise = np.random.default_rng([zlib.crc32(name.encode()), seed]).standard_normal(out[name].shape)
        drawn = base * np.exp(spread * noise) if base else spread * noise
        out[name] = jnp.asarray(drawn.astype(out[name].dtype))
    for name, factor in factors.items():
        out[name] = (out[name] * factor).astype(out[name].dtype)
    return out
```

```python
import concourse.bass as bass
from concourse import mybir
from contextlib import ExitStack
import numpy as np

P = 128
C = 256
HALVES = C // P
SIDE = 96
PIX = SIDE * SIDE
THIRDS = 3
COLS = PIX // THIRDS // P
STEPS = 6
TPC = COLS // STEPS
CHUNK = TPC * P
NCHUNK = THIRDS * STEPS
TILES = THIRDS * COLS
TPS = THIRDS * TPC
GROUPS = 8
HID = 1024
HT = HID // P
KEEP = PIX // 2 - 1
FT = (KEEP + P - 1) // P
FSTEPS = FT // TPS
ROW = C + 4
EPS_C, EPS_T = 1e-6, 1e-5
MAGIC = float(2 ** 23)
HALF = 0.5 - 2.0 ** -15
DIGIT = 3
SHIFTS = list(range(28, 0, -DIGIT)) + [0]
CAND = 1 << DIGIT
NOSLOT = 8191


def frequencies():
    pairs = [(0, 1), (1, 0), (1, 1), (1, -1)]
    lone = [(-2, v) for v in range(-2, 2)] + [(u, -2) for u in range(-1, 2)]
    return pairs, lone


NFUN = 23


def parts_of_products(n_exact, n):
    rows = []
    for i in range(n):
        for a, b in ((0, 0), (0, 1), (1, 0), (1, 1), (0, 2), (2, 0)):
            if i >= n_exact or b == 0:
                rows.append((i, a, b))
    return rows


REAL_ROWS = parts_of_products(1, NFUN)
IMAG_ROWS = parts_of_products(0, 14)
R1 = P
R2 = len(REAL_ROWS) - P
RI = len(IMAG_ROWS)
R2_AT = 96

CF = {}
at = 0
for name, width in (("ident", P), ("sel_r1", P), ("sel_r2", P), ("sel_im", P), ("mask_r1", 3), ("mask_r2", 3),
                    ("mask_im", 3), ("mask_b", 3), ("id_hi", TILES), ("id_lo", TILES), ("magic", 1)):
    CF[name] = (at, at + width)
    at += width
NCF = at
CB = {"ones": (0, P), "tri": (P, 2 * P), "iota": (2 * P, 3 * P)}
NCB = 3 * P


def layer_kernel(nc, x, wq, wv, bias, wr, br, w1, b1, w2, const_f, const_i, const_b, fwd_basis,
                 inv_basis, out):
    f32, bf16, i32 = mybir.dt.float32, mybir.dt.bfloat16, mybir.dt.int32
    u32 = mybir.dt.uint32
    ALU = mybir.AluOpType
    ACT = mybir.ActivationFunctionType
    AX = mybir.AxisListType

    table = nc.dram_tensor("token_table", [PIX, ROW], f32, kind="Internal").ap()

    def by_step(ap):
        return ap.rearrange("(b p k j) n -> b k p (j n)", b=THIRDS, p=P, k=STEPS)

    x_v, out_v, table_v = by_step(x), by_step(out), by_step(table)

    ctx = ExitStack()
    with ctx:
        def sb(name, shape, dt=f32):
            return ctx.enter_context(nc.sbuf_tensor(name, shape, dt))

        def sem(name):
            return ctx.enter_context(nc.semaphore(name))

        rows = sb("rows", [P, THIRDS, COLS, ROW])
        vcm = sb("vcm", [P, THIRDS, STEPS, HALVES * CHUNK])
        arena = sb("arena", [P, 10752])
        wq_s = sb("wq_s", [P, HALVES, C])
        wv_s = sb("wv_s", [P, HALVES, C])
        cf = sb("cf", [P, NCF])
        ci = sb("ci", [P, len(SHIFTS), CAND], i32)
        cb = sb("cb", [P, NCB], bf16)
        wr_s = sb("wr_s", [P, C])
        br_s = sb("br_s", [P, 1])
        b1_s = sb("b1_s", [P, HT])
        bias_f = sb("bias_f", [3, 3 * C])
        bias_s = sb("bias_s", [3, 3 * C], bf16)
        stats = sb("stats", [P, TPS, 6])
        mean = sb("mean_s", [P, TPS])[:, :]
        small = sb("small", [P, 14, TPS])
        ext = sb("ext", [P, 2, HALVES, NCHUNK])
        fin = sb("fin", [P, 6, HALVES])
        coef_r1 = sb("coef_r1", [P, C], bf16)
        coef_r2 = sb("coef_r2", [P, C], bf16)
        coef_im = sb("coef_im", [P, C], bf16)
        qmax = sb("qmax", [P, TPC, GROUPS, THIRDS])
        gate = sb("gate", [P, TPC, THIRDS * GROUPS])
        qm = sb("qm", [P, TPC, GROUPS])
        w_all = sb("w_all", [P, TILES])
        junk = sb("junk", [P, 1])
        unused = sb("unused", [P, TPC, C], bf16)
        idx = sb("idx", [P, FT], i32)
        idx_s = sb("idx_s", [P, THIRDS, TPC], i32)
        ps = ctx.enter_context(nc.psum_tensor("ps", [P, 8, 512], f32))

        def const(name):
            return cf[:, CF[name][0]:CF[name][1]]

        def constb(name):
            return cb[:, CB[name][0]:CB[name][1]]

        ident = const("ident")

        def words(at_, *dims, dt=f32):
            n = int(np.prod(dims))
            flat = arena[:, at_:at_ + (n if dt != bf16 else n // 2)]
            if dt != f32:
                flat = flat.bitcast(dt)
            return flat

        v_tok = [words(1024 * b, TPC, C).rearrange("p (j c) -> p j c", c=C) for b in range(THIRDS)]
        absv = [words(1024 * b, 1024) for b in range(THIRDS)]
        lev = [words(3072 + 1024 * b, 1024) for b in range(THIRDS)]
        q_tok = [words(6144 + 512 * b, TPC, C, dt=bf16).rearrange("p (j c) -> p j c", c=C) for b in range(THIRDS)]
        fwd = words(7680, TILES, 3 * NFUN, dt=bf16).rearrange("p (t m) -> p t m", m=3 * NFUN)
        sums = words(0, C)[0:3 * NFUN, :]
        resid = [words(256 + 256 * i, C) for i in range(3)]
        part = [words(1024 + 128 * i, C, dt=bf16) for i in range(3)]
        picked = [words(2048 + 256 * i, C) for i in range(2)]
        v_st = [words(1024 * b, 1024) for b in range(THIRDS)]
        gated = [words(3072 + 1024 * b, 1024) for b in range(THIRDS)]
        squares = [words(6144 + 1024 * h, 1024).rearrange("p (r n) -> p r n", r=2) for h in range(HALVES)]
        mag = words(8192, 1024)
        inv = [words(9216 + 512 * b, 1024, dt=bf16).rearrange("p (s n) -> p s n", s=2) for b in range(THIRDS)]
        u_w = words(0, TILES)
        cmp_t = words(128, CAND * TILES).rearrange("p (j t) -> p j t", j=CAND)
        cand = [words(768 + 8 * i, CAND, dt=i32) for i in range(2)]
        passed = words(800, CAND, dt=i32)
        masked = words(816, CAND, dt=i32)
        prefix = words(832, 1, dt=i32)
        cnt_f = words(840, CAND)
        cnt_b = words(848, CAND, dt=bf16)
        sc4 = words(860, 16)
        gt_m, eq_m, rank_t, sel_t, tmp_t = (words(900 + 80 * i, TILES) for i in range(5))
        ones_t = words(1300, TILES)
        slot_i, hi_i, lo_i = (words(1400 + 80 * i, TILES, dt=i32) for i in range(3))
        hi_f, lo_f = words(1640, TILES), words(1720, TILES)
        oh_lo = words(1800, TILES, P, dt=bf16).rearrange("p (t s) -> p t s", s=P)
        oh_hi = words(6500, TILES, FT, dt=bf16).rearrange("p (t s) -> p t s", s=FT)
        oh_id = words(8000, TILES, 2 * FT, dt=bf16).rearrange("p (t s) -> p t s", s=2 * FT)

        flat_v = vcm[:, :, :, :].rearrange("p b k n -> p (b k n)")
        flat_r = rows[:, :, :, :].rearrange("p b k n -> p (b k n)")
        w1_s = flat_v[:, 0:2048].rearrange("p (h n) -> p h n", h=HALVES)
        w2_s = flat_v[:, 2048:4096].rearrange("p (t n) -> p t n", t=HT)
        got = [flat_v[:, 4096 + 1040 * b:4096 + 1040 * (b + 1)].rearrange("p (j n) -> p j n", j=TPC) for b in range(THIRDS)]
        ln_tok = [flat_v[:, 7296 + 1024 * b:7296 + 1024 * (b + 1)].rearrange("p (j c) -> p j c", c=C) for b in range(THIRDS)]
        ln_ch = [flat_v[:, 10368 + 1024 * b:10368 + 1024 * (b + 1)].rearrange("p (h n) -> p h n", h=HALVES) for b in range(THIRDS)]
        base5 = [flat_v[:, 13440 + 1024 * b:13440 + 1024 * (b + 1)].rearrange("p (j c) -> p j c", c=C) for b in range(THIRDS)]
        hid = [flat_r[:, 4096 * b:4096 * (b + 1)].rearrange("p (t n) -> p t n", t=HT) for b in range(THIRDS)]
        res5 = [flat_r[:, 12288 + 1024 * b:12288 + 1024 * (b + 1)].rearrange("p (j c) -> p j c", c=C) for b in range(THIRDS)]

        consts_in = sem("consts_in")
        fwd_in = sem("fwd_in")
        x_in = [sem(f"x_in{b}") for b in range(THIRDS)]
        s1_stats = sem("s1_stats")
        s1_sd = sem("s1_sd")
        s1_norm = sem("s1_norm")
        s1_vtok = sem("s1_vtok")
        s1_tr = sem("s1_tr")
        s1_vcm = sem("s1_vcm")
        s1_ext = sem("s1_ext")
        s1_scale = sem("s1_scale")
        s2_abs = sem("s2_abs")
        s2_lev = sem("s2_lev")
        s2_tr = sem("s2_tr")
        s2_q = sem("s2_q")
        s2_dft = sem("s2_dft")
        s2_split = sem("s2_split")
        s2_sums = sem("s2_sums")
        s2_coef = sem("s2_coef")
        s2_done = sem("s2_done")
        inv_in = [sem(f"inv_in{b}") for b in range(THIRDS)]
        s3_ri = sem("s3_ri")
        s3_sq = sem("s3_sq")
        s3_sum = sem("s3_sum")
        s3_mag = sem("s3_mag")
        s3_q = sem("s3_q")
        s3_qmax = sem("s3_qmax")
        s3_qsteps = sem("s3_qsteps")
        s3_gate = sem("s3_gate")
        s3_vst = sem("s3_vst")
        s3_v = sem("s3_v")
        s3_gated = sem("s3_gated")
        s3_x1 = sem("s3_x1")
        s3_stats = sem("s3_stats")
        s3_sd = sem("s3_sd")
        s3_tail = sem("s3_tail")
        s3_w = sem("s3_w")
        s3_wsteps = sem("s3_wsteps")
        s3_rows = sem("s3_rows")
        s3_base = sem("s3_base")
        base_out = sem("base_out")
        table_out = sem("table_out")
        s4_step = sem("s4_step")
        s4_cnt = sem("s4_cnt")
        s4_tot = sem("s4_tot")
        s4_hot = sem("s4_hot")
        s4_ids = sem("s4_ids")
        s4_idx = sem("s4_idx")
        w_in = sem("w_in")
        s5_idx = sem("s5_idx")
        got_in = [sem(f"got_in{b}") for b in range(THIRDS)]
        s5_ln = sem("s5_ln")
        s5_tr = sem("s5_tr")
        s5_lnch = sem("s5_lnch")
        s5_base = sem("s5_base")
        s5_h = sem("s5_h")
        s5_gelu = sem("s5_gelu")
        s5_y = sem("s5_y")
        s5_res = sem("s5_res")
        scat = [sem(f"scat{b}") for b in range(THIRDS)]

        N1 = 8
        N3 = 8

        block = ctx.enter_context(nc.Block())

        @block.sync
        def _(sp):
            sp.dma_start(cf[:, :], const_f).then_inc(consts_in, 16)
            for b in range(THIRDS):
                sp.dma_start(rows[:, b, 0:TPC, 0:C], x_v[b, 0].rearrange("p (j n) -> p j n", j=TPC)).then_inc(x_in[b], 16)
            sp.dma_start(cb[:, :], const_b).then_inc(consts_in, 16)
            sp.dma_start(ci[:, :, :], const_i).then_inc(consts_in, 16)
            sp.dma_start(wq_s[:, :, :], wq.rearrange("(h p) n -> p h n", p=P)).then_inc(consts_in, 16)
            sp.dma_start(wv_s[:, :, :], wv.rearrange("(h p) n -> p h n", p=P)).then_inc(consts_in, 16)
            sp.dma_start(wr_s[:, :], wr).then_inc(consts_in, 16)
            sp.dma_start(br_s[:, :], br).then_inc(consts_in, 16)
            sp.dma_start(b1_s[:, :], b1).then_inc(consts_in, 16)
            sp.dma_start(bias_f[:, :], bias).then_inc(consts_in, 16)
            sp.dma_start(fwd, fwd_basis).then_inc(fwd_in, 16)
            with sp.Fori(1, STEPS) as k:
                for b in range(THIRDS):
                    sp.wait_ge(x_in[b], 16 * k)
                    sp.dma_start(rows[:, b, bass.ds(TPC * k, TPC), 0:C],
                                 x_v[b, bass.ds(k, 1)].rearrange("k p (j n) -> p (k j) n", j=TPC)).then_inc(x_in[b], 16)
            sp.wait_ge(s2_dft, NCHUNK)
            for b in range(THIRDS):
                sp.dma_start(inv[b], inv_basis[b, 0]).then_inc(inv_in[b], 16)

            def store_rows(k):
                for b in range(THIRDS):
                    sp.wait_ge(s3_rows, k + 1)
                    sp.dma_start(table_v[b, bass.ds(k, 1)].rearrange("k p (j n) -> p (k j) n", j=TPC),
                                 rows[:, b, bass.ds(TPC * k, TPC), :]).then_inc(table_out, 16)

            def store_base(k):
                for b in range(THIRDS):
                    sp.wait_ge(s3_base, THIRDS * k + b + 1)
                    sp.dma_start(out_v[b, bass.ds(k, 1)].rearrange("k p n -> p k n"),
                                 vcm[:, b, bass.ds(k, 1), :]).then_inc(base_out, 16)

            def load_inv(k):
                for b in range(THIRDS):
                    sp.wait_ge(s3_ri, HALVES * (THIRDS * (k - 1) + b + 1))
                    sp.dma_start(inv[b], inv_basis[b, bass.ds(k, 1)].rearrange("k p s n -> p (k s) n")).then_inc(inv_in[b], 16)

            load_inv(1)
            load_inv(2)
            with sp.Fori(3, STEPS) as k:
                load_inv(k)
                store_rows(k - 3)
                store_base(k - 3)
            with sp.Fori(STEPS - 3, STEPS) as k:
                store_rows(k)
                store_base(k)
            sp.wait_ge(base_out, 16 * NCHUNK)
            sp.dma_start(w1_s, w1.rearrange("(h p) n -> p h n", p=P)).then_inc(w_in, 16)
            sp.dma_start(w2_s, w2.rearrange("(t p) n -> p t n", p=P)).then_inc(w_in, 16)

        @block.gpsimd
        def _(pool):
            def add_x(k):
                for b in range(THIRDS):
                    pool.wait_ge(s3_gated, 2 * (THIRDS * k + b + 1))
                    xr = rows[:, b, bass.ds(TPC * k, TPC), 0:C]
                    pool.tensor_tensor(xr, xr, gated[b].rearrange("p (j c) -> p j c", c=C), ALU.add).then_inc(s3_x1, 1)

            with pool.Fori(0, STEPS) as k:
                add_x(k)

            def gather(f):
                for b in range(THIRDS):
                    pool.wait_ge(s5_idx, f + 1)
                    for j in range(TPC):
                        pool.indirect_dma_start(got[b][:, j, :], None, table[:, :],
                                                bass.IndirectOffsetOnAxis(idx_s[:, b, j:j + 1].bitcast(u32), 0)).then_inc(got_in[b], 16)

            def scatter(f, last=False):
                for b in range(THIRDS):
                    pool.wait_ge(s5_res, 2 * (THIRDS * f + b + 1))
                    for j in range(TPC):
                        n = KEEP - P * (FT - 1) if last and b == THIRDS - 1 and j == TPC - 1 else P
                        pool.indirect_dma_start(out[:, :], bass.IndirectOffsetOnAxis(idx_s[0:n, b, j:j + 1].bitcast(u32), 0),
                                                res5[b][0:n, j, :], None).then_inc(scat[b], 16)

            pool.wait_ge(table_out, 16 * NCHUNK)
            pool.wait_ge(base_out, 16 * NCHUNK)
            gather(0)
            for f in range(FSTEPS):
                scatter(f, last=f == FSTEPS - 1)
                for b in range(THIRDS):
                    pool.wait_ge(scat[b], 16 * TPC * (f + 1))
                if f + 1 < FSTEPS:
                    gather(f + 1)

        @block.scalar
        def _(act):
            act.wait_ge(consts_in, 16 * 9)

            def stage1(k):
                act.wait_ge(s1_stats, N1 * k + 4)
                act.activation(small[:, 1, :], small[:, 0, :], ACT.Sqrt).then_inc(s1_sd, 1)
                act.wait_ge(s1_norm, k + 1)
                for b in range(THIRDS):
                    for j in range(TPC):
                        t = TPC * b + j
                        ins = act.activation(v_tok[b][:, j, :], rows[:, b, bass.ds(TPC * k + j, 1), 0:C].rearrange("p k n -> p (k n)"),
                                             ACT.Identity, bias=small[:, 5, t:t + 1], scale=small[:, 4, t:t + 1])
                    ins.then_inc(s1_vtok, 1)
                for b in range(THIRDS):
                    act.wait_ge(s1_tr, THIRDS * k + b + 1)
                    act.activation(vcm[:, b, bass.ds(k, 1), :].rearrange("p k n -> p (k n)"),
                                   ps[:, 2 * b:2 * b + 2, :].rearrange("p a n -> p (a n)"), ACT.Copy).then_inc(s1_vcm, 1)

            with act.Fori(0, STEPS) as k:
                stage1(k)

            def scaled_abs(k, b):
                for h in range(HALVES):
                    ins = act.activation(absv[b][:, h * CHUNK:(h + 1) * CHUNK],
                                         vcm[:, b, bass.ds(k, 1), h * CHUNK:(h + 1) * CHUNK].rearrange("p k n -> p (k n)"),
                                         ACT.Abs, scale=fin[:, 3, h:h + 1])
                ins.then_inc(s2_abs, 1)

            def unmagic(k, b):
                act.wait_ge(s2_tr, THIRDS * k + b + 1)
                act.activation(q_tok[b].rearrange("p j c -> p (j c)"), ps[:, 2 * b:2 * b + 2, :].rearrange("p a n -> p (a n)"),
                               ACT.Identity, bias=const("magic")).then_inc(s2_q, 1)

            act.wait_ge(s1_scale, 1)
            for b in range(THIRDS):
                scaled_abs(0, b)
            with act.Fori(1, STEPS) as k:
                for b in range(THIRDS):
                    unmagic(k - 1, b)
                    scaled_abs(k, b)
            for b in range(THIRDS):
                unmagic(STEPS - 1, b)

            def squares_of(k, b):
                for h in range(HALVES):
                    act.wait_ge(s3_ri, HALVES * (THIRDS * k + b) + h + 1)
                    if not (isinstance(k, int) and k == 0 and b == 0):
                        act.wait_ge(s3_mag, HALVES * (THIRDS * k + b - 1) + h + 1)
                    act.activation(squares[h].rearrange("p r n -> p (r n)"), ps[:, 2 * h:2 * h + 2, :].rearrange("p a n -> p (a n)"),
                                   ACT.Square).then_inc(s3_sq, 1)

            def roots_of(k, b):
                for h in range(HALVES):
                    act.wait_ge(s3_sum, HALVES * (THIRDS * k + b) + h + 1)
                    if h == 0 and not (isinstance(k, int) and k == 0 and b == 0):
                        act.wait_ge(s3_q, 2 * (THIRDS * k + b))
                    act.activation(mag[:, h * CHUNK:(h + 1) * CHUNK], squares[h][:, 0, :], ACT.Sqrt).then_inc(s3_mag, 1)

            def copy_v(k, b):
                if not isinstance(k, int) or k >= 1:
                    act.wait_ge(s3_v, 2 * (THIRDS * (k - 1) + b + 1))
                act.activation(v_st[b], vcm[:, b, bass.ds(k, 1), :].rearrange("p k n -> p (k n)"), ACT.Copy).then_inc(s3_vst, 1)

            def sd_of(k):
                act.wait_ge(s3_stats, N3 * k + 4)
                act.activation(small[:, 1, :], small[:, 0, :], ACT.Sqrt).then_inc(s3_sd, 1)

            def base_of(k, b):
                act.wait_ge(s3_tail, k + 1)
                for j in range(TPC):
                    r = rows[:, b, bass.ds(TPC * k + j, 1), :].rearrange("p k n -> p (k n)")
                    ins = act.activation(vcm[:, b, bass.ds(k, 1), j * C:(j + 1) * C].rearrange("p k n -> p (k n)"), r[:, 0:C],
                                         ACT.Identity, bias=r[:, C + 1:C + 2], scale=r[:, C + 2:C + 3])
                ins.then_inc(s3_base, 1)

            def stage3(k, query=True, value=True, base=True, ahead=True):
                for b in range(THIRDS):
                    if query:
                        roots_of(k, b)
                        if b + 1 < THIRDS:
                            squares_of(k, b + 1)
                        elif ahead:
                            squares_of(k + 1, 0)
                    if value:
                        copy_v(k - 1, b)
                    if base and b == 0:
                        sd_of(k - 2)
                    if base and b >= 1:
                        base_of(k - 2, b - 1)
                if base:
                    base_of(k - 2, THIRDS - 1)

            squares_of(0, 0)
            stage3(0, value=False, base=False)
            stage3(1, base=False)
            with act.Fori(2, STEPS - 1) as k:
                stage3(k)
            stage3(STEPS - 1, ahead=False)
            stage3(STEPS, query=False)
            stage3(STEPS + 1, query=False, value=False)

            with act.Fori(0, FSTEPS) as f:
                for b in range(THIRDS):
                    for t in range(HT):
                        n = HT * (THIRDS * f + b) + t
                        act.wait_ge(s5_h, n + 1)
                        act.activation(hid[b][:, t, :], ps[:, 2 + (HT * b + t) % 3, :], ACT.Gelu_apprx_tanh, bias=b1_s[:, t:t + 1]).then_inc(s5_gelu, 1)

        @block.vector
        def _(dve):
            def moments(k, eps, steps, per):
                n = per * k
                dve.wait_ge(steps, n + 1)
                even, odd = stats[:, :, 1:3], stats[:, :, 4:6]
                dve.tensor_tensor(small[:, 8, :], even[:, :, 0], odd[:, :, 0], ALU.add)
                dve.tensor_tensor(small[:, 9, :], even[:, :, 0], odd[:, :, 0], ALU.subtract)
                dve.tensor_tensor(small[:, 10, :], even[:, :, 1], odd[:, :, 1], ALU.add).then_inc(steps, 1)
                dve.wait_ge(steps, n + 2)
                dve.tensor_scalar(mean, small[:, 8, :], 0.5, None, ALU.mult)
                dve.scalar_tensor_tensor(small[:, 11, :], small[:, 9, :], 0.25, small[:, 9, :], ALU.mult, ALU.mult)
                dve.tensor_scalar(small[:, 12, :], small[:, 10, :], 1.0 / C, eps, ALU.mult, ALU.add).then_inc(steps, 1)
                dve.wait_ge(steps, n + 3)
                dve.tensor_tensor(small[:, 0, :], small[:, 11, :], small[:, 12, :], ALU.add).then_inc(steps, 1)

            def rstd(k, steps, per, sd):
                n = per * k + 4
                dve.wait_ge(sd, k + 1)
                dve.reciprocal(small[:, 2, :], small[:, 1, :]).then_inc(steps, 1)
                dve.wait_ge(steps, n + 1)
                dve.tensor_tensor(small[:, 3, :], small[:, 2, :], small[:, 2, :], ALU.mult).then_inc(steps, 1)
                dve.wait_ge(steps, n + 2)
                dve.scalar_tensor_tensor(small[:, 6, :], small[:, 3, :], -0.5, small[:, 0, :], ALU.mult, ALU.mult).then_inc(steps, 1)
                dve.wait_ge(steps, n + 3)
                dve.scalar_tensor_tensor(small[:, 4, :], small[:, 6, :], 1.5, small[:, 2, :], ALU.add, ALU.mult).then_inc(steps, 1)
                dve.wait_ge(steps, n + 4)

            def extremes(k):
                for b in range(THIRDS):
                    dve.wait_ge(s1_vcm, THIRDS * k + b + 1)
                    chunk = vcm[:, b, bass.ds(k, 1), :].rearrange("p k (h n) -> p (k h) n", h=HALVES)
                    for which, op in ((0, ALU.max), (1, ALU.min)):
                        ins = dve.tensor_reduce(ext[:, which, :, bass.ds(THIRDS * k + b, 1)].rearrange("p h k -> p (h k)"), chunk, AX.X, op,
                                                apply_absolute_value=True)
                ins.then_inc(s1_ext, 1)

            dve.wait_ge(consts_in, 16 * 9)

            def stage1(k, reduce=True):
                for b in range(THIRDS):
                    dve.wait_ge(x_in[b], 16 * (k + 1))
                    for j in range(TPC):
                        ins = dve.bn_stats(stats[:, TPC * b + j, :], rows[:, b, bass.ds(TPC * k + j, 1), 0:C].rearrange("p k n -> p (k n)"))
                ins.then_inc(s1_stats, 1)
                moments(k, EPS_C, s1_stats, N1)
                if reduce:
                    extremes(k - 1)
                rstd(k, s1_stats, N1, s1_sd)
                dve.scalar_tensor_tensor(small[:, 5, :], mean, -1.0, small[:, 4, :], ALU.mult, ALU.mult).then_inc(s1_norm, 1)

            stage1(0, reduce=False)
            with dve.Fori(1, STEPS) as k:
                stage1(k)
            extremes(STEPS - 1)

            n = STEPS
            dve.wait_ge(s1_ext, n)
            dve.tensor_reduce(fin[:, 0, :], ext[:, 0, :, :], AX.X, ALU.max)
            dve.tensor_reduce(fin[:, 1, :], ext[:, 1, :, :], AX.X, ALU.min).then_inc(s1_ext, 1)
            dve.wait_ge(s1_ext, n + 1)
            dve.tensor_tensor(fin[:, 2, :], fin[:, 0, :], fin[:, 1, :], ALU.subtract).then_inc(s1_ext, 1)
            dve.wait_ge(s1_ext, n + 2)
            dve.reciprocal(fin[:, 5, :], fin[:, 2, :]).then_inc(s1_ext, 1)
            dve.wait_ge(s1_ext, n + 3)
            dve.tensor_scalar(fin[:, 3, :], fin[:, 5, :], 255.0, None, ALU.mult).then_inc(s1_ext, 1)
            dve.wait_ge(s1_ext, n + 4)
            dve.scalar_tensor_tensor(fin[:, 5, :], fin[:, 1, :], -1.0, fin[:, 3, :], ALU.mult, ALU.mult).then_inc(s1_ext, 1)
            dve.wait_ge(s1_ext, n + 5)
            dve.tensor_scalar(fin[:, 4, :], fin[:, 5, :], -HALF, None, ALU.add).then_inc(s1_scale, 1)

            def levels(k):
                for b in range(THIRDS):
                    dve.wait_ge(s2_abs, THIRDS * k + b + 1)
                    if not isinstance(k, int) or k >= 1:
                        dve.wait_ge(s2_tr, THIRDS * (k - 1) + b + 1)
                    for h in range(HALVES):
                        ins = dve.tensor_scalar(lev[b][:, h * CHUNK:(h + 1) * CHUNK], absv[b][:, h * CHUNK:(h + 1) * CHUNK],
                                                fin[:, 4, h:h + 1], MAGIC, ALU.add, ALU.add)
                    ins.then_inc(s2_lev, 1)

            dve.wait_ge(s1_scale, 1)
            levels(0)
            with dve.Fori(1, STEPS) as k:
                levels(k)

            splits = [0]

            def step(ins):
                splits[0] += 1
                ins.then_inc(s2_split, 1)
                dve.wait_ge(s2_split, splits[0])

            def split(dst, src, mask, n, width):
                r0, r1 = resid[1][n, 0:width], resid[2][n, 0:width]
                pt = [p_[n, 0:width] for p_ in part]
                pk = [p_[n, 0:width] for p_ in picked]
                step(dve.tensor_copy(pt[0], src))
                step(dve.tensor_tensor(r0, src, pt[0], ALU.subtract))
                step(dve.tensor_copy(pt[1], r0))
                step(dve.tensor_tensor(r1, r0, pt[1], ALU.subtract))
                step(dve.tensor_copy(pt[2], r1))
                step(dve.tensor_scalar(pk[0], pt[0], mask[:, 0:1], None, ALU.mult))
                step(dve.scalar_tensor_tensor(pk[1], pt[1], mask[:, 1:2], pk[0], ALU.mult, ALU.add))
                step(dve.scalar_tensor_tensor(dst, pt[2], mask[:, 2:3], pk[1], ALU.mult, ALU.add))

            dve.wait_ge(s2_dft, NCHUNK)
            dve.tensor_copy(sums, ps[0:3 * NFUN, 6, 0:C]).then_inc(s2_sums, 1)
            for i in range(3):
                split(bias_s[:, i * C:(i + 1) * C], bias_f[:, i * C:(i + 1) * C], const("mask_b")[0:3, :], slice(0, 3), C)
            dve.wait_ge(s2_coef, 3)
            for dst, bank, name, n in ((coef_r1, 0, "mask_r1", slice(0, R1)), (coef_r2, 1, "mask_r2", slice(R2_AT, R2_AT + R2)),
                                       (coef_im, 2, "mask_im", slice(0, RI))):
                split(dst[n, :], ps[n, bank, 0:C], const(name)[n, :], n, C)
            dve.tensor_copy(junk[:, :], const("magic")).then_inc(s2_done, 1)

            def add_squares(k, b):
                for h in range(HALVES):
                    dve.wait_ge(s3_sq, HALVES * (THIRDS * k + b) + h + 1)
                    dve.tensor_tensor(squares[h][:, 0, :], squares[h][:, 0, :], squares[h][:, 1, :], ALU.add).then_inc(s3_sum, 1)

            def query_max(k, b):
                for jj in range(2):
                    dve.wait_ge(s3_q, 2 * (THIRDS * k + b) + jj + 1)
                    dve.tensor_reduce(qmax[:, 2 * jj:2 * jj + 2, :, b], ps[:, 4 + jj, :].rearrange("p (j g m) -> p j m g", j=2, m=GROUPS),
                                      AX.X, ALU.max).then_inc(s3_qmax, 1)

            def gate_of(k):
                dve.wait_ge(s3_qmax, 2 * THIRDS * (k + 1))
                if not isinstance(k, int) or k >= 1:
                    dve.wait_ge(s3_gated, 2 * THIRDS * k)
                dve.tensor_reduce(qm[:, :, :], qmax[:, :, :, :].rearrange("p j m b -> p j (m b)").rearrange("p j (a r) -> p j r a", a=THIRDS),
                                  AX.X, ALU.max).then_inc(s3_qsteps, 1)
                dve.wait_ge(s3_qsteps, k + 1)
                for a in range(THIRDS):
                    ins = dve.tensor_scalar(gate[:, :, a * GROUPS:(a + 1) * GROUPS], qm[:, :, :], 1.0, None, ALU.add)
                ins.then_inc(s3_gate, 1)

            def gated_value(k, b):
                for jj in range(2):
                    dve.wait_ge(s3_v, 2 * (THIRDS * k + b) + jj + 1)
                    dve.wait_ge(s3_gate, k + 1)
                    if not isinstance(k, int) or k >= 1:
                        dve.wait_ge(s3_x1, THIRDS * (k - 1) + b + 1)
                    g = gate[:, 2 * jj:2 * jj + 2, :].rearrange("p j (m b) -> p j b m", b=THIRDS)[:, :, b:b + 1, :]
                    dve.tensor_tensor(gated[b][:, jj * 512:(jj + 1) * 512].rearrange("p (j g m) -> p j g m", j=2, m=GROUPS),
                                      ps[:, 6 + jj, :].rearrange("p (j g m) -> p j g m", j=2, m=GROUPS),
                                      g.broadcast_to([P, 2, C // GROUPS, GROUPS]), ALU.mult).then_inc(s3_gated, 1)

            def row(k, b, j):
                return rows[:, b, bass.ds(TPC * k + j, 1), :].rearrange("p k n -> p (k n)")

            def statistics(k, b):
                dve.wait_ge(s3_x1, THIRDS * k + b + 1)
                for j in range(TPC):
                    ins = dve.bn_stats(stats[:, TPC * b + j, :], row(k, b, j)[:, 0:C])
                if b == THIRDS - 1:
                    ins.then_inc(s3_stats, 1)

            def tails(k):
                rstd(k, s3_stats, N3, s3_sd)
                for b in range(THIRDS):
                    tail = rows[:, b, bass.ds(TPC * k, TPC), C:ROW]
                    ts = slice(TPC * b, TPC * (b + 1))
                    dve.tensor_copy(tail[:, :, 0], small[:, 4, ts])
                    dve.scalar_tensor_tensor(tail[:, :, 1], mean[:, ts], -1.0, small[:, 4, ts], ALU.mult, ALU.mult)
                    ins = dve.tensor_scalar(tail[:, :, 2], small[:, 4, ts], 1.0, None, ALU.add)
                ins.then_inc(s3_tail, 1)

            def router_sum(k, b):
                if b == 0:
                    dve.wait_ge(s3_stats, N3 * k + 4)
                if not (isinstance(k, int) and k == 0 and b == 0):
                    dve.wait_ge(s3_w, THIRDS * k + b)
                for j in range(TPC):
                    t = TPC * b + j
                    ins = dve.scalar_tensor_tensor(unused[:, j, :],
                                                   row(k, b, j)[:, 0:C], mean[:, t:t + 1], wr_s[:, :],
                                                   ALU.subtract, ALU.mult, accum_out=small[:, 7, t:t + 1])
                ins.then_inc(s3_w, 1)

            def router(k):
                dve.wait_ge(s3_w, THIRDS * (k + 1))
                dve.tensor_tensor(small[:, 13, :], small[:, 7, :], small[:, 4, :], ALU.mult).then_inc(s3_wsteps, 1)
                dve.wait_ge(s3_wsteps, k + 1)
                for b in range(THIRDS):
                    ts = slice(TPC * b, TPC * (b + 1))
                    dve.tensor_scalar(rows[:, b, bass.ds(TPC * k, TPC), C + 3], small[:, 13, ts], br_s[:, 0:1], None, ALU.add)
                    ins = dve.tensor_scalar(w_all[:, bass.ds(COLS * b + TPC * k, TPC)], small[:, 13, ts], br_s[:, 0:1], None, ALU.add)
                ins.then_inc(s3_rows, 1)

            def stage3(k, query=True, value=True, weigh=True, ahead=True):
                for b in range(THIRDS):
                    if query:
                        if b + 1 < THIRDS:
                            add_squares(k, b + 1)
                        elif ahead:
                            add_squares(k + 1, 0)
                    if weigh:
                        if b == 0:
                            statistics(k - 2, THIRDS - 1)
                            moments(k - 2, EPS_T, s3_stats, N3)
                        if b == 1:
                            tails(k - 2)
                        router_sum(k - 2, b)
                    if query:
                        query_max(k, b)
                    if value:
                        if b > 0:
                            statistics(k - 1, b - 1)
                        gated_value(k - 1, b)
                if weigh:
                    router(k - 2)
                if query:
                    gate_of(k)

            add_squares(0, 0)
            stage3(0, value=False, weigh=False)
            stage3(1, weigh=False)
            with dve.Fori(2, STEPS - 1) as k:
                stage3(k)
            stage3(STEPS - 1, ahead=False)
            stage3(STEPS, query=False)
            stage3(STEPS + 1, query=False, value=False)

            count = [0]

            def link(ins):
                count[0] += 1
                ins.then_inc(s4_step, 1)
                dve.wait_ge(s4_step, count[0])

            totals = [0]

            def total(width):
                totals[0] += 1
                dve.wait_ge(s4_tot, totals[0])
                return ps[:, 0, 0:width]

            dve.wait_ge(s3_rows, STEPS)
            dve.wait_ge(s3_base, NCHUNK)
            sign, target, wstar, need = (sc4[:, i:i + 1] for i in range(4))
            link(dve.tensor_scalar(u_w, w_all[:, :], 0.0, 0.0, ALU.is_ge, ALU.add, accum_out=cnt_f[:, 0:1]))
            dve.tensor_copy(cnt_b[:, 0:1], cnt_f[:, 0:1]).then_inc(s4_cnt, 1)
            link(dve.tensor_scalar(sc4[:, 4:5], total(1), float(KEEP), None, ALU.is_ge))
            link(dve.tensor_scalar(sign, sc4[:, 4:5], 2.0, -1.0, ALU.mult, ALU.add))
            link(dve.tensor_scalar(target, sc4[:, 4:5], float(2 * KEEP - PIX - 1), float(PIX - KEEP + 1), ALU.mult, ALU.add))
            link(dve.tensor_scalar(u_w, w_all[:, :], sign, None, ALU.mult))
            link(dve.tensor_copy(cand[0], ci[:, 0, :]))
            for r in range(len(SHIFTS)):
                c = cand[r % 2].bitcast(f32)
                link(dve.tensor_tensor(cmp_t, u_w.rearrange("p (a t) -> p a t", a=1).broadcast_to([P, CAND, TILES]),
                                       c.rearrange("p (j a) -> p j a", a=1).broadcast_to([P, CAND, TILES]), ALU.is_ge))
                with nc.allow_low_precision(reason="a partition's count is at most 72, exact in bfloat16"):
                    dve.tensor_reduce(cnt_b, cmp_t, AX.X, ALU.add).then_inc(s4_cnt, 1)
                link(dve.tensor_scalar(passed, total(CAND), target, -1.0, ALU.is_ge, ALU.mult))
                link(dve.tensor_tensor(masked, passed, cand[r % 2], ALU.bitwise_and))
                link(dve.tensor_reduce(prefix.bitcast(f32), masked.bitcast(f32), AX.X, ALU.max))
                if r + 1 < len(SHIFTS):
                    link(dve.tensor_tensor(cand[(r + 1) % 2], prefix.broadcast_to([P, CAND]), ci[:, r + 1, :], ALU.bitwise_or))
            link(dve.tensor_scalar(wstar, prefix.bitcast(f32), sign, None, ALU.mult))
            link(dve.memset(ones_t, 1.0))
            link(dve.tensor_scalar(gt_m, w_all[:, :], wstar, 0.0, ALU.is_gt, ALU.add, accum_out=cnt_f[:, 0:1]))
            link(dve.tensor_scalar(eq_m, w_all[:, :], wstar, None, ALU.is_equal))
            link(dve.tensor_reduce(cnt_f[:, 1:4], eq_m.rearrange("p (b t) -> p b t", b=THIRDS), AX.X, ALU.add))
            dve.tensor_copy(cnt_b[:, 0:4], cnt_f[:, 0:4]).then_inc(s4_cnt, 1)
            tot = total(8)
            link(dve.tensor_copy(cnt_f[:, 0:8], tot))
            link(dve.tensor_scalar(need, cnt_f[:, 0:1], -1.0, float(KEEP), ALU.mult, ALU.add))
            link(dve.tensor_tensor(cnt_f[:, 6:7], cnt_f[:, 6:7], cnt_f[:, 1:2], ALU.add))
            link(dve.tensor_tensor(cnt_f[:, 7:8], cnt_f[:, 7:8], cnt_f[:, 1:2], ALU.add))
            link(dve.tensor_tensor(cnt_f[:, 7:8], cnt_f[:, 7:8], cnt_f[:, 2:3], ALU.add))
            for b in range(THIRDS):
                s = slice(b * COLS, (b + 1) * COLS)
                link(dve.tensor_tensor_scan(rank_t[:, s], ones_t[:, s], eq_m[:, s], cnt_f[:, 5 + b:6 + b], ALU.mult, ALU.add))
            link(dve.scalar_tensor_tensor(tmp_t, rank_t, need, eq_m, ALU.is_le, ALU.mult))
            link(dve.tensor_tensor(sel_t, tmp_t, gt_m, ALU.add))
            link(dve.tensor_reduce(cnt_f[:, 0:1], sel_t, AX.X, ALU.add))
            dve.tensor_copy(cnt_b[:, 0:1], cnt_f[:, 0:1]).then_inc(s4_cnt, 1)
            tot = total(8)
            link(dve.tensor_copy(cnt_f[:, 0:8], tot))
            link(dve.tensor_tensor_scan(rank_t, ones_t, sel_t, cnt_f[:, 4:5], ALU.mult, ALU.add))
            link(dve.tensor_tensor(rank_t, rank_t, sel_t, ALU.mult))
            link(dve.tensor_scalar(tmp_t, sel_t, float(-NOSLOT - 1), float(NOSLOT), ALU.mult, ALU.add))
            link(dve.tensor_tensor(slot_i, rank_t, tmp_t, ALU.add))
            link(dve.tensor_single_scalar(hi_i, slot_i, 7, ALU.arith_shift_right))
            link(dve.tensor_single_scalar(lo_i, slot_i, P - 1, ALU.bitwise_and))
            link(dve.tensor_copy(hi_f, hi_i))
            link(dve.tensor_copy(lo_f, lo_i))
            for t in range(TILES):
                dve.tensor_scalar(oh_lo[:, t, :], constb("iota"), lo_f[:, t:t + 1], None, ALU.is_equal)
            wide = [P, TILES, FT]

            def by_tile(v):
                return v.rearrange("p (t a) -> p t a", a=1).broadcast_to(wide)

            link(dve.tensor_tensor(oh_hi, constb("iota")[:, 0:FT].rearrange("p (a s) -> p a s", a=1).broadcast_to(wide), by_tile(hi_f), ALU.is_equal))
            dve.tensor_tensor(oh_id[:, :, 0:FT], oh_hi, by_tile(const("id_hi")), ALU.mult)
            dve.tensor_tensor(oh_id[:, :, FT:2 * FT], oh_hi, by_tile(const("id_lo")), ALU.mult).then_inc(s4_hot, 1)
            dve.wait_ge(s4_ids, 1)
            link(dve.tensor_copy(cmp_t[:, 0, 0:2 * FT], ps[:, 1, 0:2 * FT]))
            dve.scalar_tensor_tensor(idx[:, :], cmp_t[:, 0, 0:FT], float(P), cmp_t[:, 0, FT:2 * FT], ALU.mult, ALU.add).then_inc(s4_idx, 1)

            dve.wait_ge(s4_idx, 1)
            dve.wait_ge(table_out, 16 * NCHUNK)
            dve.wait_ge(base_out, 16 * NCHUNK)

            def place_idx(f):
                dve.tensor_copy(idx_s[:, :, :].rearrange("p b j -> p (b j)"), idx[:, TPS * f:TPS * (f + 1)]).then_inc(s5_idx, 1)

            def rows_in(f, b):
                dve.wait_ge(got_in[b], 16 * TPC * (f + 1))
                for j in range(TPC):
                    ins = dve.tensor_scalar(ln_tok[b][:, j, :], got[b][:, j, 0:C], got[b][:, j, C:C + 1], got[b][:, j, C + 1:C + 2], ALU.mult, ALU.add)
                ins.then_inc(s5_ln, 1)
                if f >= 1:
                    dve.wait_ge(s5_res, 2 * (THIRDS * (f - 1) + b + 1))
                for j in range(TPC):
                    ins = dve.tensor_scalar(base5[b][:, j, :], got[b][:, j, 0:C], got[b][:, j, C + 2:C + 3], got[b][:, j, C + 1:C + 2], ALU.mult, ALU.add)
                ins.then_inc(s5_base, 1)

            def channels(f, b):
                dve.wait_ge(s5_tr, THIRDS * f + b + 1)
                dve.tensor_copy(ln_ch[b].rearrange("p h n -> p (h n)"), ps[:, 0:2, :].rearrange("p a n -> p (a n)")).then_inc(s5_lnch, 1)

            def result(f, b):
                dve.wait_ge(s5_base, THIRDS * f + b + 1)
                if f >= 1:
                    dve.wait_ge(scat[b], 16 * TPC * f)
                for jj in range(2):
                    dve.wait_ge(s5_y, 2 * (THIRDS * f + b) + jj + 1)
                    for j in (2 * jj, 2 * jj + 1):
                        ins = dve.scalar_tensor_tensor(res5[b][:, j, :], ps[:, 5 + jj, (j % 2) * C:(j % 2 + 1) * C], got[b][:, j, C + 3:C + 4],
                                                       base5[b][:, j, :], ALU.mult, ALU.add)
                    ins.then_inc(s5_res, 1)

            place_idx(0)
            for f in range(FSTEPS):
                rows_in(f, 0)
                channels(f, 0)
                for b in range(THIRDS):
                    if b + 1 < THIRDS:
                        rows_in(f, b + 1)
                        channels(f, b + 1)
                    result(f, b)
                if f + 1 < FSTEPS:
                    for b in range(THIRDS):
                        dve.wait_ge(scat[b], 16 * TPC * (f + 1))
                    place_idx(f + 1)

        @block.tensor
        def _(pe):
            pe.wait_ge(consts_in, 16 * 9)

            def transpose1(k):
                for b in range(THIRDS):
                    pe.wait_ge(s1_vtok, THIRDS * k + b + 1)
                    if not isinstance(k, int) or k >= 1:
                        pe.wait_ge(s1_vcm, THIRDS * (k - 1) + b + 1)
                    for h in range(HALVES):
                        for j in range(TPC):
                            ins = pe.transpose(ps[:, 2 * b + h, j * P:(j + 1) * P], v_tok[b][:, j, h * P:(h + 1) * P], ident)
                    ins.then_inc(s1_tr, 1)

            transpose1(0)
            with pe.Fori(1, STEPS) as k:
                transpose1(k)

            def transpose2(k, b):
                pe.wait_ge(s2_lev, THIRDS * k + b + 1)
                if isinstance(k, int) and k == 0:
                    pe.wait_ge(s1_vcm, THIRDS * (STEPS - 1) + b + 1)
                else:
                    pe.wait_ge(s2_q, THIRDS * (k - 1) + b + 1)
                for j in range(TPC):
                    for h in range(HALVES):
                        ins = pe.transpose(ps[:, 2 * b + j // 2, (j % 2) * C + h * P:(j % 2) * C + (h + 1) * P],
                                           lev[b][:, h * CHUNK + j * P:h * CHUNK + (j + 1) * P], ident)
                ins.then_inc(s2_tr, 1)

            def fourier(k, b, first=False, last=False):
                pe.wait_ge(s2_q, THIRDS * k + b + 1)
                for j in range(TPC):
                    ins = pe.matmul(ps[0:3 * NFUN, 6, 0:C], fwd[:, bass.ds(COLS * b + TPC * k + j, 1), :].rearrange("p k m -> p (k m)"),
                                    q_tok[b][:, j, :], start=first and j == 0, stop=last and j == TPC - 1)
                ins.then_inc(s2_dft, 1)

            pe.wait_ge(fwd_in, 16)
            for b in range(THIRDS):
                transpose2(0, b)
            for b in range(THIRDS):
                fourier(0, b, first=b == 0)
            with pe.Fori(1, STEPS - 1) as k:
                for b in range(THIRDS):
                    transpose2(k, b)
                for b in range(THIRDS):
                    fourier(k, b)
            for b in range(THIRDS):
                transpose2(STEPS - 1, b)
            for b in range(THIRDS):
                fourier(STEPS - 1, b, last=b == THIRDS - 1)

            pe.wait_ge(s2_sums, 1)
            for bank, name, n in ((0, "sel_r1", R1), (1, "sel_r2", R2_AT + R2), (2, "sel_im", RI)):
                pe.matmul(ps[0:n, bank, 0:C], const(name)[0:3 * NFUN, 0:n], sums, start=True, stop=True).then_inc(s2_coef, 1)
            pe.wait_ge(s2_done, 1)

            def invert(k, b):
                pe.wait_ge(inv_in[b], 16 * (k + 1))
                for h in range(HALVES):
                    if not (isinstance(k, int) and k == 0 and b == 0):
                        pe.wait_ge(s3_sq, HALVES * (THIRDS * k + b - 1) + h + 1)
                    cs = slice(h * P, (h + 1) * P)
                    pe.matmul(ps[:, 2 * h, :], coef_r1[:, cs], inv[b][:, 0, :], start=True, stop=False)
                    pe.matmul(ps[:, 2 * h, :], coef_r2[R2_AT:R2_AT + R2, cs], inv[b][R2_AT:R2_AT + R2, 1, :], start=False, stop=True)
                    pe.matmul(ps[:, 2 * h + 1, :], coef_im[0:RI, cs], inv[b][0:RI, 1, :], start=True, stop=True).then_inc(s3_ri, 1)

            def product(k, b, lhs, bank, w, bias_i, ready, done, used):
                for jj in range(2):
                    for j in (2 * jj, 2 * jj + 1):
                        o = ps[:, bank + jj, (j % 2) * C:(j % 2 + 1) * C]
                        if j % 2 == 0:
                            used(jj)
                        pe.matmul(o, constb("ones")[0:3, :], bias_s[:, bias_i * C:(bias_i + 1) * C], start=True, stop=False)
                        for h in range(HALVES):
                            if jj == 0 and j == 0:
                                ready(h)
                            ins = pe.matmul(o, lhs[:, h * CHUNK + j * P:h * CHUNK + (j + 1) * P], w[:, h, :], start=False, stop=h == HALVES - 1)
                    ins.then_inc(done, 1)

            def query(k, b):
                product(k, b, mag, 4, wq_s, 0, lambda h: pe.wait_ge(s3_mag, HALVES * (THIRDS * k + b) + h + 1), s3_q,
                        lambda jj: None if isinstance(k, int) and k == 0 and b == 0 else pe.wait_ge(s3_qmax, 2 * (THIRDS * k + b - 1) + jj + 1))

            def value(k, b):
                product(k, b, v_st[b], 6, wv_s, 1, lambda h: pe.wait_ge(s3_vst, THIRDS * k + b + 1), s3_v,
                        lambda jj: None if isinstance(k, int) and k == 0 and b == 0 else pe.wait_ge(s3_gated, 2 * (THIRDS * k + b - 1) + jj + 1))

            def stage3(k, ahead=True, first=False):
                for b in range(THIRDS):
                    if b + 1 < THIRDS:
                        invert(k, b + 1)
                    elif ahead:
                        invert(k + 1, 0)
                    query(k, b)
                    if not first:
                        value(k - 1, b)

            invert(0, 0)
            stage3(0, first=True)
            stage3(1)
            with pe.Fori(2, STEPS - 1) as k:
                stage3(k)
            stage3(STEPS - 1, ahead=False)
            for b in range(THIRDS):
                value(STEPS - 1, b)

            n_rounds = len(SHIFTS)
            for i in range(n_rounds + 3):
                pe.wait_ge(s4_cnt, i + 1)
                width = 1 if i == 0 else CAND if i <= n_rounds else 4
                prefixes = i > n_rounds
                ins = pe.matmul(ps[:, 0, 0:width], constb("ones"), cnt_b[:, 0:width], start=True, stop=True)
                if prefixes:
                    ins = pe.matmul(ps[:, 0, 4:8], constb("tri"), cnt_b[:, 0:4], start=True, stop=True)
                ins.then_inc(s4_tot, 1)
            pe.wait_ge(s4_hot, 1)
            for t in range(TILES):
                ins = pe.matmul(ps[:, 1, 0:2 * FT], oh_lo[:, t, :], oh_id[:, t, :], start=t == 0, stop=t == TILES - 1)
            ins.then_inc(s4_ids, 1)

            pe.wait_ge(w_in, 32)

            def transpose5(f, b):
                pe.wait_ge(s5_ln, THIRDS * f + b + 1)
                if not (f == 0 and b == 0):
                    pe.wait_ge(s5_lnch, THIRDS * f + b)
                for h in range(HALVES):
                    for j in range(TPC):
                        ins = pe.transpose(ps[:, h, j * P:(j + 1) * P], ln_tok[b][:, j, h * P:(h + 1) * P], ident)
                ins.then_inc(s5_tr, 1)

            def hidden(f, b):
                pe.wait_ge(s5_lnch, THIRDS * f + b + 1)
                for t in range(HT):
                    n = HT * (THIRDS * f + b) + t
                    if n >= 3:
                        pe.wait_ge(s5_gelu, n - 2)
                    for h in range(HALVES):
                        ins = pe.matmul(ps[:, 2 + n % 3, :], w1_s[:, h, t * P:(t + 1) * P], ln_ch[b][:, h, :], start=h == 0, stop=h == HALVES - 1)
                    ins.then_inc(s5_h, 1)

            def second(f, b):
                c = THIRDS * f + b
                for jj in range(2):
                    if c >= 1:
                        pe.wait_ge(s5_res, 2 * (c - 1) + jj + 1)
                    for j in (2 * jj, 2 * jj + 1):
                        o = ps[:, 5 + jj, (j % 2) * C:(j % 2 + 1) * C]
                        pe.matmul(o, constb("ones")[0:3, :], bias_s[:, 2 * C:3 * C], start=True, stop=False)
                        for t in range(HT):
                            if jj == 0 and j == 0:
                                pe.wait_ge(s5_gelu, HT * c + t + 1)
                            ins = pe.matmul(o, hid[b][:, t, j * P:(j + 1) * P], w2_s[:, t, :], start=False, stop=t == HT - 1)
                    ins.then_inc(s5_y, 1)

            chunks = [(f, b) for f in range(FSTEPS) for b in range(THIRDS)]
            for n, (f, b) in enumerate(chunks):
                transpose5(f, b)
                hidden(f, b)
                second(f, b)


def bases():
    bf = mybir.dt.np(mybir.dt.bfloat16)
    pairs, lone = frequencies()
    pix = np.arange(PIX)
    y, x = pix // SIDE, pix % SIDE
    funs = [np.ones(PIX)]
    for u, v in pairs + lone:
        turn = 2 * np.pi * ((u * y + v * x) % SIDE) / SIDE
        funs += [np.cos(turn), np.sin(turn)]
    funs = np.stack(funs)

    def parts(a):
        out_, rest = [], a.astype(np.float64)
        for _ in range(3):
            p_ = rest.astype(bf)
            out_.append(p_)
            rest = rest - p_.astype(np.float64)
        return out_

    fp = np.stack(parts(funs))
    cube = fp.reshape(3, NFUN, THIRDS, P, COLS)
    fwd = np.ascontiguousarray(cube.transpose(3, 2, 4, 0, 1)).reshape(P, TILES * 3 * NFUN)
    flat = cube.reshape(3, NFUN, THIRDS, P, STEPS, TPC).transpose(0, 1, 2, 4, 5, 3).reshape(3, NFUN, THIRDS, STEPS, CHUNK)
    inv = np.zeros((THIRDS, STEPS, P, 2, CHUNK), bf)
    for r, (i, _, b) in enumerate(REAL_ROWS[:P]):
        inv[:, :, r, 0] = flat[b, i]
    n0 = 1 + 2 * len(pairs)
    for r, (i, _, b) in enumerate(IMAG_ROWS):
        inv[:, :, r, 1] = flat[b, n0 + i]
    const = np.zeros((P, NCF), np.float32)

    def put(name, rows_, cols, val):
        const[rows_, CF[name][0] + cols] = val

    for p_ in range(P):
        put("ident", p_, p_, 1.0)
    n = float(PIX)
    for r, (i, a, _) in enumerate(REAL_ROWS):
        name, col = ("sel_r1", r) if r < P else ("sel_r2", R2_AT + r - P)
        mask = "mask_r1" if r < P else "mask_r2"
        w = (2.0 if 0 < i < n0 else 1.0) / n
        for part_ in range(3):
            put(name, part_ * NFUN + i, col, w)
        put(mask, col, a, 1.0)
        if r >= P:
            inv[:, :, col, 1] = flat[REAL_ROWS[r][2], i]
    for r, (i, a, _) in enumerate(IMAG_ROWS):
        src, w = (i - 1, 1.0 / n) if i % 2 else (i + 1, -1.0 / n)
        for part_ in range(3):
            put("sel_im", part_ * NFUN + n0 + src, r, w)
        put("mask_im", r, a, 1.0)
    for part_ in range(3):
        put("mask_b", part_, part_, 1.0)
    token = (np.arange(THIRDS)[None, :, None] * (PIX // THIRDS) + np.arange(P)[:, None, None] * COLS + np.arange(COLS)[None, None, :]).reshape(P, TILES)
    const[:, CF["id_hi"][0]:CF["id_hi"][1]] = token >> 7
    const[:, CF["id_lo"][0]:CF["id_lo"][1]] = token & 127
    const[:, CF["magic"][0]] = -MAGIC
    digits = np.zeros((P, len(SHIFTS), CAND), np.int32)
    for r, s in enumerate(SHIFTS):
        digits[:, r, :] = [(j << s) if (s or j < 2) else 0 for j in range(CAND)]
    cb = np.zeros((P, NCB), np.float32)
    cb[:, 0:P] = 1.0
    cb[:, P:2 * P] = np.arange(P)[:, None] < np.arange(P)[None, :]
    cb[:, 2 * P:3 * P] = np.arange(P)[None, :]
    return fwd, inv, const, digits, cb.astype(bf)


def kernel(**inputs):
    import numpy as _np
    import concourse.bacc as _bacc
    from concourse import mybir as _mybir
    from concourse.bass_utils import run_bass_kernel_spmd as _run

    a = {k: _np.asarray(v) for k, v in inputs.items()}
    fwd, inv, const, digits, cb = bases()
    arrays = {
        "x": a["x"].reshape(C, PIX).T,
        "wq": a["L0_conv_Wq"].T,
        "wv": a["L0_conv_Wv"].T,
        "bias": _np.broadcast_to(_np.concatenate([a["L0_conv_bq"], a["L0_conv_bv"], a["L0_ffn_b2"]])[None], (3, 3 * C)),
        "wr": _np.broadcast_to(a["L0_ffn_wr"].reshape(1, C), (P, C)),
        "br": _np.broadcast_to(a["L0_ffn_br"].reshape(1, 1), (P, 1)),
        "w1": a["L0_ffn_w1"],
        "b1": a["L0_ffn_b1"].reshape(HT, P).T,
        "w2": a["L0_ffn_w2"],
        "const_f": const, "const_i": digits, "const_b": cb, "fwd_basis": fwd, "inv_basis": inv,
    }
    nc = _bacc.Bacc("TRN2", target_bir_lowering=False, num_devices=1)
    feeds, args = {}, []
    for name, arr in arrays.items():
        arr = _np.ascontiguousarray(arr)
        feeds["in_" + name] = arr
        args.append(nc.dram_tensor("in_" + name, arr.shape, _mybir.dt.from_np(arr.dtype), kind="ExternalInput").ap())
    args.append(nc.dram_tensor("out_tokens", (PIX, C), _mybir.dt.float32, kind="ExternalOutput").ap())
    layer_kernel(nc, *args)
    r = _run(nc, [feeds], core_ids=[0])
    got = r.results[0]["out_tokens"]
    return _np.ascontiguousarray(got.T).reshape(1, C, SIDE, SIDE)
```

```python
import concourse.bass as bass
from concourse import mybir
from contextlib import ExitStack
import numpy as np

P = 128
C = 256
HALVES = C // P
SIDE = 96
PIX = SIDE * SIDE
THIRDS = 3
COLS = PIX // THIRDS // P
STEPS = 6
TPC = COLS // STEPS
CHUNK = TPC * P
NCHUNK = THIRDS * STEPS
TILES = THIRDS * COLS
TPS = THIRDS * TPC
GROUPS = 8
HID = 1024
HT = HID // P
KEEP = PIX // 2 - 1
FT = (KEEP + P - 1) // P
FSTEPS = FT // TPS
ROW = C + 4
EPS_C, EPS_T = 1e-6, 1e-5
MAGIC = float(2 ** 23)
HALF = 0.5 - 2.0 ** -15
DIGIT = 3
SHIFTS = list(range(28, 0, -DIGIT)) + [0]
CAND = 1 << DIGIT
NOSLOT = 8191


def frequencies():
    pairs = [(0, 1), (1, 0), (1, 1), (1, -1)]
    lone = [(-2, v) for v in range(-2, 2)] + [(u, -2) for u in range(-1, 2)]
    return pairs, lone


NFUN = 23


def parts_of_products(n_exact, n):
    rows = []
    for i in range(n):
        for a, b in ((0, 0), (0, 1), (1, 0), (1, 1), (0, 2), (2, 0)):
            if i >= n_exact or b == 0:
                rows.append((i, a, b))
    return rows


REAL_ROWS = parts_of_products(1, NFUN)
IMAG_ROWS = parts_of_products(0, 14)
R1 = P
R2 = len(REAL_ROWS) - P
RI = len(IMAG_ROWS)
R2_AT = 96

CF = {}
at = 0
for name, width in (("ident", P), ("sel_r1", P), ("sel_r2", P), ("sel_im", P), ("mask_r1", 3), ("mask_r2", 3),
                    ("mask_im", 3), ("mask_b", 3), ("id_hi", TILES), ("id_lo", TILES), ("magic", 1)):
    CF[name] = (at, at + width)
    at += width
NCF = at
CB = {"ones": (0, P), "tri": (P, 2 * P), "iota": (2 * P, 3 * P)}
NCB = 3 * P


def layer_kernel(nc, x, wq, wv, bias, wr, br, w1, b1, w2, const_f, const_i, const_b, fwd_basis,
                 inv_basis, out):
    f32, bf16, i32 = mybir.dt.float32, mybir.dt.bfloat16, mybir.dt.int32
    u32, f32r = mybir.dt.uint32, mybir.dt.float32r
    ALU = mybir.AluOpType
    ACT = mybir.ActivationFunctionType
    AX = mybir.AxisListType

    table = nc.dram_tensor("token_table", [PIX, ROW], f32, kind="Internal").ap()

    def by_step(ap):
        return ap.rearrange("(b p k j) n -> b k p (j n)", b=THIRDS, p=P, k=STEPS)

    x_v, out_v, table_v = by_step(x), by_step(out), by_step(table)

    ctx = ExitStack()
    with ctx:
        def sb(name, shape, dt=f32, until=ctx):
            return until.enter_context(nc.sbuf_tensor(name, shape, dt))

        def sem(name):
            return ctx.enter_context(nc.semaphore(name))

        wq_s = sb("wq_s", [P, HALVES, C])
        wv_s = sb("wv_s", [P, HALVES, C])
        cf = sb("cf", [P, NCF])
        ci = sb("ci", [P, len(SHIFTS), CAND], i32)
        cb = sb("cb", [P, NCB], bf16)
        wr_s = sb("wr_s", [P, C])
        br_s = sb("br_s", [P, 1])
        b1_s = sb("b1_s", [P, HT])
        bias_f = sb("bias_f", [3, 3 * C])
        bias_s = sb("bias_s", [3, 3 * C], bf16)
        stats = sb("stats", [P, TPS, 6])
        mean = sb("mean_s", [P, TPS])[:, :]
        small = sb("small", [P, 14, TPS])
        ext = sb("ext", [P, 2, HALVES, NCHUNK])
        fin = sb("fin", [P, 6, HALVES])
        coef_r1 = sb("coef_r1", [P, C], bf16)
        coef_r2 = sb("coef_r2", [P, C], bf16)
        coef_im = sb("coef_im", [P, C], bf16)
        qmax = sb("qmax", [P, TPC, GROUPS, THIRDS])
        gate = sb("gate", [P, TPC, THIRDS * GROUPS])
        qm = sb("qm", [P, TPC, GROUPS])
        w_all = sb("w_all", [P, TILES])
        junk = sb("junk", [P, 1])
        unused = sb("unused", [P, TPC, C], bf16)
        idx = sb("idx", [P, FT], i32)
        idx_get = sb("idx_get", [P, THIRDS, TPC], i32)
        idx_put = sb("idx_put", [P, THIRDS, TPC], i32)

        early = ExitStack()
        rows = sb("rows", [P, THIRDS, COLS, ROW], until=early)
        vcm = sb("vcm", [P, THIRDS, STEPS, HALVES * CHUNK], until=early)
        arena = sb("arena", [P, 10752], until=early)
        early.close()

        w1_hi, w1_lo = (sb(f"w1_{x}", [P, HALVES, HID], f32r) for x in ("hi", "lo"))
        w2_hi, w2_lo = (sb(f"w2_{x}", [P, HT, C], f32r) for x in ("hi", "lo"))
        raw = ExitStack()
        w1_raw = sb("w1_raw", [P, HALVES, HID], until=raw)
        w2_raw = sb("w2_raw", [P, HT, C], until=raw)
        raw.close()
        hid_hi, hid_lo = [None] * THIRDS, [None] * THIRDS
        hid_hi[2], hid_lo[2] = (sb(f"hid_{x}2", [P, HT, CHUNK], f32r) for x in ("hi", "lo"))
        got = [sb(f"got{b}", [P, TPC, ROW]) for b in range(THIRDS)]
        ln_tok = sb("ln_tok", [P, TPC, C])
        ln_hi = [sb(f"ln_hi{b}", [P, HALVES, CHUNK], f32r) for b in range(THIRDS)]
        ln_lo = [sb(f"ln_lo{b}", [P, HALVES, CHUNK], f32r) for b in range(THIRDS)]
        act_out = sb("act_out", [P, 4, CHUNK])
        res = sb("res", [P, TPC, C])
        for b in (0, 1):
            hid_hi[b], hid_lo[b] = (sb(f"hid_{x}{b}", [P, HT, CHUNK], f32r) for x in ("hi", "lo"))
        ps = ctx.enter_context(nc.psum_tensor("ps", [P, 8, 512], f32))

        def const(name):
            return cf[:, CF[name][0]:CF[name][1]]

        def constb(name):
            return cb[:, CB[name][0]:CB[name][1]]

        ident = const("ident")

        def words(at_, *dims, dt=f32):
            n = int(np.prod(dims))
            flat = arena[:, at_:at_ + (n if dt != bf16 else n // 2)]
            if dt != f32:
                flat = flat.bitcast(dt)
            return flat

        v_tok = [words(1024 * b, TPC, C).rearrange("p (j c) -> p j c", c=C) for b in range(THIRDS)]
        absv = [words(1024 * b, 1024) for b in range(THIRDS)]
        lev = [words(3072 + 1024 * b, 1024) for b in range(THIRDS)]
        q_tok = [words(6144 + 512 * b, TPC, C, dt=bf16).rearrange("p (j c) -> p j c", c=C) for b in range(THIRDS)]
        fwd = words(7680, TILES, 3 * NFUN, dt=bf16).rearrange("p (t m) -> p t m", m=3 * NFUN)
        sums = words(0, C)[0:3 * NFUN, :]
        resid = [words(256 + 256 * i, C) for i in range(3)]
        part = [words(1024 + 128 * i, C, dt=bf16) for i in range(3)]
        picked = [words(2048 + 256 * i, C) for i in range(2)]
        v_st = [words(1024 * b, 1024) for b in range(THIRDS)]
        gated = [words(3072 + 1024 * b, 1024) for b in range(THIRDS)]
        squares = [words(6144 + 1024 * h, 1024).rearrange("p (r n) -> p r n", r=2) for h in range(HALVES)]
        mag = words(8192, 1024)
        inv = [words(9216 + 512 * b, 1024, dt=bf16).rearrange("p (s n) -> p s n", s=2) for b in range(THIRDS)]
        u_w = words(0, TILES)
        cmp_t = words(128, CAND * TILES).rearrange("p (j t) -> p j t", j=CAND)
        cand = [words(768 + 8 * i, CAND, dt=i32) for i in range(2)]
        passed = words(800, CAND, dt=i32)
        masked = words(816, CAND, dt=i32)
        prefix = words(832, 1, dt=i32)
        cnt_f = words(840, CAND)
        cnt_b = words(848, CAND, dt=bf16)
        sc4 = words(860, 16)
        gt_m, eq_m, rank_t, sel_t, tmp_t = (words(900 + 80 * i, TILES) for i in range(5))
        ones_t = words(1300, TILES)
        slot_i, hi_i, lo_i = (words(1400 + 80 * i, TILES, dt=i32) for i in range(3))
        hi_f, lo_f = words(1640, TILES), words(1720, TILES)
        oh_lo = words(1800, TILES, P, dt=bf16).rearrange("p (t s) -> p t s", s=P)
        oh_hi = words(6500, TILES, FT, dt=bf16).rearrange("p (t s) -> p t s", s=FT)
        oh_id = words(8000, TILES, 2 * FT, dt=bf16).rearrange("p (t s) -> p t s", s=2 * FT)

        consts_in = sem("consts_in")
        fwd_in = sem("fwd_in")
        x_in = [sem(f"x_in{b}") for b in range(THIRDS)]
        s1_stats = sem("s1_stats")
        s1_sd = sem("s1_sd")
        s1_norm = sem("s1_norm")
        s1_vtok = sem("s1_vtok")
        s1_tr = sem("s1_tr")
        s1_vcm = sem("s1_vcm")
        s1_ext = sem("s1_ext")
        s1_scale = sem("s1_scale")
        s2_abs = sem("s2_abs")
        s2_lev = sem("s2_lev")
        s2_tr = sem("s2_tr")
        s2_q = sem("s2_q")
        s2_dft = sem("s2_dft")
        s2_split = sem("s2_split")
        s2_sums = sem("s2_sums")
        s2_coef = sem("s2_coef")
        s2_done = sem("s2_done")
        inv_in = [sem(f"inv_in{b}") for b in range(THIRDS)]
        s3_ri = sem("s3_ri")
        s3_sq = sem("s3_sq")
        s3_sum = sem("s3_sum")
        s3_mag = sem("s3_mag")
        s3_q = sem("s3_q")
        s3_qmax = sem("s3_qmax")
        s3_qsteps = sem("s3_qsteps")
        s3_gate = sem("s3_gate")
        s3_vst = sem("s3_vst")
        s3_v = sem("s3_v")
        s3_gated = sem("s3_gated")
        s3_x1 = sem("s3_x1")
        s3_stats = sem("s3_stats")
        s3_sd = sem("s3_sd")
        s3_tail = sem("s3_tail")
        s3_w = sem("s3_w")
        s3_wsteps = sem("s3_wsteps")
        s3_rows = sem("s3_rows")
        s3_base = sem("s3_base")
        base_out = sem("base_out")
        table_out = sem("table_out")
        s4_step = sem("s4_step")
        s4_cnt = sem("s4_cnt")
        s4_tot = sem("s4_tot")
        s4_hot = sem("s4_hot")
        s4_ids = sem("s4_ids")
        s4_idx = sem("s4_idx")
        w_in = sem("w_in")
        w_hi = sem("w_hi")
        w_parts = sem("w_parts")
        s5_idx = sem("s5_idx")
        got_in = [sem(f"got_in{b}") for b in range(THIRDS)]
        s5_ln = sem("s5_ln")
        s5_base = sem("s5_base")
        s5_tr = sem("s5_tr")
        s5_lnch = sem("s5_lnch")
        s5_h = sem("s5_h")
        s5_gelu = sem("s5_gelu")
        s5_hi = sem("s5_hi")
        s5_split = sem("s5_split")
        s5_y = sem("s5_y")
        s5_res = sem("s5_res")
        scat = [sem(f"scat{b}") for b in range(THIRDS)]

        N1 = 8
        N3 = 8

        block = ctx.enter_context(nc.Block())

        @block.sync
        def _(sp):
            sp.dma_start(cf[:, :], const_f).then_inc(consts_in, 16)
            for b in range(THIRDS):
                sp.dma_start(rows[:, b, 0:TPC, 0:C], x_v[b, 0].rearrange("p (j n) -> p j n", j=TPC)).then_inc(x_in[b], 16)
            sp.dma_start(cb[:, :], const_b).then_inc(consts_in, 16)
            sp.dma_start(ci[:, :, :], const_i).then_inc(consts_in, 16)
            sp.dma_start(wq_s[:, :, :], wq.rearrange("(h p) n -> p h n", p=P)).then_inc(consts_in, 16)
            sp.dma_start(wv_s[:, :, :], wv.rearrange("(h p) n -> p h n", p=P)).then_inc(consts_in, 16)
            sp.dma_start(wr_s[:, :], wr).then_inc(consts_in, 16)
            sp.dma_start(br_s[:, :], br).then_inc(consts_in, 16)
            sp.dma_start(b1_s[:, :], b1).then_inc(consts_in, 16)
            sp.dma_start(bias_f[:, :], bias).then_inc(consts_in, 16)
            sp.dma_start(fwd, fwd_basis).then_inc(fwd_in, 16)
            with sp.Fori(1, STEPS) as k:
                for b in range(THIRDS):
                    sp.wait_ge(x_in[b], 16 * k)
                    sp.dma_start(rows[:, b, bass.ds(TPC * k, TPC), 0:C],
                                 x_v[b, bass.ds(k, 1)].rearrange("k p (j n) -> p (k j) n", j=TPC)).then_inc(x_in[b], 16)
            sp.wait_ge(s2_dft, NCHUNK)
            for b in range(THIRDS):
                sp.dma_start(inv[b], inv_basis[b, 0]).then_inc(inv_in[b], 16)

            def store_rows(k):
                for b in range(THIRDS):
                    sp.wait_ge(s3_rows, k + 1)
                    sp.dma_start(table_v[b, bass.ds(k, 1)].rearrange("k p (j n) -> p (k j) n", j=TPC),
                                 rows[:, b, bass.ds(TPC * k, TPC), :]).then_inc(table_out, 16)

            def store_base(k):
                for b in range(THIRDS):
                    sp.wait_ge(s3_base, THIRDS * k + b + 1)
                    sp.dma_start(out_v[b, bass.ds(k, 1)].rearrange("k p n -> p k n"),
                                 vcm[:, b, bass.ds(k, 1), :]).then_inc(base_out, 16)

            def load_inv(k):
                for b in range(THIRDS):
                    sp.wait_ge(s3_ri, HALVES * (THIRDS * (k - 1) + b + 1))
                    sp.dma_start(inv[b], inv_basis[b, bass.ds(k, 1)].rearrange("k p s n -> p (k s) n")).then_inc(inv_in[b], 16)

            load_inv(1)
            load_inv(2)
            with sp.Fori(3, STEPS) as k:
                load_inv(k)
                store_rows(k - 3)
                store_base(k - 3)
            with sp.Fori(STEPS - 3, STEPS) as k:
                store_rows(k)
                store_base(k)
            sp.wait_ge(base_out, 16 * NCHUNK)
            sp.wait_ge(table_out, 16 * NCHUNK)
            sp.dma_start(w1_raw[:, :, :], w1.rearrange("(h p) n -> p h n", p=P)).then_inc(w_in, 16)
            sp.dma_start(w2_raw[:, :, :], w2.rearrange("(t p) n -> p t n", p=P)).then_inc(w_in, 16)

        @block.gpsimd
        def _(pool):
            def add_x(k):
                for b in range(THIRDS):
                    pool.wait_ge(s3_gated, 2 * (THIRDS * k + b + 1))
                    xr = rows[:, b, bass.ds(TPC * k, TPC), 0:C]
                    pool.tensor_tensor(xr, xr, gated[b].rearrange("p (j c) -> p j c", c=C), ALU.add).then_inc(s3_x1, 1)

            with pool.Fori(0, STEPS) as k:
                add_x(k)

            pool.wait_ge(w_hi, 2)
            for raw_w, hi, lo in ((w1_raw, w1_hi, w1_lo), (w2_raw, w2_hi, w2_lo)):
                pool.tensor_tensor(lo[:, :, :], raw_w[:, :, :], hi[:, :, :].bitcast(f32), ALU.subtract).then_inc(w_parts, 1)

            def gather(b):
                for j in range(TPC):
                    pool.indirect_dma_start(got[b][:, j, :], None, table[:, :],
                                            bass.IndirectOffsetOnAxis(idx_get[:, b, j:j + 1].bitcast(u32), 0)).then_inc(got_in[b], 16)

            def scatter(b, short=False):
                for j in range(TPC):
                    n = KEEP - P * (FT - 1) if short and j == TPC - 1 else P
                    pool.indirect_dma_start(out[:, :], bass.IndirectOffsetOnAxis(idx_put[0:n, b, j:j + 1].bitcast(u32), 0),
                                            res[0:n, j, :], None).then_inc(scat[b], 16)

            pool.wait_ge(table_out, 16 * NCHUNK)
            pool.wait_ge(base_out, 16 * NCHUNK)
            pool.wait_ge(s5_idx, 1)
            for b in range(THIRDS):
                gather(b)
            for f in range(FSTEPS):
                for b in range(THIRDS):
                    last = f == FSTEPS - 1
                    pool.wait_ge(s5_idx, THIRDS * f + b + 2)
                    pool.wait_ge(s5_res, 2 * (THIRDS * f + b + 1))
                    if not last:
                        gather(b)
                    scatter(b, short=last and b == THIRDS - 1)
            for b in range(THIRDS):
                pool.wait_ge(scat[b], 16 * TPC * FSTEPS)

        @block.scalar
        def _(act):
            act.wait_ge(consts_in, 16 * 9)

            def stage1(k):
                act.wait_ge(s1_stats, N1 * k + 4)
                act.activation(small[:, 1, :], small[:, 0, :], ACT.Sqrt).then_inc(s1_sd, 1)
                act.wait_ge(s1_norm, k + 1)
                for b in range(THIRDS):
                    for j in range(TPC):
                        t = TPC * b + j
                        ins = act.activation(v_tok[b][:, j, :], rows[:, b, bass.ds(TPC * k + j, 1), 0:C].rearrange("p k n -> p (k n)"),
                                             ACT.Identity, bias=small[:, 5, t:t + 1], scale=small[:, 4, t:t + 1])
                    ins.then_inc(s1_vtok, 1)
                for b in range(THIRDS):
                    act.wait_ge(s1_tr, THIRDS * k + b + 1)
                    act.activation(vcm[:, b, bass.ds(k, 1), :].rearrange("p k n -> p (k n)"),
                                   ps[:, 2 * b:2 * b + 2, :].rearrange("p a n -> p (a n)"), ACT.Copy).then_inc(s1_vcm, 1)

            with act.Fori(0, STEPS) as k:
                stage1(k)

            def scaled_abs(k, b):
                for h in range(HALVES):
                    ins = act.activation(absv[b][:, h * CHUNK:(h + 1) * CHUNK],
                                         vcm[:, b, bass.ds(k, 1), h * CHUNK:(h + 1) * CHUNK].rearrange("p k n -> p (k n)"),
                                         ACT.Abs, scale=fin[:, 3, h:h + 1])
                ins.then_inc(s2_abs, 1)

            def unmagic(k, b):
                act.wait_ge(s2_tr, THIRDS * k + b + 1)
                act.activation(q_tok[b].rearrange("p j c -> p (j c)"), ps[:, 2 * b:2 * b + 2, :].rearrange("p a n -> p (a n)"),
                               ACT.Identity, bias=const("magic")).then_inc(s2_q, 1)

            act.wait_ge(s1_scale, 1)
            for b in range(THIRDS):
                scaled_abs(0, b)
            with act.Fori(1, STEPS) as k:
                for b in range(THIRDS):
                    unmagic(k - 1, b)
                    scaled_abs(k, b)
            for b in range(THIRDS):
                unmagic(STEPS - 1, b)

            def squares_of(k, b):
                for h in range(HALVES):
                    act.wait_ge(s3_ri, HALVES * (THIRDS * k + b) + h + 1)
                    if not (isinstance(k, int) and k == 0 and b == 0):
                        act.wait_ge(s3_mag, HALVES * (THIRDS * k + b - 1) + h + 1)
                    act.activation(squares[h].rearrange("p r n -> p (r n)"), ps[:, 2 * h:2 * h + 2, :].rearrange("p a n -> p (a n)"),
                                   ACT.Square).then_inc(s3_sq, 1)

            def roots_of(k, b):
                for h in range(HALVES):
                    act.wait_ge(s3_sum, HALVES * (THIRDS * k + b) + h + 1)
                    if h == 0 and not (isinstance(k, int) and k == 0 and b == 0):
                        act.wait_ge(s3_q, 2 * (THIRDS * k + b))
                    act.activation(mag[:, h * CHUNK:(h + 1) * CHUNK], squares[h][:, 0, :], ACT.Sqrt).then_inc(s3_mag, 1)

            def copy_v(k, b):
                if not isinstance(k, int) or k >= 1:
                    act.wait_ge(s3_v, 2 * (THIRDS * (k - 1) + b + 1))
                act.activation(v_st[b], vcm[:, b, bass.ds(k, 1), :].rearrange("p k n -> p (k n)"), ACT.Copy).then_inc(s3_vst, 1)

            def sd_of(k):
                act.wait_ge(s3_stats, N3 * k + 4)
                act.activation(small[:, 1, :], small[:, 0, :], ACT.Sqrt).then_inc(s3_sd, 1)

            def base_of(k, b):
                act.wait_ge(s3_tail, k + 1)
                for j in range(TPC):
                    r = rows[:, b, bass.ds(TPC * k + j, 1), :].rearrange("p k n -> p (k n)")
                    ins = act.activation(vcm[:, b, bass.ds(k, 1), j * C:(j + 1) * C].rearrange("p k n -> p (k n)"), r[:, 0:C],
                                         ACT.Identity, bias=r[:, C + 1:C + 2], scale=r[:, C + 2:C + 3])
                ins.then_inc(s3_base, 1)

            def stage3(k, query=True, value=True, base=True, ahead=True):
                for b in range(THIRDS):
                    if query:
                        roots_of(k, b)
                        if b + 1 < THIRDS:
                            squares_of(k, b + 1)
                        elif ahead:
                            squares_of(k + 1, 0)
                    if value:
                        copy_v(k - 1, b)
                    if base and b == 0:
                        sd_of(k - 2)
                    if base and b >= 1:
                        base_of(k - 2, b - 1)
                if base:
                    base_of(k - 2, THIRDS - 1)

            squares_of(0, 0)
            stage3(0, value=False, base=False)
            stage3(1, base=False)
            with act.Fori(2, STEPS - 1) as k:
                stage3(k)
            stage3(STEPS - 1, ahead=False)
            stage3(STEPS, query=False)
            stage3(STEPS + 1, query=False, value=False)

            act.wait_ge(w_in, 32)
            act.activation(w1_hi[:, :, :], w1_raw[:, :, :], ACT.Copy).then_inc(w_hi, 1)
            act.activation(w2_hi[:, :, :], w2_raw[:, :, :], ACT.Copy).then_inc(w_hi, 1)

            def gelu(f, b):
                for t in range(HT):
                    n = HT * (THIRDS * f + b) + t
                    act.wait_ge(s5_h, n + 1)
                    if not isinstance(n, int) or n >= 4:
                        act.wait_ge(s5_split, n - 3)
                    act.activation(act_out[:, t % 4, :], ps[:, 2 + (HT * b + t) % 3, :], ACT.Gelu_apprx_tanh,
                                   bias=b1_s[:, t:t + 1]).then_inc(s5_gelu, 1)

            act.wait_ge(s4_idx, 1)
            for b in range(THIRDS):
                gelu(0, b)
            with act.Fori(1, FSTEPS) as f:
                for b in range(THIRDS):
                    gelu(f, b)

        @block.vector
        def _(dve):
            def moments(k, eps, steps, per):
                n = per * k
                dve.wait_ge(steps, n + 1)
                even, odd = stats[:, :, 1:3], stats[:, :, 4:6]
                dve.tensor_tensor(small[:, 8, :], even[:, :, 0], odd[:, :, 0], ALU.add)
                dve.tensor_tensor(small[:, 9, :], even[:, :, 0], odd[:, :, 0], ALU.subtract)
                dve.tensor_tensor(small[:, 10, :], even[:, :, 1], odd[:, :, 1], ALU.add).then_inc(steps, 1)
                dve.wait_ge(steps, n + 2)
                dve.tensor_scalar(mean, small[:, 8, :], 0.5, None, ALU.mult)
                dve.scalar_tensor_tensor(small[:, 11, :], small[:, 9, :], 0.25, small[:, 9, :], ALU.mult, ALU.mult)
                dve.tensor_scalar(small[:, 12, :], small[:, 10, :], 1.0 / C, eps, ALU.mult, ALU.add).then_inc(steps, 1)
                dve.wait_ge(steps, n + 3)
                dve.tensor_tensor(small[:, 0, :], small[:, 11, :], small[:, 12, :], ALU.add).then_inc(steps, 1)

            def rstd(k, steps, per, sd):
                n = per * k + 4
                dve.wait_ge(sd, k + 1)
                dve.reciprocal(small[:, 2, :], small[:, 1, :]).then_inc(steps, 1)
                dve.wait_ge(steps, n + 1)
                dve.tensor_tensor(small[:, 3, :], small[:, 2, :], small[:, 2, :], ALU.mult).then_inc(steps, 1)
                dve.wait_ge(steps, n + 2)
                dve.scalar_tensor_tensor(small[:, 6, :], small[:, 3, :], -0.5, small[:, 0, :], ALU.mult, ALU.mult).then_inc(steps, 1)
                dve.wait_ge(steps, n + 3)
                dve.scalar_tensor_tensor(small[:, 4, :], small[:, 6, :], 1.5, small[:, 2, :], ALU.add, ALU.mult).then_inc(steps, 1)
                dve.wait_ge(steps, n + 4)

            def extremes(k):
                for b in range(THIRDS):
                    dve.wait_ge(s1_vcm, THIRDS * k + b + 1)
                    chunk = vcm[:, b, bass.ds(k, 1), :].rearrange("p k (h n) -> p (k h) n", h=HALVES)
                    for which, op in ((0, ALU.max), (1, ALU.min)):
                        ins = dve.tensor_reduce(ext[:, which, :, bass.ds(THIRDS * k + b, 1)].rearrange("p h k -> p (h k)"), chunk, AX.X, op,
                                                apply_absolute_value=True)
                ins.then_inc(s1_ext, 1)

            dve.wait_ge(consts_in, 16 * 9)

            def stage1(k, reduce=True):
                for b in range(THIRDS):
                    dve.wait_ge(x_in[b], 16 * (k + 1))
                    for j in range(TPC):
                        ins = dve.bn_stats(stats[:, TPC * b + j, :], rows[:, b, bass.ds(TPC * k + j, 1), 0:C].rearrange("p k n -> p (k n)"))
                ins.then_inc(s1_stats, 1)
                moments(k, EPS_C, s1_stats, N1)
                if reduce:
                    extremes(k - 1)
                rstd(k, s1_stats, N1, s1_sd)
                dve.scalar_tensor_tensor(small[:, 5, :], mean, -1.0, small[:, 4, :], ALU.mult, ALU.mult).then_inc(s1_norm, 1)

            stage1(0, reduce=False)
            with dve.Fori(1, STEPS) as k:
                stage1(k)
            extremes(STEPS - 1)

            n = STEPS
            dve.wait_ge(s1_ext, n)
            dve.tensor_reduce(fin[:, 0, :], ext[:, 0, :, :], AX.X, ALU.max)
            dve.tensor_reduce(fin[:, 1, :], ext[:, 1, :, :], AX.X, ALU.min).then_inc(s1_ext, 1)
            dve.wait_ge(s1_ext, n + 1)
            dve.tensor_tensor(fin[:, 2, :], fin[:, 0, :], fin[:, 1, :], ALU.subtract).then_inc(s1_ext, 1)
            dve.wait_ge(s1_ext, n + 2)
            dve.reciprocal(fin[:, 5, :], fin[:, 2, :]).then_inc(s1_ext, 1)
            dve.wait_ge(s1_ext, n + 3)
            dve.tensor_scalar(fin[:, 3, :], fin[:, 5, :], 255.0, None, ALU.mult).then_inc(s1_ext, 1)
            dve.wait_ge(s1_ext, n + 4)
            dve.scalar_tensor_tensor(fin[:, 5, :], fin[:, 1, :], -1.0, fin[:, 3, :], ALU.mult, ALU.mult).then_inc(s1_ext, 1)
            dve.wait_ge(s1_ext, n + 5)
            dve.tensor_scalar(fin[:, 4, :], fin[:, 5, :], -HALF, None, ALU.add).then_inc(s1_scale, 1)

            def levels(k):
                for b in range(THIRDS):
                    dve.wait_ge(s2_abs, THIRDS * k + b + 1)
                    if not isinstance(k, int) or k >= 1:
                        dve.wait_ge(s2_tr, THIRDS * (k - 1) + b + 1)
                    for h in range(HALVES):
                        ins = dve.tensor_scalar(lev[b][:, h * CHUNK:(h + 1) * CHUNK], absv[b][:, h * CHUNK:(h + 1) * CHUNK],
                                                fin[:, 4, h:h + 1], MAGIC, ALU.add, ALU.add)
                    ins.then_inc(s2_lev, 1)

            dve.wait_ge(s1_scale, 1)
            levels(0)
            with dve.Fori(1, STEPS) as k:
                levels(k)

            splits = [0]

            def step(ins):
                splits[0] += 1
                ins.then_inc(s2_split, 1)
                dve.wait_ge(s2_split, splits[0])

            def split(dst, src, mask, n, width):
                r0, r1 = resid[1][n, 0:width], resid[2][n, 0:width]
                pt = [p_[n, 0:width] for p_ in part]
                pk = [p_[n, 0:width] for p_ in picked]
                step(dve.tensor_copy(pt[0], src))
                step(dve.tensor_tensor(r0, src, pt[0], ALU.subtract))
                step(dve.tensor_copy(pt[1], r0))
                step(dve.tensor_tensor(r1, r0, pt[1], ALU.subtract))
                step(dve.tensor_copy(pt[2], r1))
                step(dve.tensor_scalar(pk[0], pt[0], mask[:, 0:1], None, ALU.mult))
                step(dve.scalar_tensor_tensor(pk[1], pt[1], mask[:, 1:2], pk[0], ALU.mult, ALU.add))
                step(dve.scalar_tensor_tensor(dst, pt[2], mask[:, 2:3], pk[1], ALU.mult, ALU.add))

            dve.wait_ge(s2_dft, NCHUNK)
            dve.tensor_copy(sums, ps[0:3 * NFUN, 6, 0:C]).then_inc(s2_sums, 1)
            for i in range(3):
                split(bias_s[:, i * C:(i + 1) * C], bias_f[:, i * C:(i + 1) * C], const("mask_b")[0:3, :], slice(0, 3), C)
            dve.wait_ge(s2_coef, 3)
            for dst, bank, name, n in ((coef_r1, 0, "mask_r1", slice(0, R1)), (coef_r2, 1, "mask_r2", slice(R2_AT, R2_AT + R2)),
                                       (coef_im, 2, "mask_im", slice(0, RI))):
                split(dst[n, :], ps[n, bank, 0:C], const(name)[n, :], n, C)
            dve.tensor_copy(junk[:, :], const("magic")).then_inc(s2_done, 1)

            def add_squares(k, b):
                for h in range(HALVES):
                    dve.wait_ge(s3_sq, HALVES * (THIRDS * k + b) + h + 1)
                    dve.tensor_tensor(squares[h][:, 0, :], squares[h][:, 0, :], squares[h][:, 1, :], ALU.add).then_inc(s3_sum, 1)

            def query_max(k, b):
                for jj in range(2):
                    dve.wait_ge(s3_q, 2 * (THIRDS * k + b) + jj + 1)
                    dve.tensor_reduce(qmax[:, 2 * jj:2 * jj + 2, :, b], ps[:, 4 + jj, :].rearrange("p (j g m) -> p j m g", j=2, m=GROUPS),
                                      AX.X, ALU.max).then_inc(s3_qmax, 1)

            def gate_of(k):
                dve.wait_ge(s3_qmax, 2 * THIRDS * (k + 1))
                if not isinstance(k, int) or k >= 1:
                    dve.wait_ge(s3_gated, 2 * THIRDS * k)
                dve.tensor_reduce(qm[:, :, :], qmax[:, :, :, :].rearrange("p j m b -> p j (m b)").rearrange("p j (a r) -> p j r a", a=THIRDS),
                                  AX.X, ALU.max).then_inc(s3_qsteps, 1)
                dve.wait_ge(s3_qsteps, k + 1)
                for a in range(THIRDS):
                    ins = dve.tensor_scalar(gate[:, :, a * GROUPS:(a + 1) * GROUPS], qm[:, :, :], 1.0, None, ALU.add)
                ins.then_inc(s3_gate, 1)

            def gated_value(k, b):
                for jj in range(2):
                    dve.wait_ge(s3_v, 2 * (THIRDS * k + b) + jj + 1)
                    dve.wait_ge(s3_gate, k + 1)
                    if not isinstance(k, int) or k >= 1:
                        dve.wait_ge(s3_x1, THIRDS * (k - 1) + b + 1)
                    g = gate[:, 2 * jj:2 * jj + 2, :].rearrange("p j (m b) -> p j b m", b=THIRDS)[:, :, b:b + 1, :]
                    dve.tensor_tensor(gated[b][:, jj * 512:(jj + 1) * 512].rearrange("p (j g m) -> p j g m", j=2, m=GROUPS),
                                      ps[:, 6 + jj, :].rearrange("p (j g m) -> p j g m", j=2, m=GROUPS),
                                      g.broadcast_to([P, 2, C // GROUPS, GROUPS]), ALU.mult).then_inc(s3_gated, 1)

            def row(k, b, j):
                return rows[:, b, bass.ds(TPC * k + j, 1), :].rearrange("p k n -> p (k n)")

            def statistics(k, b):
                dve.wait_ge(s3_x1, THIRDS * k + b + 1)
                for j in range(TPC):
                    ins = dve.bn_stats(stats[:, TPC * b + j, :], row(k, b, j)[:, 0:C])
                if b == THIRDS - 1:
                    ins.then_inc(s3_stats, 1)

            def tails(k):
                rstd(k, s3_stats, N3, s3_sd)
                for b in range(THIRDS):
                    tail = rows[:, b, bass.ds(TPC * k, TPC), C:ROW]
                    ts = slice(TPC * b, TPC * (b + 1))
                    dve.tensor_copy(tail[:, :, 0], small[:, 4, ts])
                    dve.scalar_tensor_tensor(tail[:, :, 1], mean[:, ts], -1.0, small[:, 4, ts], ALU.mult, ALU.mult)
                    ins = dve.tensor_scalar(tail[:, :, 2], small[:, 4, ts], 1.0, None, ALU.add)
                ins.then_inc(s3_tail, 1)

            def router_sum(k, b):
                if b == 0:
                    dve.wait_ge(s3_stats, N3 * k + 4)
                if not (isinstance(k, int) and k == 0 and b == 0):
                    dve.wait_ge(s3_w, THIRDS * k + b)
                for j in range(TPC):
                    t = TPC * b + j
                    ins = dve.scalar_tensor_tensor(unused[:, j, :],
                                                   row(k, b, j)[:, 0:C], mean[:, t:t + 1], wr_s[:, :],
                                                   ALU.subtract, ALU.mult, accum_out=small[:, 7, t:t + 1])
                ins.then_inc(s3_w, 1)

            def router(k):
                dve.wait_ge(s3_w, THIRDS * (k + 1))
                dve.tensor_tensor(small[:, 13, :], small[:, 7, :], small[:, 4, :], ALU.mult).then_inc(s3_wsteps, 1)
                dve.wait_ge(s3_wsteps, k + 1)
                for b in range(THIRDS):
                    ts = slice(TPC * b, TPC * (b + 1))
                    dve.tensor_scalar(rows[:, b, bass.ds(TPC * k, TPC), C + 3], small[:, 13, ts], br_s[:, 0:1], None, ALU.add)
                    ins = dve.tensor_scalar(w_all[:, bass.ds(COLS * b + TPC * k, TPC)], small[:, 13, ts], br_s[:, 0:1], None, ALU.add)
                ins.then_inc(s3_rows, 1)

            def stage3(k, query=True, value=True, weigh=True, ahead=True):
                for b in range(THIRDS):
                    if query:
                        if b + 1 < THIRDS:
                            add_squares(k, b + 1)
                        elif ahead:
                            add_squares(k + 1, 0)
                    if weigh:
                        if b == 0:
                            statistics(k - 2, THIRDS - 1)
                            moments(k - 2, EPS_T, s3_stats, N3)
                        if b == 1:
                            tails(k - 2)
                        router_sum(k - 2, b)
                    if query:
                        query_max(k, b)
                    if value:
                        if b > 0:
                            statistics(k - 1, b - 1)
                        gated_value(k - 1, b)
                if weigh:
                    router(k - 2)
                if query:
                    gate_of(k)

            add_squares(0, 0)
            stage3(0, value=False, weigh=False)
            stage3(1, weigh=False)
            with dve.Fori(2, STEPS - 1) as k:
                stage3(k)
            stage3(STEPS - 1, ahead=False)
            stage3(STEPS, query=False)
            stage3(STEPS + 1, query=False, value=False)

            count = [0]

            def link(ins):
                count[0] += 1
                ins.then_inc(s4_step, 1)
                dve.wait_ge(s4_step, count[0])

            totals = [0]

            def total(width):
                totals[0] += 1
                dve.wait_ge(s4_tot, totals[0])
                return ps[:, 0, 0:width]

            dve.wait_ge(s3_rows, STEPS)
            dve.wait_ge(s3_base, NCHUNK)
            sign, target, wstar, need = (sc4[:, i:i + 1] for i in range(4))
            link(dve.tensor_scalar(u_w, w_all[:, :], 0.0, 0.0, ALU.is_ge, ALU.add, accum_out=cnt_f[:, 0:1]))
            dve.tensor_copy(cnt_b[:, 0:1], cnt_f[:, 0:1]).then_inc(s4_cnt, 1)
            link(dve.tensor_scalar(sc4[:, 4:5], total(1), float(KEEP), None, ALU.is_ge))
            link(dve.tensor_scalar(sign, sc4[:, 4:5], 2.0, -1.0, ALU.mult, ALU.add))
            link(dve.tensor_scalar(target, sc4[:, 4:5], float(2 * KEEP - PIX - 1), float(PIX - KEEP + 1), ALU.mult, ALU.add))
            link(dve.tensor_scalar(u_w, w_all[:, :], sign, None, ALU.mult))
            link(dve.tensor_copy(cand[0], ci[:, 0, :]))
            for r in range(len(SHIFTS)):
                c = cand[r % 2].bitcast(f32)
                link(dve.tensor_tensor(cmp_t, u_w.rearrange("p (a t) -> p a t", a=1).broadcast_to([P, CAND, TILES]),
                                       c.rearrange("p (j a) -> p j a", a=1).broadcast_to([P, CAND, TILES]), ALU.is_ge))
                with nc.allow_low_precision(reason="a partition's count is at most 72, exact in bfloat16"):
                    dve.tensor_reduce(cnt_b, cmp_t, AX.X, ALU.add).then_inc(s4_cnt, 1)
                link(dve.tensor_scalar(passed, total(CAND), target, -1.0, ALU.is_ge, ALU.mult))
                link(dve.tensor_tensor(masked, passed, cand[r % 2], ALU.bitwise_and))
                link(dve.tensor_reduce(prefix.bitcast(f32), masked.bitcast(f32), AX.X, ALU.max))
                if r + 1 < len(SHIFTS):
                    link(dve.tensor_tensor(cand[(r + 1) % 2], prefix.broadcast_to([P, CAND]), ci[:, r + 1, :], ALU.bitwise_or))
            link(dve.tensor_scalar(wstar, prefix.bitcast(f32), sign, None, ALU.mult))
            link(dve.memset(ones_t, 1.0))
            link(dve.tensor_scalar(gt_m, w_all[:, :], wstar, 0.0, ALU.is_gt, ALU.add, accum_out=cnt_f[:, 0:1]))
            link(dve.tensor_scalar(eq_m, w_all[:, :], wstar, None, ALU.is_equal))
            link(dve.tensor_reduce(cnt_f[:, 1:4], eq_m.rearrange("p (b t) -> p b t", b=THIRDS), AX.X, ALU.add))
            dve.tensor_copy(cnt_b[:, 0:4], cnt_f[:, 0:4]).then_inc(s4_cnt, 1)
            tot = total(8)
            link(dve.tensor_copy(cnt_f[:, 0:8], tot))
            link(dve.tensor_scalar(need, cnt_f[:, 0:1], -1.0, float(KEEP), ALU.mult, ALU.add))
            link(dve.tensor_tensor(cnt_f[:, 6:7], cnt_f[:, 6:7], cnt_f[:, 1:2], ALU.add))
            link(dve.tensor_tensor(cnt_f[:, 7:8], cnt_f[:, 7:8], cnt_f[:, 1:2], ALU.add))
            link(dve.tensor_tensor(cnt_f[:, 7:8], cnt_f[:, 7:8], cnt_f[:, 2:3], ALU.add))
            for b in range(THIRDS):
                s = slice(b * COLS, (b + 1) * COLS)
                link(dve.tensor_tensor_scan(rank_t[:, s], ones_t[:, s], eq_m[:, s], cnt_f[:, 5 + b:6 + b], ALU.mult, ALU.add))
            link(dve.scalar_tensor_tensor(tmp_t, rank_t, need, eq_m, ALU.is_le, ALU.mult))
            link(dve.tensor_tensor(sel_t, tmp_t, gt_m, ALU.add))
            link(dve.tensor_reduce(cnt_f[:, 0:1], sel_t, AX.X, ALU.add))
            dve.tensor_copy(cnt_b[:, 0:1], cnt_f[:, 0:1]).then_inc(s4_cnt, 1)
            tot = total(8)
            link(dve.tensor_copy(cnt_f[:, 0:8], tot))
            link(dve.tensor_tensor_scan(rank_t, ones_t, sel_t, cnt_f[:, 4:5], ALU.mult, ALU.add))
            link(dve.tensor_tensor(rank_t, rank_t, sel_t, ALU.mult))
            link(dve.tensor_scalar(tmp_t, sel_t, float(-NOSLOT - 1), float(NOSLOT), ALU.mult, ALU.add))
            link(dve.tensor_tensor(slot_i, rank_t, tmp_t, ALU.add))
            link(dve.tensor_single_scalar(hi_i, slot_i, 7, ALU.arith_shift_right))
            link(dve.tensor_single_scalar(lo_i, slot_i, P - 1, ALU.bitwise_and))
            link(dve.tensor_copy(hi_f, hi_i))
            link(dve.tensor_copy(lo_f, lo_i))
            for t in range(TILES):
                dve.tensor_scalar(oh_lo[:, t, :], constb("iota"), lo_f[:, t:t + 1], None, ALU.is_equal)
            wide = [P, TILES, FT]

            def by_tile(v):
                return v.rearrange("p (t a) -> p t a", a=1).broadcast_to(wide)

            link(dve.tensor_tensor(oh_hi, constb("iota")[:, 0:FT].rearrange("p (a s) -> p a s", a=1).broadcast_to(wide), by_tile(hi_f), ALU.is_equal))
            dve.tensor_tensor(oh_id[:, :, 0:FT], oh_hi, by_tile(const("id_hi")), ALU.mult)
            dve.tensor_tensor(oh_id[:, :, FT:2 * FT], oh_hi, by_tile(const("id_lo")), ALU.mult).then_inc(s4_hot, 1)
            dve.wait_ge(s4_ids, 1)
            link(dve.tensor_copy(cmp_t[:, 0, 0:2 * FT], ps[:, 1, 0:2 * FT]))
            dve.scalar_tensor_tensor(idx[:, :], cmp_t[:, 0, 0:FT], float(P), cmp_t[:, 0, FT:2 * FT], ALU.mult, ALU.add).then_inc(s4_idx, 1)

            def later(f, b, n):
                return f + (b + n) // THIRDS, (b + n) % THIRDS

            def rows_in(f, b):
                c = THIRDS * f + b
                dve.wait_ge(got_in[b], 16 * TPC * (f + 1))
                if not isinstance(c, int) or c >= 1:
                    dve.wait_ge(s5_tr, c)
                for j in range(TPC):
                    ins = dve.tensor_scalar(ln_tok[:, j, :], got[b][:, j, 0:C], got[b][:, j, C:C + 1], got[b][:, j, C + 1:C + 2], ALU.mult, ALU.add)
                ins.then_inc(s5_ln, 1)
                dve.wait_ge(s5_ln, c + 1)
                for j in range(TPC):
                    ins = dve.tensor_scalar(got[b][:, j, 0:C], got[b][:, j, 0:C], got[b][:, j, C + 2:C + 3], got[b][:, j, C + 1:C + 2], ALU.mult, ALU.add)
                ins.then_inc(s5_base, 1)

            def channels(f, b):
                c = THIRDS * f + b
                dve.wait_ge(s5_tr, c + 1)
                dve.tensor_copy(ln_hi[b][:, :, :], ps[:, 0:2, :]).then_inc(s5_lnch, 1)
                dve.wait_ge(s5_lnch, 2 * c + 1)
                dve.tensor_tensor(ln_lo[b][:, :, :], ps[:, 0:2, :], ln_hi[b][:, :, :].bitcast(f32), ALU.subtract).then_inc(s5_lnch, 1)

            def splits(f, b, ts):
                n0 = HT * (THIRDS * f + b)
                for t in ts:
                    dve.wait_ge(s5_gelu, n0 + t + 1)
                    dve.tensor_copy(hid_hi[b][:, t, :], act_out[:, t % 4, :]).then_inc(s5_hi, 1)
                    dve.wait_ge(s5_hi, n0 + t + 1)
                    dve.tensor_tensor(hid_lo[b][:, t, :], act_out[:, t % 4, :], hid_hi[b][:, t, :].bitcast(f32), ALU.subtract).then_inc(s5_split, 1)

            def place_idx(f, b, ahead=True):
                if not isinstance(f, int) or f >= 1:
                    dve.wait_ge(scat[b], 16 * TPC * f)
                ins = dve.tensor_copy(idx_put[:, b, :], idx[:, bass.ds(TPS * f + TPC * b, TPC)])
                if ahead:
                    ins = dve.tensor_copy(idx_get[:, b, :], idx[:, bass.ds(TPS * (f + 1) + TPC * b, TPC)])
                ins.then_inc(s5_idx, 1)

            def result(f, b):
                c = THIRDS * f + b
                dve.wait_ge(s5_base, c + 1)
                pf, pb = later(f, b, -1)
                if not isinstance(c, int) or c >= 1:
                    dve.wait_ge(scat[pb], 16 * TPC * (pf + 1))
                for jj in range(2):
                    dve.wait_ge(s5_y, 2 * c + jj + 1)
                    for j in (2 * jj, 2 * jj + 1):
                        ins = dve.scalar_tensor_tensor(res[:, j, :], ps[:, 5 + jj, (j % 2) * C:(j % 2 + 1) * C], got[b][:, j, C + 3:C + 4],
                                                       got[b][:, j, 0:C], ALU.mult, ALU.add)
                    ins.then_inc(s5_res, 1)

            def stage5(f, b, one=True, two=True):
                if one:
                    splits(*later(f, b, 1), range(0, 4))
                if two:
                    rows_in(*later(f, b, 2))
                if one:
                    splits(*later(f, b, 1), range(4, HT))
                if two:
                    channels(*later(f, b, 2))
                place_idx(f, b, ahead=not isinstance(f, int) or f < FSTEPS - 1)
                result(f, b)

            dve.wait_ge(s4_idx, 1)
            dve.wait_ge(table_out, 16 * NCHUNK)
            dve.wait_ge(base_out, 16 * NCHUNK)
            dve.tensor_copy(idx_get[:, :, :].rearrange("p b j -> p (b j)"), idx[:, 0:TPS]).then_inc(s5_idx, 1)
            rows_in(0, 0)
            channels(0, 0)
            rows_in(0, 1)
            splits(0, 0, range(0, 4))
            channels(0, 1)
            splits(0, 0, range(4, HT))
            for b in range(THIRDS):
                stage5(0, b)
            with dve.Fori(1, FSTEPS - 1) as f:
                for b in range(THIRDS):
                    stage5(f, b)
            for b in range(THIRDS):
                stage5(FSTEPS - 1, b, one=b + 1 < THIRDS, two=b + 2 < THIRDS)

        @block.tensor
        def _(pe):
            pe.wait_ge(consts_in, 16 * 9)

            def transpose1(k):
                for b in range(THIRDS):
                    pe.wait_ge(s1_vtok, THIRDS * k + b + 1)
                    if not isinstance(k, int) or k >= 1:
                        pe.wait_ge(s1_vcm, THIRDS * (k - 1) + b + 1)
                    for h in range(HALVES):
                        for j in range(TPC):
                            ins = pe.transpose(ps[:, 2 * b + h, j * P:(j + 1) * P], v_tok[b][:, j, h * P:(h + 1) * P], ident)
                    ins.then_inc(s1_tr, 1)

            transpose1(0)
            with pe.Fori(1, STEPS) as k:
                transpose1(k)

            def transpose2(k, b):
                pe.wait_ge(s2_lev, THIRDS * k + b + 1)
                if isinstance(k, int) and k == 0:
                    pe.wait_ge(s1_vcm, THIRDS * (STEPS - 1) + b + 1)
                else:
                    pe.wait_ge(s2_q, THIRDS * (k - 1) + b + 1)
                for j in range(TPC):
                    for h in range(HALVES):
                        ins = pe.transpose(ps[:, 2 * b + j // 2, (j % 2) * C + h * P:(j % 2) * C + (h + 1) * P],
                                           lev[b][:, h * CHUNK + j * P:h * CHUNK + (j + 1) * P], ident)
                ins.then_inc(s2_tr, 1)

            def fourier(k, b, first=False, last=False):
                pe.wait_ge(s2_q, THIRDS * k + b + 1)
                for j in range(TPC):
                    ins = pe.matmul(ps[0:3 * NFUN, 6, 0:C], fwd[:, bass.ds(COLS * b + TPC * k + j, 1), :].rearrange("p k m -> p (k m)"),
                                    q_tok[b][:, j, :], start=first and j == 0, stop=last and j == TPC - 1)
                ins.then_inc(s2_dft, 1)

            pe.wait_ge(fwd_in, 16)
            for b in range(THIRDS):
                transpose2(0, b)
            for b in range(THIRDS):
                fourier(0, b, first=b == 0)
            with pe.Fori(1, STEPS - 1) as k:
                for b in range(THIRDS):
                    transpose2(k, b)
                for b in range(THIRDS):
                    fourier(k, b)
            for b in range(THIRDS):
                transpose2(STEPS - 1, b)
            for b in range(THIRDS):
                fourier(STEPS - 1, b, last=b == THIRDS - 1)

            pe.wait_ge(s2_sums, 1)
            for bank, name, n in ((0, "sel_r1", R1), (1, "sel_r2", R2_AT + R2), (2, "sel_im", RI)):
                pe.matmul(ps[0:n, bank, 0:C], const(name)[0:3 * NFUN, 0:n], sums, start=True, stop=True).then_inc(s2_coef, 1)
            pe.wait_ge(s2_done, 1)

            def invert(k, b):
                pe.wait_ge(inv_in[b], 16 * (k + 1))
                for h in range(HALVES):
                    if not (isinstance(k, int) and k == 0 and b == 0):
                        pe.wait_ge(s3_sq, HALVES * (THIRDS * k + b - 1) + h + 1)
                    cs = slice(h * P, (h + 1) * P)
                    pe.matmul(ps[:, 2 * h, :], coef_r1[:, cs], inv[b][:, 0, :], start=True, stop=False)
                    pe.matmul(ps[:, 2 * h, :], coef_r2[R2_AT:R2_AT + R2, cs], inv[b][R2_AT:R2_AT + R2, 1, :], start=False, stop=True)
                    pe.matmul(ps[:, 2 * h + 1, :], coef_im[0:RI, cs], inv[b][0:RI, 1, :], start=True, stop=True).then_inc(s3_ri, 1)

            def product(k, b, lhs, bank, w, bias_i, ready, done, used):
                for jj in range(2):
                    for j in (2 * jj, 2 * jj + 1):
                        o = ps[:, bank + jj, (j % 2) * C:(j % 2 + 1) * C]
                        if j % 2 == 0:
                            used(jj)
                        pe.matmul(o, constb("ones")[0:3, :], bias_s[:, bias_i * C:(bias_i + 1) * C], start=True, stop=False)
                        for h in range(HALVES):
                            if jj == 0 and j == 0:
                                ready(h)
                            ins = pe.matmul(o, lhs[:, h * CHUNK + j * P:h * CHUNK + (j + 1) * P], w[:, h, :], start=False, stop=h == HALVES - 1)
                    ins.then_inc(done, 1)

            def query(k, b):
                product(k, b, mag, 4, wq_s, 0, lambda h: pe.wait_ge(s3_mag, HALVES * (THIRDS * k + b) + h + 1), s3_q,
                        lambda jj: None if isinstance(k, int) and k == 0 and b == 0 else pe.wait_ge(s3_qmax, 2 * (THIRDS * k + b - 1) + jj + 1))

            def value(k, b):
                product(k, b, v_st[b], 6, wv_s, 1, lambda h: pe.wait_ge(s3_vst, THIRDS * k + b + 1), s3_v,
                        lambda jj: None if isinstance(k, int) and k == 0 and b == 0 else pe.wait_ge(s3_gated, 2 * (THIRDS * k + b - 1) + jj + 1))

            def stage3(k, ahead=True, first=False):
                for b in range(THIRDS):
                    if b + 1 < THIRDS:
                        invert(k, b + 1)
                    elif ahead:
                        invert(k + 1, 0)
                    query(k, b)
                    if not first:
                        value(k - 1, b)

            invert(0, 0)
            stage3(0, first=True)
            stage3(1)
            with pe.Fori(2, STEPS - 1) as k:
                stage3(k)
            stage3(STEPS - 1, ahead=False)
            for b in range(THIRDS):
                value(STEPS - 1, b)

            n_rounds = len(SHIFTS)
            for i in range(n_rounds + 3):
                pe.wait_ge(s4_cnt, i + 1)
                width = 1 if i == 0 else CAND if i <= n_rounds else 4
                prefixes = i > n_rounds
                ins = pe.matmul(ps[:, 0, 0:width], constb("ones"), cnt_b[:, 0:width], start=True, stop=True)
                if prefixes:
                    ins = pe.matmul(ps[:, 0, 4:8], constb("tri"), cnt_b[:, 0:4], start=True, stop=True)
                ins.then_inc(s4_tot, 1)
            pe.wait_ge(s4_hot, 1)
            for t in range(TILES):
                ins = pe.matmul(ps[:, 1, 0:2 * FT], oh_lo[:, t, :], oh_id[:, t, :], start=t == 0, stop=t == TILES - 1)
            ins.then_inc(s4_ids, 1)

            def later(f, b, n):
                return f + (b + n) // THIRDS, (b + n) % THIRDS

            def transpose5(f, b):
                c = THIRDS * f + b
                pe.wait_ge(s5_ln, c + 1)
                if not isinstance(c, int) or c >= 1:
                    pe.wait_ge(s5_lnch, 2 * c)
                for h in range(HALVES):
                    for j in range(TPC):
                        ins = pe.transpose(ps[:, h, j * P:(j + 1) * P], ln_tok[:, j, h * P:(h + 1) * P], ident)
                ins.then_inc(s5_tr, 1)

            def hidden(f, b):
                c = THIRDS * f + b
                pe.wait_ge(s5_lnch, 2 * (c + 1))
                for t in range(HT):
                    n = HT * c + t
                    if not isinstance(n, int) or n >= 3:
                        pe.wait_ge(s5_gelu, n - 2)
                    o = ps[:, 2 + (HT * b + t) % 3, :]
                    ws = slice(t * P, (t + 1) * P)
                    products = [(w, x, h) for h in range(HALVES) for w, x in ((w1_hi, ln_hi), (w1_hi, ln_lo), (w1_lo, ln_hi))]
                    for i, (w, x, h) in enumerate(products):
                        ins = pe.matmul(o, w[:, h, ws], x[b][:, h, :], start=i == 0, stop=i == len(products) - 1)
                    ins.then_inc(s5_h, 1)

            def second(f, b):
                c = THIRDS * f + b
                pe.wait_ge(s5_split, HT * (c + 1))
                for jj in range(2):
                    if not isinstance(c, int) or c >= 1:
                        pe.wait_ge(s5_res, 2 * (c - 1) + jj + 1)
                    for j in (2 * jj, 2 * jj + 1):
                        o = ps[:, 5 + jj, (j % 2) * C:(j % 2 + 1) * C]
                        pe.matmul(o, constb("ones")[0:3, :], bias_s[:, 2 * C:3 * C], start=True, stop=False)
                        for t in range(HT):
                            js = slice(j * P, (j + 1) * P)
                            for x, w in ((hid_hi, w2_hi), (hid_hi, w2_lo), (hid_lo, w2_hi)):
                                last = t == HT - 1 and x is hid_lo
                                ins = pe.matmul(o, x[b][:, t, js], w[:, t, :], start=False, stop=last)
                    ins.then_inc(s5_y, 1)

            def stage5(f, b, one=True, two=True):
                if one:
                    hidden(*later(f, b, 1))
                if two:
                    transpose5(*later(f, b, 2))
                second(f, b)

            transpose5(0, 0)
            pe.wait_ge(w_parts, 2)
            hidden(0, 0)
            transpose5(0, 1)
            for b in range(THIRDS):
                stage5(0, b)
            with pe.Fori(1, FSTEPS - 1) as f:
                for b in range(THIRDS):
                    stage5(f, b)
            for b in range(THIRDS):
                stage5(FSTEPS - 1, b, one=b + 1 < THIRDS, two=b + 2 < THIRDS)


def bases():
    bf = mybir.dt.np(mybir.dt.bfloat16)
    pairs, lone = frequencies()
    pix = np.arange(PIX)
    y, x = pix // SIDE, pix % SIDE
    funs = [np.ones(PIX)]
    for u, v in pairs + lone:
        turn = 2 * np.pi * ((u * y + v * x) % SIDE) / SIDE
        funs += [np.cos(turn), np.sin(turn)]
    funs = np.stack(funs)

    def parts(a):
        out_, rest = [], a.astype(np.float64)
        for _ in range(3):
            p_ = rest.astype(bf)
            out_.append(p_)
            rest = rest - p_.astype(np.float64)
        return out_

    fp = np.stack(parts(funs))
    cube = fp.reshape(3, NFUN, THIRDS, P, COLS)
    fwd = np.ascontiguousarray(cube.transpose(3, 2, 4, 0, 1)).reshape(P, TILES * 3 * NFUN)
    flat = cube.reshape(3, NFUN, THIRDS, P, STEPS, TPC).transpose(0, 1, 2, 4, 5, 3).reshape(3, NFUN, THIRDS, STEPS, CHUNK)
    inv = np.zeros((THIRDS, STEPS, P, 2, CHUNK), bf)
    for r, (i, _, b) in enumerate(REAL_ROWS[:P]):
        inv[:, :, r, 0] = flat[b, i]
    n0 = 1 + 2 * len(pairs)
    for r, (i, _, b) in enumerate(IMAG_ROWS):
        inv[:, :, r, 1] = flat[b, n0 + i]
    const = np.zeros((P, NCF), np.float32)

    def put(name, rows_, cols, val):
        const[rows_, CF[name][0] + cols] = val

    for p_ in range(P):
        put("ident", p_, p_, 1.0)
    n = float(PIX)
    for r, (i, a, _) in enumerate(REAL_ROWS):
        name, col = ("sel_r1", r) if r < P else ("sel_r2", R2_AT + r - P)
        mask = "mask_r1" if r < P else "mask_r2"
        w = (2.0 if 0 < i < n0 else 1.0) / n
        for part_ in range(3):
            put(name, part_ * NFUN + i, col, w)
        put(mask, col, a, 1.0)
        if r >= P:
            inv[:, :, col, 1] = flat[REAL_ROWS[r][2], i]
    for r, (i, a, _) in enumerate(IMAG_ROWS):
        src, w = (i - 1, 1.0 / n) if i % 2 else (i + 1, -1.0 / n)
        for part_ in range(3):
            put("sel_im", part_ * NFUN + n0 + src, r, w)
        put("mask_im", r, a, 1.0)
    for part_ in range(3):
        put("mask_b", part_, part_, 1.0)
    token = (np.arange(THIRDS)[None, :, None] * (PIX // THIRDS) + np.arange(P)[:, None, None] * COLS + np.arange(COLS)[None, None, :]).reshape(P, TILES)
    const[:, CF["id_hi"][0]:CF["id_hi"][1]] = token >> 7
    const[:, CF["id_lo"][0]:CF["id_lo"][1]] = token & 127
    const[:, CF["magic"][0]] = -MAGIC
    digits = np.zeros((P, len(SHIFTS), CAND), np.int32)
    for r, s in enumerate(SHIFTS):
        digits[:, r, :] = [(j << s) if (s or j < 2) else 0 for j in range(CAND)]
    cb = np.zeros((P, NCB), np.float32)
    cb[:, 0:P] = 1.0
    cb[:, P:2 * P] = np.arange(P)[:, None] < np.arange(P)[None, :]
    cb[:, 2 * P:3 * P] = np.arange(P)[None, :]
    return fwd, inv, const, digits, cb.astype(bf)


def kernel(**inputs):
    import numpy as _np
    import concourse.bacc as _bacc
    from concourse import mybir as _mybir
    from concourse.bass_utils import run_bass_kernel_spmd as _run

    a = {k: _np.asarray(v) for k, v in inputs.items()}
    fwd, inv, const, digits, cb = bases()
    arrays = {
        "x": a["x"].reshape(C, PIX).T,
        "wq": a["L0_conv_Wq"].T,
        "wv": a["L0_conv_Wv"].T,
        "bias": _np.broadcast_to(_np.concatenate([a["L0_conv_bq"], a["L0_conv_bv"], a["L0_ffn_b2"]])[None], (3, 3 * C)),
        "wr": _np.broadcast_to(a["L0_ffn_wr"].reshape(1, C), (P, C)),
        "br": _np.broadcast_to(a["L0_ffn_br"].reshape(1, 1), (P, 1)),
        "w1": a["L0_ffn_w1"],
        "b1": a["L0_ffn_b1"].reshape(HT, P).T,
        "w2": a["L0_ffn_w2"],
        "const_f": const, "const_i": digits, "const_b": cb, "fwd_basis": fwd, "inv_basis": inv,
    }
    nc = _bacc.Bacc("TRN2", target_bir_lowering=False, num_devices=1)
    feeds, args = {}, []
    for name, arr in arrays.items():
        arr = _np.ascontiguousarray(arr)
        feeds["in_" + name] = arr
        args.append(nc.dram_tensor("in_" + name, arr.shape, _mybir.dt.from_np(arr.dtype), kind="ExternalInput").ap())
    args.append(nc.dram_tensor("out_tokens", (PIX, C), _mybir.dt.float32, kind="ExternalOutput").ap())
    layer_kernel(nc, *args)
    r = _run(nc, [feeds], core_ids=[0])
    got = r.results[0]["out_tokens"]
    return _np.ascontiguousarray(got.T).reshape(1, C, SIDE, SIDE)
```

```python
import concourse.bass as bass
from concourse import mybir
from contextlib import ExitStack
import numpy as np

P = 128
C = 256
HALVES = C // P
SIDE = 96
PIX = SIDE * SIDE
THIRDS = 3
COLS = PIX // THIRDS // P
STEPS = 6
TPC = COLS // STEPS
CHUNK = TPC * P
NCHUNK = THIRDS * STEPS
TILES = THIRDS * COLS
TPS = THIRDS * TPC
DVE_TILES = TPC - 1
GROUPS = 8
HID = 1024
HT = HID // P
KEEP = PIX // 2 - 1
FT = (KEEP + P - 1) // P
FSTEPS = FT // TPS
ROW = C + 4
EPS_C, EPS_T = 1e-6, 1e-5
MAGIC = float(2 ** 23)
HALF = 0.5 - 2.0 ** -15
DIGIT = 3
SHIFTS = list(range(28, 0, -DIGIT)) + [0]
CAND = 1 << DIGIT
NO_SIGN = 0x7FFFFFFF
NOSLOT = 8191


def frequencies():
    pairs = [(0, 1), (1, 0), (1, 1), (1, -1)]
    lone = [(-2, v) for v in range(-2, 2)] + [(u, -2) for u in range(-1, 2)]
    return pairs, lone


NFUN = 23


def parts_of_products(n_exact, n):
    rows = []
    for i in range(n):
        for a, b in ((0, 0), (0, 1), (1, 0), (1, 1), (0, 2), (2, 0)):
            if i >= n_exact or b == 0:
                rows.append((i, a, b))
    return rows


REAL_ROWS = parts_of_products(1, NFUN)
IMAG_ROWS = parts_of_products(0, 14)
R1 = P
R2 = len(REAL_ROWS) - P
RI = len(IMAG_ROWS)
R2_AT = 96

CF = {}
at = 0
for name, width in (("ident", P), ("sel_0", P), ("sel_1", P), ("mask_0", 3), ("mask_1", 3), ("mask_b", 3), ("part", 1), ("magic", 1)):
    CF[name] = (at, at + width)
    at += width
NCF = at
CB = {"ones": (0, P), "tri": (P, 2 * P), "iota": (2 * P, 3 * P)}
NCB = 3 * P


def layer_kernel(nc, x, wq, wv, bq, bv, wr, b2, br, w1, b1, w2, const_f, const_i, const_b, fwd_basis,
                 inv_basis, out):
    f32, bf16, i32 = mybir.dt.float32, mybir.dt.bfloat16, mybir.dt.int32
    u32, f32r = mybir.dt.uint32, mybir.dt.float32r
    ALU = mybir.AluOpType
    ACT = mybir.ActivationFunctionType
    AX = mybir.AxisListType

    table = nc.dram_tensor("token_table", [PIX, ROW], f32, kind="Internal").ap()

    def by_step(ap):
        return ap.rearrange("(b p k j) n -> b k p (j n)", b=THIRDS, p=P, k=STEPS)

    x_v, out_v, table_v = by_step(x), by_step(out), by_step(table)

    ctx = ExitStack()
    with ctx:
        def sb(name, shape, dt=f32, until=ctx):
            return until.enter_context(nc.sbuf_tensor(name, shape, dt))

        def sem(name):
            return ctx.enter_context(nc.semaphore(name))

        wq_s = sb("wq_s", [P, HALVES, C])
        wv_s = sb("wv_s", [P, HALVES, C])
        cf = sb("cf", [P, NCF])
        ci = sb("ci", [P, len(SHIFTS), CAND], i32)
        cb = sb("cb", [P, NCB], bf16)
        wr_s = sb("wr_s", [P, C])
        b2_s = sb("b2_s", [P, C])
        br_s = sb("br_s", [P, 1])
        b1_s = sb("b1_s", [P, HT])
        bq_f = sb("bq_f", [3, C])
        bq_s = sb("bq_s", [3, C], bf16)
        bv_s = sb("bv_s", [P, C])
        stats = sb("stats", [P, TPS, 6])
        mean = sb("mean_s", [P, TPS])[:, :]
        small = sb("small", [P, 14, TPS])
        fin = sb("fin", [P, 6, HALVES])
        coef = sb("coef", [P, 2, C], bf16)
        qmax = sb("qmax", [P, TPC, GROUPS, THIRDS])
        gate = sb("gate", [P, TPC, THIRDS * GROUPS])
        qm = sb("qm", [P, TPC, GROUPS])
        w_all = sb("w_all", [P, TILES])
        junk = sb("junk", [P, 1])
        ones_t = sb("ones_t", [P, TILES])[:, :]
        unused = sb("unused", [P, TPC, C], bf16)
        idx = sb("idx", [P, FT], i32)
        idx_get = sb("idx_get", [P, THIRDS, TPC], i32)
        idx_put = sb("idx_put", [P, THIRDS, TPC], i32)

        early = ExitStack()
        rows = sb("rows", [P, THIRDS, COLS, ROW], until=early)
        vabs = sb("vabs", [P, THIRDS, STEPS, TPC * C], until=early)
        arena = sb("arena", [P, 10752], until=early)
        early.close()

        w1_hi, w1_lo = (sb(f"w1_{x}", [P, HALVES, HID], f32r) for x in ("hi", "lo"))
        w2_hi, w2_lo = (sb(f"w2_{x}", [P, HT, C], f32r) for x in ("hi", "lo"))
        raw = ExitStack()
        w1_raw = sb("w1_raw", [P, HALVES, HID], until=raw)
        w2_raw = sb("w2_raw", [P, HT, C], until=raw)
        raw.close()
        hid_hi, hid_lo = [None] * THIRDS, [None] * THIRDS
        hid_hi[2], hid_lo[2] = (sb(f"hid_{x}2", [P, HT, CHUNK], f32r) for x in ("hi", "lo"))
        got = [sb(f"got{b}", [P, TPC, ROW]) for b in range(THIRDS)]
        ln_tok = sb("ln_tok", [P, TPC, C])
        lnt_hi, lnt_lo = (sb(f"lnt_{x}", [P, TPC, C], f32r) for x in ("hi", "lo"))
        ident_r = sb("ident_r", [P, P], f32r)
        ln_hi = [sb(f"ln_hi{b}", [P, HALVES, CHUNK], f32r) for b in range(THIRDS)]
        ln_lo = [sb(f"ln_lo{b}", [P, HALVES, CHUNK], f32r) for b in range(THIRDS)]
        act_out = sb("act_out", [P, 4, CHUNK])
        res = sb("res", [P, TPC, C])
        for b in (0, 1):
            hid_hi[b], hid_lo[b] = (sb(f"hid_{x}{b}", [P, HT, CHUNK], f32r) for x in ("hi", "lo"))
        ps = ctx.enter_context(nc.psum_tensor("ps", [P, 8, 512], f32))

        def const(name):
            return cf[:, CF[name][0]:CF[name][1]]

        def constb(name):
            return cb[:, CB[name][0]:CB[name][1]]

        rows_by_step = rows[:, :, :, :].rearrange("p b (k j) n -> p b k j n", j=TPC)

        def by_tile(v):
            return v.rearrange("p (t a) -> p t a", a=1).broadcast_to([P, TILES, FT])

        rows_by_pair = rows[:, :, :, :].rearrange("p b (i j) n -> p b i j n", j=2)

        def gate_of_third(b):
            g = gate[:, :, :].rearrange("p j (m b) -> p j b m", b=THIRDS)[:, :, b:b + 1, :]
            return g.broadcast_to([P, TPC, C // GROUPS, GROUPS])

        def by_channel(row_, tiles):
            return row_.rearrange("p (a c) -> p a c", a=1).broadcast_to([P, tiles, C])

        ident = const("ident")

        def words(at_, *dims, dt=f32):
            n = int(np.prod(dims))
            flat = arena[:, at_:at_ + (n if dt != bf16 else n // 2)]
            if dt != f32:
                flat = flat.bitcast(dt)
            return flat

        v_tok = [words(1024 * b, TPC, C).rearrange("p (j c) -> p j c", c=C) for b in range(THIRDS)]
        v_st = [words(3072 + 1024 * b, HALVES * CHUNK) for b in range(THIRDS)]
        a_max, a_min = (words(6144 + 1024 * i, TPC * C) for i in range(2))
        fwd = words(8192, TILES, 3 * NFUN, dt=bf16).rearrange("p (t m) -> p t m", m=3 * NFUN)
        resid_b = [vabs[0:3, THIRDS - 1, STEPS - 1 - n, 0:C] for n in range(2)]
        picked_b = [vabs[0:3, THIRDS - 1, STEPS - 3 - n, 0:C] for n in range(2)]
        part_b = [vabs[0:3, 1, STEPS - 1 - n, 0:C // 2].bitcast(bf16) for n in range(3)]
        q_tok = [words(512 * b, TPC, C, dt=bf16) for b in range(THIRDS)]
        fin_wide = words(1536, 2 * HALVES, P).rearrange("p (i n) -> p i n", n=P)
        row_both = words(2048, 2 * C)
        row_scale, row_shift = row_both[:, 0:C], row_both[:, C:2 * C]
        sums = words(0, C)[0:3 * NFUN, :]
        resid, part, picked = ([words(at_ + step * n, 2, C, dt=dt).rearrange("p (a n) -> p a n", a=2) for n in range(count)]
                               for at_, step, count, dt in ((256, 2 * C, 2, f32), (1280, C, 3, bf16), (2048, 2 * C, 2, f32)))
        x_again = [words(3072 + 1024 * b, 1024) for b in range(THIRDS)]
        squares = [words(6144 + 1024 * h, 1024).rearrange("p (r n) -> p r n", r=2) for h in range(HALVES)]
        mag = [words(1024 * b, 1024) for b in range(THIRDS)]
        inv = [words(9216 + 512 * b, 1024, dt=bf16).rearrange("p (s n) -> p s n", s=2) for b in range(THIRDS)]
        u_w = words(0, TILES)
        cmp_t = words(128, CAND * TILES).rearrange("p (j t) -> p j t", j=CAND)
        cand = [words(768 + 8 * i, CAND, dt=i32) for i in range(2)]
        passed = words(800, CAND, dt=i32)
        masked = words(816, CAND, dt=i32)
        prefix = words(832, 1, dt=i32)
        cnt_f = words(840, CAND)
        cnt_b = words(848, CAND, dt=bf16)
        sc4 = words(860, 16)
        gt_m, eq_m, rank_t, sel_t, tmp_t = (words(900 + 80 * i, TILES) for i in range(5))
        slot_i, hi_i, lo_i = (words(1400 + 80 * i, TILES, dt=i32) for i in range(3))
        hi_b = words(1640, TILES, dt=bf16)
        lo_f = words(1720, TILES)
        oh_lo = words(1800, TILES, P, dt=bf16).rearrange("p (t s) -> p t s", s=P)
        oh_hi = words(6500, TILES, FT, dt=bf16).rearrange("p (t s) -> p t s", s=FT)
        oh_id = words(8000, TILES, 2 * FT, dt=bf16).rearrange("p (t s) -> p t s", s=2 * FT)
        id_t, id_p = words(1300, FT), words(1340, FT)
        id_1, id_2, id_3 = (words(1640 + 40 * i, FT) for i in range(3))

        first_in = sem("first_in")
        bias_in = sem("bias_in")
        consts_in = sem("consts_in")
        bias_parts = sem("bias_parts")
        fwd_in = sem("fwd_in")
        x_in = [sem(f"x_in{b}") for b in range(THIRDS)]
        s1_stats = sem("s1_stats")
        s1_sd = sem("s1_sd")
        s1_norm = sem("s1_norm")
        s1_vtok = sem("s1_vtok")
        s1_tr = sem("s1_tr")
        s1_vst = sem("s1_vst")
        s1_val = sem("s1_val")
        s1_out = sem("s1_out")
        s1_biased = sem("s1_biased")
        s1_aabs = sem("s1_aabs")
        s1_abs = sem("s1_abs")
        s1_mm = sem("s1_mm")
        s1_extt = sem("s1_extt")
        s1_ext = sem("s1_ext")
        s1_scale = sem("s1_scale")
        s1_rows = sem("s1_rows")
        s2_rows = sem("s2_rows")
        s2_prod = sem("s2_prod")
        s2_sum = sem("s2_sum")
        s2_pprod = sem("s2_pprod")
        s2_psum = sem("s2_psum")
        s2_q = sem("s2_q")
        s2_dft = sem("s2_dft")
        s2_split = sem("s2_split")
        s2_sums = sem("s2_sums")
        s2_coef = sem("s2_coef")
        s2_done = sem("s2_done")
        inv_in = [sem(f"inv_in{b}") for b in range(THIRDS)]
        s3_ri = sem("s3_ri")
        s3_sq = sem("s3_sq")
        s3_sum = sem("s3_sum")
        s3_psum = sem("s3_psum")
        s3_mag = sem("s3_mag")
        s3_q = sem("s3_q")
        s3_qmax = sem("s3_qmax")
        s3_qsteps = sem("s3_qsteps")
        s3_gate = sem("s3_gate")
        x_back = [sem(f"x_back{b}") for b in range(THIRDS)]
        s3_gated = sem("s3_gated")
        s3_x1 = sem("s3_x1")
        s3_dgated = sem("s3_dgated")
        s3_dx1 = sem("s3_dx1")
        s3_stats = sem("s3_stats")
        s3_sd = sem("s3_sd")
        s3_tail = sem("s3_tail")
        s3_w = sem("s3_w")
        s3_wsteps = sem("s3_wsteps")
        s3_rows = sem("s3_rows")
        s3_base = sem("s3_base")
        base_out = sem("base_out")
        table_out = sem("table_out")
        s4_step = sem("s4_step")
        s4_cnt = sem("s4_cnt")
        s4_tot = sem("s4_tot")
        s4_hi = sem("s4_hi")
        s4_oht = sem("s4_oht")
        s4_hot = sem("s4_hot")
        s4_ids = sem("s4_ids")
        s4_idx = sem("s4_idx")
        w_in = sem("w_in")
        w_hi = sem("w_hi")
        w_parts = sem("w_parts")
        s5_idx = sem("s5_idx")
        got_in = [sem(f"got_in{b}") for b in range(THIRDS)]
        tile_in = [sem(f"tile_in{j}") for j in range(TPC)]
        s5_ln = sem("s5_ln")
        s5_unr = sem("s5_unr")
        s5_base = sem("s5_base")
        ident_in = sem("ident_in")
        s5_lnhi = sem("s5_lnhi")
        s5_lnlo = sem("s5_lnlo")
        s5_tr = sem("s5_tr")
        s5_chhi = sem("s5_chhi")
        s5_chlo = sem("s5_chlo")
        s5_h = sem("s5_h")
        s5_gelu = sem("s5_gelu")
        s5_hi = sem("s5_hi")
        s5_split = sem("s5_split")
        s5_y = sem("s5_y")
        s5_res = sem("s5_res")
        scat = [sem(f"scat{b}") for b in range(THIRDS)]

        N1 = 8
        N3 = 8

        block = ctx.enter_context(nc.Block())

        @block.sync
        def _(sp):
            for b in range(THIRDS):
                sp.dma_start(rows[:, b, 0:TPC, 0:C], x_v[b, 0].rearrange("p (j n) -> p j n", j=TPC)).then_inc(x_in[b], 16)
            sp.dma_start(cf[:, :], const_f).then_inc(first_in, 16)
            sp.dma_start(wv_s[:, :, :], wv.rearrange("(h p) n -> p h n", p=P)).then_inc(first_in, 16)
            sp.dma_start(bq_f[:, :], bq).then_inc(bias_in, 16)
            sp.dma_start(bv_s[:, :], bv).then_inc(bias_in, 16)
            with sp.Fori(1, STEPS) as k:
                for b in range(THIRDS):
                    sp.wait_ge(x_in[b], 16 * k)
                    sp.dma_start(rows[:, b, bass.ds(TPC * k, TPC), 0:C],
                                 x_v[b, bass.ds(k, 1)].rearrange("k p (j n) -> p (k j) n", j=TPC)).then_inc(x_in[b], 16)
            sp.dma_start(cb[:, :], const_b).then_inc(consts_in, 16)
            sp.dma_start(ci[:, :, :], const_i).then_inc(consts_in, 16)
            sp.dma_start(wq_s[:, :, :], wq.rearrange("(h p) n -> p h n", p=P)).then_inc(consts_in, 16)
            sp.dma_start(wr_s[:, :], wr).then_inc(consts_in, 16)
            sp.dma_start(b2_s[:, :], b2).then_inc(consts_in, 16)
            sp.dma_start(br_s[:, :], br).then_inc(consts_in, 16)
            sp.dma_start(b1_s[:, :], b1).then_inc(consts_in, 16)
            sp.dma_start(fwd, fwd_basis).then_inc(fwd_in, 16)
            sp.wait_ge(s2_dft, NCHUNK)
            for b in range(THIRDS):
                sp.dma_start(inv[b], inv_basis[b, 0]).then_inc(inv_in[b], 16)

            def store_rows(k):
                for b in range(THIRDS):
                    sp.wait_ge(s3_rows, k + 1)
                    sp.dma_start(table_v[b, bass.ds(k, 1)].rearrange("k p (j n) -> p (k j) n", j=TPC),
                                 rows[:, b, bass.ds(TPC * k, TPC), :]).then_inc(table_out, 16)

            def store_base(k):
                for b in range(THIRDS):
                    sp.wait_ge(s3_base, THIRDS * k + b + 1)
                    sp.dma_start(out_v[b, bass.ds(k, 1)].rearrange("k p n -> p k n"),
                                 vabs[:, b, bass.ds(k, 1), :]).then_inc(base_out, 16)

            def load_inv(k, b):
                sp.wait_ge(s3_ri, HALVES * (THIRDS * (k - 1) + b + 1))
                sp.dma_start(inv[b], inv_basis[b, bass.ds(k, 1)].rearrange("k p s n -> p (k s) n")).then_inc(inv_in[b], 16)

            def load_x(k, b):
                if not isinstance(k, int) or k >= 1:
                    sp.wait_ge(s3_x1, THIRDS * (k - 1) + b + 1)
                sp.dma_start(x_again[b], x_v[b, bass.ds(k, 1)].rearrange("k p n -> p (k n)")).then_inc(x_back[b], 16)

            sp.wait_ge(s2_done, 1)
            for b in range(THIRDS):
                load_x(0, b)
            for b in range(THIRDS):
                load_inv(1, b)
            for b in range(THIRDS):
                load_inv(2, b)
                load_x(1, b)
            load_inv(3, 0)
            load_inv(3, 1)
            load_inv(3, 2)
            for b in range(THIRDS):
                load_x(2, b)
            with sp.Fori(4, STEPS) as k:
                load_inv(k, 0)
                load_inv(k, 1)
                store_rows(k - 4)
                load_inv(k, 2)
                load_x(k - 1, 0)
                load_x(k - 1, 1)
                store_base(k - 4)
                load_x(k - 1, 2)
            store_rows(STEPS - 4)
            for b in range(THIRDS):
                load_x(STEPS - 1, b)
            store_base(STEPS - 4)
            with sp.Fori(STEPS - 3, STEPS) as k:
                store_rows(k)
                store_base(k)
            sp.wait_ge(base_out, 16 * NCHUNK)
            sp.wait_ge(table_out, 16 * NCHUNK)
            sp.dma_start(w1_raw[:, :, :], w1.rearrange("(h p) n -> p h n", p=P)).then_inc(w_in, 16)
            sp.dma_start(w2_raw[:, :, :], w2.rearrange("(t p) n -> p t n", p=P)).then_inc(w_in, 16)

        @block.gpsimd
        def _(pool):
            pool.memset(ones_t, 1.0)
            pool.memset(a_max, 0.0)
            pool.memset(a_min, 3.0e38).then_inc(s1_mm, 1)

            def value_bias(k, b):
                pool.wait_ge(s1_out, 2 * (THIRDS * k + b + 1))
                r = rows[:, b, bass.ds(TPC * k, TPC), 0:C]
                pool.tensor_tensor(r, r, by_channel(bv_s[:, :], TPC), ALU.add).then_inc(s1_biased, 1)

            pool.wait_ge(bias_in, 16 * 2)
            with pool.Fori(0, STEPS - 1) as k:
                for b in range(THIRDS):
                    value_bias(k, b)

            def scale_shift(k):
                pairs = ((1, DVE_TILES, TPC), (2, 0, TPC))
                for b, j0, j1 in pairs:
                    v = vabs[:, b, bass.ds(k, 1), j0 * C:j1 * C].rearrange("p k (j c) -> p (k j) c", c=C)
                    ins = pool.tensor_tensor(v, v, by_channel(row_scale, j1 - j0), ALU.mult)
                ins.then_inc(s2_pprod, 1)
                pool.wait_ge(s2_pprod, k + 1)
                for b, j0, j1 in pairs:
                    v = vabs[:, :, :, :].rearrange("p b k (j c) -> p b (k j) c", c=C)[:, b, bass.ds(TPC * k + j0, j1 - j0), :]
                    ins = pool.tensor_tensor(v, v, by_channel(row_shift, j1 - j0), ALU.add)
                ins.then_inc(s2_psum, 1)

            pool.wait_ge(s2_rows, 1)
            with pool.Fori(0, STEPS) as k:
                scale_shift(k)

            for b in range(THIRDS):
                value_bias(STEPS - 1, b)

            def gate_add(k, b):
                pool.wait_ge(s3_gate, k + 1)
                r = rows[:, b, bass.ds(TPC * k, TPC), 0:C].rearrange("p j (g m) -> p j g m", m=GROUPS)
                pool.tensor_tensor(r, r, gate_of_third(b), ALU.mult).then_inc(s3_gated, 1)
                pool.wait_ge(x_back[b], 16 * (k + 1))
                pool.wait_ge(s3_gated, THIRDS * k + b + 1)
                r = rows_by_step[:, b, bass.ds(k, 1), :, 0:C].rearrange("p k j c -> p (k j) c")
                pool.tensor_tensor(r, r, x_again[b].rearrange("p (j c) -> p j c", c=C), ALU.add).then_inc(s3_x1, 1)

            def pool_squares(k):
                for h in range(HALVES):
                    pool.wait_ge(s3_sq, HALVES * (THIRDS * k + THIRDS - 1) + h + 1)
                    pool.tensor_tensor(squares[h][:, 0, :], squares[h][:, 0, :], squares[h][:, 1, :], ALU.add).then_inc(s3_psum, 1)

            pool_squares(0)
            pool.wait_ge(s1_biased, NCHUNK)
            with pool.Fori(0, STEPS - 1) as k:
                gate_add(k, 0)
                pool_squares(k + 1)
                gate_add(k, 1)
                gate_add(k, 2)
            gate_add(STEPS - 1, 0)
            gate_add(STEPS - 1, 1)

            pool.wait_ge(w_hi, 2)
            for raw_w, hi, lo in ((w1_raw, w1_hi, w1_lo), (w2_raw, w2_hi, w2_lo)):
                pool.tensor_tensor(lo[:, :, :], raw_w[:, :, :], hi[:, :, :].bitcast(f32), ALU.subtract).then_inc(w_parts, 1)

            def gather(b, arrived=None):
                for j in range(TPC):
                    pool.indirect_dma_start(got[b][:, j, :], None, table[:, :],
                                            bass.IndirectOffsetOnAxis(idx_get[:, b, j:j + 1].bitcast(u32), 0)).then_inc(arrived[j] if arrived else got_in[b], 16)

            def scatter(b, short=False, js=range(TPC)):
                for j in js:
                    n = KEEP - P * (FT - 1) if short and j == TPC - 1 else P
                    pool.indirect_dma_start(out[:, :], bass.IndirectOffsetOnAxis(idx_put[0:n, b, j:j + 1].bitcast(u32), 0),
                                            res[0:n, j, :], None).then_inc(scat[b], 16)

            pool.wait_ge(s4_hi, 1)
            pool.tensor_tensor(oh_id[:, :, 0:FT], oh_hi, by_tile(constb("iota")[:, 0:TILES]), ALU.mult).then_inc(s4_oht, 1)

            pool.wait_ge(table_out, 16 * NCHUNK)
            pool.wait_ge(base_out, 16 * NCHUNK)
            pool.wait_ge(s5_idx, 1)
            gather(0, arrived=tile_in)
            for b in range(1, THIRDS):
                gather(b)
            for f in range(FSTEPS):
                for b in range(THIRDS):
                    last = f == FSTEPS - 1
                    pool.wait_ge(s5_idx, THIRDS * f + b + 2)
                    if last and b == THIRDS - 1:
                        for jj in range(2):
                            pool.wait_ge(s5_res, 2 * (THIRDS * f + b) + jj + 1)
                            scatter(b, short=True, js=(2 * jj, 2 * jj + 1))
                    else:
                        pool.wait_ge(s5_res, 2 * (THIRDS * f + b + 1))
                        if not last:
                            gather(b)
                        scatter(b)
            for b in range(THIRDS):
                pool.wait_ge(scat[b], 16 * TPC * FSTEPS)

        @block.scalar
        def _(act):
            def earlier(k, b, n):
                return k + (b - n) // THIRDS, (b - n) % THIRDS

            def sd1_of(k):
                act.wait_ge(s1_stats, N1 * k + 4)
                act.activation(small[:, 1, :], small[:, 0, :], ACT.Sqrt).then_inc(s1_sd, 1)

            def normalise(k, b):
                if b == 0:
                    act.wait_ge(s1_norm, k + 1)
                if not isinstance(k, int) or k >= 1:
                    if b == 0:
                        act.wait_ge(s1_aabs, k)
                    else:
                        act.wait_ge(s1_abs, 2 * (k - 1) + b)
                for j in range(TPC):
                    t = TPC * b + j
                    ins = act.activation(v_tok[b][:, j, :], rows[:, b, bass.ds(TPC * k + j, 1), 0:C].rearrange("p k n -> p (k n)"),
                                         ACT.Identity, bias=small[:, 5, t:t + 1], scale=small[:, 4, t:t + 1])
                ins.then_inc(s1_vtok, 1)

            def absolute(k):
                act.wait_ge(s1_vtok, THIRDS * k + 1)
                act.activation(vabs[:, 0, bass.ds(k, 1), :].rearrange("p k n -> p (k n)"), v_tok[0].rearrange("p j c -> p (j c)"),
                               ACT.Abs).then_inc(s1_aabs, 1)

            def hold_v(k, b):
                act.wait_ge(s1_tr, THIRDS * k + b + 1)
                act.activation(v_st[b], ps[:, 2 * b:2 * b + 2, :].rearrange("p a n -> p (a n)"), ACT.Copy).then_inc(s1_vst, 1)

            def keep_value(k, b):
                for jj, places in enumerate((rows_by_step[:, b, bass.ds(k, 1), :, 0:C], rows_by_pair[:, b, bass.ds(TPC // 2 * k + 1, 1), :, 0:C])):
                    act.wait_ge(s1_val, 2 * (THIRDS * k + b) + jj + 1)
                    act.activation(places.rearrange("p k j c -> p (k j) c")[:, 0:2, :], ps[:, 6 + jj, :].rearrange("p (j c) -> p j c", c=C),
                                   ACT.Copy).then_inc(s1_out, 1)

            def stage1(k, b, new=True, held=True, kept=True, sd=True, early=False):
                if new and early:
                    normalise(k, b)
                if held:
                    hold_v(*earlier(k, b, 1))
                first = isinstance(k, int) and k == 0
                if sd and b == THIRDS - 1 and not first:
                    sd1_of(k + 1)
                if new and not early:
                    normalise(k, b)
                if sd and b == THIRDS - 1 and first:
                    sd1_of(k + 1)
                if new and b == 0:
                    absolute(k)
                if kept:
                    keep_value(*earlier(k, b, 2))

            sd1_of(0)
            for b in range(THIRDS):
                stage1(0, b, held=b >= 1, kept=b >= 2)
            with act.Fori(1, STEPS - 1) as k:
                for b in range(THIRDS):
                    stage1(k, b)
            for b in range(THIRDS):
                stage1(STEPS - 1, b, sd=False, early=b > 0)
            for b in range(2):
                stage1(STEPS, b, new=False, held=b < 1, sd=False)

            def squares_of(k, b):
                for h in range(HALVES):
                    act.wait_ge(s3_ri, HALVES * (THIRDS * k + b) + h + 1)
                    if not (isinstance(k, int) and k == 0 and b == 0):
                        act.wait_ge(s3_mag, HALVES * (THIRDS * k + b - 1) + h + 1)
                    act.activation(squares[h].rearrange("p r n -> p (r n)"), ps[:, 2 * h:2 * h + 2, :].rearrange("p a n -> p (a n)"),
                                   ACT.Square).then_inc(s3_sq, 1)

            def roots_of(k, b):
                for h in range(HALVES):
                    if b < THIRDS - 1:
                        act.wait_ge(s3_sum, HALVES * ((THIRDS - 1) * k + b) + h + 1)
                    else:
                        act.wait_ge(s3_psum, HALVES * k + h + 1)
                    if h == 0 and (not isinstance(k, int) or k >= 1):
                        act.wait_ge(s3_q, 2 * (THIRDS * (k - 1) + b + 1))
                    act.activation(mag[b][:, h * CHUNK:(h + 1) * CHUNK], squares[h][:, 0, :], ACT.Sqrt).then_inc(s3_mag, 1)

            def sd_of(k):
                act.wait_ge(s3_stats, N3 * k + 4)
                act.activation(small[:, 1, :], small[:, 0, :], ACT.Sqrt).then_inc(s3_sd, 1)

            def base_of(k, b):
                act.wait_ge(s3_tail, k + 1)
                for j in range(TPC):
                    r = rows[:, b, bass.ds(TPC * k + j, 1), :].rearrange("p k n -> p (k n)")
                    ins = act.activation(vabs[:, b, bass.ds(k, 1), j * C:(j + 1) * C].rearrange("p k n -> p (k n)"), r[:, 0:C],
                                         ACT.Identity, bias=r[:, C + 1:C + 2], scale=r[:, C + 2:C + 3])
                ins.then_inc(s3_base, 1)

            def stage3(k, query=True, base=True, base_last=True, ahead=True):
                for b in range(THIRDS):
                    if query:
                        roots_of(k, b)
                        if b + 1 < THIRDS:
                            squares_of(k, b + 1)
                        elif ahead:
                            squares_of(k + 1, 0)
                    if base and b == 1:
                        sd_of(k - 2)
                    if base_last and b < THIRDS - 1:
                        base_of(k - 3, b + 1)
                    if base and b == THIRDS - 1:
                        base_of(k - 2, 0)

            squares_of(0, 0)
            stage3(0, base=False, base_last=False)
            stage3(1, base=False, base_last=False)
            stage3(2, base_last=False)
            with act.Fori(3, STEPS - 1) as k:
                stage3(k)
            stage3(STEPS - 1, ahead=False)
            stage3(STEPS, query=False)
            stage3(STEPS + 1, query=False)
            for b in range(1, THIRDS):
                base_of(STEPS - 1, b)

            act.wait_ge(w_in, 32)
            act.activation(w1_hi[:, :, :], w1_raw[:, :, :], ACT.Copy).then_inc(w_hi, 1)
            act.activation(w2_hi[:, :, :], w2_raw[:, :, :], ACT.Copy).then_inc(w_hi, 1)

            act.activation(junk[:, :], br_s[:, :], ACT.Gelu_apprx_tanh)

            def gelu(f, b):
                for t in range(HT):
                    n = HT * (THIRDS * f + b) + t
                    act.wait_ge(s5_h, n + 1)
                    if not isinstance(n, int) or n >= 4:
                        act.wait_ge(s5_split, n - 3)
                    act.activation(act_out[:, t % 4, :], ps[:, 2 + t % 2, :], ACT.Gelu_apprx_tanh,
                                   bias=b1_s[:, t:t + 1]).then_inc(s5_gelu, 1)

            def high(f, b):
                c = THIRDS * f + b
                act.wait_ge(s5_ln, c + 1)
                if not isinstance(c, int) or c >= 1:
                    act.wait_ge(s5_tr, 2 * c - 1)
                act.activation(lnt_hi[:, :, :], ln_tok[:, :, :], ACT.Copy).then_inc(s5_lnhi, 1)

            def channels_low(f, b):
                c = THIRDS * f + b
                act.wait_ge(s5_tr, 2 * (c + 1))
                act.activation(ln_lo[b][:, :, :], ps[:, 6:8, :], ACT.Copy).then_inc(s5_chlo, 1)

            def stage5(f, b, one=True, two=True):
                if one:
                    gelu(*earlier(f, b, -1))
                if two:
                    high(*earlier(f, b, -2))
                    channels_low(*earlier(f, b, -2))

            act.wait_ge(s4_idx, 1)
            high(0, 0)
            channels_low(0, 0)
            high(0, 1)
            gelu(0, 0)
            channels_low(0, 1)
            for b in range(THIRDS):
                stage5(0, b)
            with act.Fori(1, FSTEPS - 1) as f:
                for b in range(THIRDS):
                    stage5(f, b)
            for b in range(THIRDS):
                stage5(FSTEPS - 1, b, one=b + 1 < THIRDS, two=b + 2 < THIRDS)

        @block.vector
        def _(dve):
            def moments(k, eps, steps, per):
                n = per * k
                dve.wait_ge(steps, n + 1)
                even, odd = stats[:, :, 1:3], stats[:, :, 4:6]
                dve.tensor_tensor(small[:, 8, :], even[:, :, 0], odd[:, :, 0], ALU.add)
                dve.tensor_tensor(small[:, 9, :], even[:, :, 0], odd[:, :, 0], ALU.subtract)
                dve.tensor_tensor(small[:, 10, :], even[:, :, 1], odd[:, :, 1], ALU.add).then_inc(steps, 1)
                dve.wait_ge(steps, n + 2)
                dve.tensor_scalar(mean, small[:, 8, :], 0.5, None, ALU.mult)
                dve.scalar_tensor_tensor(small[:, 11, :], small[:, 9, :], 0.25, small[:, 9, :], ALU.mult, ALU.mult)
                dve.tensor_scalar(small[:, 12, :], small[:, 10, :], 1.0 / C, eps, ALU.mult, ALU.add).then_inc(steps, 1)
                dve.wait_ge(steps, n + 3)
                dve.tensor_tensor(small[:, 0, :], small[:, 11, :], small[:, 12, :], ALU.add).then_inc(steps, 1)

            def rstd(k, steps, per, sd, free=None):
                n = per * k + 4
                dve.wait_ge(sd, k + 1)
                dve.reciprocal(small[:, 2, :], small[:, 1, :]).then_inc(steps, 1)
                dve.wait_ge(steps, n + 1)
                dve.tensor_tensor(small[:, 3, :], small[:, 2, :], small[:, 2, :], ALU.mult).then_inc(steps, 1)
                dve.wait_ge(steps, n + 2)
                dve.scalar_tensor_tensor(small[:, 6, :], small[:, 3, :], -0.5, small[:, 0, :], ALU.mult, ALU.mult).then_inc(steps, 1)
                dve.wait_ge(steps, n + 3)
                if free is not None:
                    dve.wait_ge(s1_vtok, free)
                dve.scalar_tensor_tensor(small[:, 4, :], small[:, 6, :], 1.5, small[:, 2, :], ALU.add, ALU.mult).then_inc(steps, 1)
                dve.wait_ge(steps, n + 4)

            splits = [0]

            def split(signal, dst, src, masks, r, p, m):
                def step(*ins):
                    splits[0] += 1
                    ins[-1].then_inc(signal, 1)
                    dve.wait_ge(signal, splits[0])
                step(dve.tensor_copy(p[0], src))
                step(dve.tensor_tensor(r[0], src, p[0], ALU.subtract))
                step(dve.tensor_copy(p[1], r[0]))
                step(dve.tensor_tensor(r[1], r[0], p[1], ALU.subtract))
                step(dve.tensor_copy(p[2], r[1]))
                each = list(enumerate(masks))
                step(*[dve.tensor_scalar(m[0][:, i, :], p[0][:, i, :], mask[:, 0:1], None, ALU.mult) for i, mask in each])
                step(*[dve.scalar_tensor_tensor(m[1][:, i, :], p[1][:, i, :], mask[:, 1:2], m[0][:, i, :], ALU.mult, ALU.add) for i, mask in each])
                step(*[dve.scalar_tensor_tensor(dst[:, i, :], p[2][:, i, :], mask[:, 2:3], m[1][:, i, :], ALU.mult, ALU.add) for i, mask in each])


            def statistics1(k, b):
                dve.wait_ge(x_in[b], 16 * (k + 1))
                for j in range(TPC):
                    ins = dve.bn_stats(stats[:, TPC * b + j, :], rows[:, b, bass.ds(TPC * k + j, 1), 0:C].rearrange("p k n -> p (k n)"))
                if b == THIRDS - 1:
                    ins.then_inc(s1_stats, 1)

            def norm(k):
                rstd(k, s1_stats, N1, s1_sd, free=None if isinstance(k, int) and k == 0 else THIRDS * k)
                dve.scalar_tensor_tensor(small[:, 5, :], mean, -1.0, small[:, 4, :], ALU.mult, ALU.mult).then_inc(s1_norm, 1)

            def extremes(k, b):
                c = THIRDS * k + b
                v = vabs[:, b, bass.ds(k, 1), :].rearrange("p k n -> p (k n)")
                if b == 0:
                    dve.wait_ge(s1_aabs, k + 1)
                else:
                    dve.wait_ge(s1_vtok, c + 1)
                    dve.tensor_single_scalar(v.bitcast(i32), v_tok[b].rearrange("p j c -> p (j c)").bitcast(i32), NO_SIGN, ALU.bitwise_and).then_inc(s1_abs, 1)
                    dve.wait_ge(s1_abs, 2 * k + b)
                dve.wait_ge(s1_mm, c + 1)
                dve.tensor_tensor(a_max, a_max, v, ALU.max)
                dve.tensor_tensor(a_min, a_min, v, ALU.min).then_inc(s1_mm, 1)

            def stage1(k, ahead=True):
                for b in range(THIRDS):
                    if ahead and b < 2:
                        statistics1(k + 1, b)
                    if ahead and b == 1:
                        statistics1(k + 1, 2)
                        moments(k + 1, EPS_C, s1_stats, N1)
                    if ahead and b == THIRDS - 1:
                        norm(k + 1)
                    extremes(k, b)

            for b in range(THIRDS):
                statistics1(0, b)
            moments(0, EPS_C, s1_stats, N1)
            norm(0)
            stage1(0)
            dve.wait_ge(first_in, 16 * 2)
            dve.wait_ge(bias_in, 16 * 2)
            one = [[v.rearrange("p (a n) -> p a n", a=1) for v in vs] for vs in ((bq_s[:, :], bq_f[:, :]), resid_b, part_b, picked_b)]
            split(bias_parts, *one[0], [const("mask_b")[0:3, :]], *one[1:])
            with dve.Fori(1, STEPS - 1) as k:
                stage1(k)
            stage1(STEPS - 1, ahead=False)
            for i, w in enumerate((2 * C, C)):
                dve.wait_ge(s1_mm, NCHUNK + 1 + i)
                dve.tensor_tensor(a_max[:, 0:w], a_max[:, 0:w], a_max[:, w:2 * w], ALU.max)
                dve.tensor_tensor(a_min[:, 0:w], a_min[:, 0:w], a_min[:, w:2 * w], ALU.min).then_inc(s1_mm, 1)
            dve.wait_ge(s1_extt, 1)

            n = 0
            both = ps[:, 1, :].rearrange("p (i h n) -> p i h n", i=2, h=HALVES)
            dve.tensor_reduce(fin[:, 0, :], both[:, 0, :, :], AX.X, ALU.max)
            dve.tensor_reduce(fin[:, 1, :], both[:, 1, :, :], AX.X, ALU.min).then_inc(s1_ext, 1)
            dve.wait_ge(s1_ext, n + 1)
            dve.tensor_tensor(fin[:, 2, :], fin[:, 0, :], fin[:, 1, :], ALU.subtract).then_inc(s1_ext, 1)
            dve.wait_ge(s1_ext, n + 2)
            dve.reciprocal(fin[:, 5, :], fin[:, 2, :]).then_inc(s1_ext, 1)
            dve.wait_ge(s1_ext, n + 3)
            dve.tensor_scalar(fin[:, 3, :], fin[:, 5, :], 255.0, None, ALU.mult).then_inc(s1_ext, 1)
            dve.wait_ge(s1_ext, n + 4)
            dve.scalar_tensor_tensor(fin[:, 5, :], fin[:, 1, :], -1.0, fin[:, 3, :], ALU.mult, ALU.mult).then_inc(s1_ext, 1)
            dve.wait_ge(s1_ext, n + 5)
            dve.tensor_scalar(fin[:, 4, :], fin[:, 5, :], -HALF, None, ALU.add).then_inc(s1_ext, 1)
            dve.wait_ge(s1_ext, n + 6)
            dve.tensor_copy(fin_wide, fin[:, 3:5, :].rearrange("p i (h a) -> p (i h) a", a=1).broadcast_to([P, 2 * HALVES, P])).then_inc(s1_scale, 1)
            dve.wait_ge(s1_rows, 1)
            dve.tensor_copy(row_both, ps[:, 0, 0:2 * C]).then_inc(s2_rows, 1)

            def levels(k):
                for b, tiles in ((0, TPC), (1, DVE_TILES)):
                    v = vabs[:, b, bass.ds(k, 1), 0:tiles * C].rearrange("p k (j c) -> p (k j) c", c=C)
                    dve.tensor_tensor(v, v, by_channel(row_scale, tiles), ALU.mult).then_inc(s2_prod, 1)
                for b, tiles in ((0, TPC), (1, DVE_TILES)):
                    v = vabs[:, b, bass.ds(k, 1), 0:tiles * C].rearrange("p k (j c) -> p (k j) c", c=C)
                    dve.wait_ge(s2_prod, 2 * k + b + 1)
                    dve.tensor_tensor(v, v, by_channel(row_shift, tiles), ALU.add).then_inc(s2_sum, 1)
                for b in range(THIRDS):
                    if b < THIRDS - 1:
                        dve.wait_ge(s2_sum, 2 * k + b + 1)
                    if b > 0:
                        dve.wait_ge(s2_psum, k + 1)
                    if not isinstance(k, int) or k >= 1:
                        dve.wait_ge(s2_dft, THIRDS * (k - 1) + b + 1)
                    dve.tensor_scalar(q_tok[b], vabs[:, b, bass.ds(k, 1), :].rearrange("p k n -> p (k n)"),
                                      MAGIC, -MAGIC, ALU.add, ALU.add).then_inc(s2_q, 1)

            dve.wait_ge(s2_rows, 1)
            levels(0)
            with dve.Fori(1, STEPS) as k:
                levels(k)

            dve.wait_ge(s2_dft, NCHUNK)
            dve.tensor_copy(sums, ps[0:3 * NFUN, 5, 0:C]).then_inc(s2_sums, 1)
            dve.wait_ge(s2_coef, 2)
            splits[0] = 0
            split(s2_split, coef[:, :, :], ps[:, 0:2, 0:C], [const("mask_0"), const("mask_1")], resid, part, picked)
            dve.tensor_copy(junk[:, :], const("magic")).then_inc(s2_done, 1)

            dve.wait_ge(consts_in, 16 * 7)

            def add_squares(k, b):
                for h in range(HALVES):
                    dve.wait_ge(s3_sq, HALVES * (THIRDS * k + b) + h + 1)
                    dve.tensor_tensor(squares[h][:, 0, :], squares[h][:, 0, :], squares[h][:, 1, :], ALU.add).then_inc(s3_sum, 1)

            def query_max(k, b):
                for jj in range(2):
                    dve.wait_ge(s3_q, 2 * (THIRDS * k + b) + jj + 1)
                    dve.tensor_reduce(qmax[:, 2 * jj:2 * jj + 2, :, b], ps[:, (6 if b == 1 else 4) + jj, :].rearrange("p (j g m) -> p j m g", j=2, m=GROUPS),
                                      AX.X, ALU.max).then_inc(s3_qmax, 1)

            def gate_of(k):
                dve.wait_ge(s3_qmax, 2 * THIRDS * (k + 1))
                if not isinstance(k, int) or k >= 1:
                    dve.wait_ge(s3_gated, THIRDS * k)
                dve.tensor_reduce(qm[:, :, :], qmax[:, :, :, :].rearrange("p j m b -> p j (m b)").rearrange("p j (a r) -> p j r a", a=THIRDS),
                                  AX.X, ALU.max).then_inc(s3_qsteps, 1)
                dve.wait_ge(s3_qsteps, k + 1)
                for a in range(THIRDS):
                    ins = dve.tensor_scalar(gate[:, :, a * GROUPS:(a + 1) * GROUPS], qm[:, :, :], 1.0, None, ALU.add)
                ins.then_inc(s3_gate, 1)

            def row(k, b, j):
                return rows[:, b, bass.ds(TPC * k + j, 1), :].rearrange("p k n -> p (k n)")

            def statistics(k, b):
                if isinstance(k, int) and k == STEPS - 1 and b == THIRDS - 1:
                    dve.wait_ge(s3_dx1, 1)
                else:
                    dve.wait_ge(s3_x1, THIRDS * k + b + 1)
                for j in range(TPC):
                    ins = dve.bn_stats(stats[:, TPC * b + j, :], row(k, b, j)[:, 0:C])
                if b == THIRDS - 1:
                    ins.then_inc(s3_stats, 1)

            def by_third(v):
                return v.rearrange("p (b j) -> p b j", b=THIRDS)

            def tails(k):
                rstd(k, s3_stats, N3, s3_sd)
                tail = rows[:, :, bass.ds(TPC * k, TPC), C:ROW]
                dve.tensor_copy(tail[:, :, :, 0], by_third(small[:, 4, :]))
                dve.scalar_tensor_tensor(tail[:, :, :, 1], by_third(mean), -1.0, by_third(small[:, 4, :]), ALU.mult, ALU.mult)
                dve.tensor_scalar(tail[:, :, :, 2], by_third(small[:, 4, :]), 1.0, None, ALU.add).then_inc(s3_tail, 1)

            def router_sum(k, b):
                if b == 0:
                    dve.wait_ge(s3_stats, N3 * k + 4)
                if not (isinstance(k, int) and k == 0 and b == 0):
                    dve.wait_ge(s3_w, THIRDS * k + b)
                for j in range(TPC):
                    t = TPC * b + j
                    ins = dve.scalar_tensor_tensor(unused[:, j, :],
                                                   row(k, b, j)[:, 0:C], mean[:, t:t + 1], wr_s[:, :],
                                                   ALU.subtract, ALU.mult, accum_out=small[:, 7, t:t + 1])
                ins.then_inc(s3_w, 1)

            def gate_add_last():
                k, b = STEPS - 1, THIRDS - 1
                dve.wait_ge(s3_gate, STEPS)
                dve.wait_ge(s1_biased, NCHUNK)
                r = rows[:, b, TPC * k:TPC * (k + 1), 0:C]
                r4 = r.rearrange("p j (g m) -> p j g m", m=GROUPS)
                dve.tensor_tensor(r4, r4, gate_of_third(b), ALU.mult).then_inc(s3_dgated, 1)
                dve.wait_ge(x_back[b], 16 * STEPS)
                dve.wait_ge(s3_dgated, 1)
                dve.tensor_tensor(r, r, x_again[b].rearrange("p (j c) -> p j c", c=C), ALU.add).then_inc(s3_dx1, 1)

            def router(k):
                dve.wait_ge(s3_w, THIRDS * (k + 1))
                dve.tensor_tensor(small[:, 13, :], small[:, 7, :], small[:, 4, :], ALU.mult).then_inc(s3_wsteps, 1)
                dve.wait_ge(s3_wsteps, k + 1)
                dve.tensor_scalar(rows[:, :, bass.ds(TPC * k, TPC), C + 3], by_third(small[:, 13, :]), br_s[:, 0:1], None, ALU.add)
                dve.tensor_scalar(w_all[:, :].rearrange("p (b t) -> p b t", b=THIRDS)[:, :, bass.ds(TPC * k, TPC)], by_third(small[:, 13, :]),
                                  br_s[:, 0:1], None, ALU.add).then_inc(s3_rows, 1)

            def stage3(k, query=True, value=True, weigh=True, ahead=True):
                if not query and value:
                    statistics(k - 2, THIRDS - 1)
                    moments(k - 2, EPS_T, s3_stats, N3)
                    gate_add_last()
                for b in range(THIRDS):
                    if query:
                        if b + 2 < THIRDS:
                            add_squares(k, b + 1)
                        elif ahead and b == THIRDS - 1:
                            add_squares(k + 1, 0)
                    if weigh:
                        if b == 0 and (query or not value):
                            statistics(k - 2, THIRDS - 1)
                            moments(k - 2, EPS_T, s3_stats, N3)
                        if b == 1:
                            tails(k - 2)
                        router_sum(k - 2, b)
                    if query:
                        query_max(k, b)
                    if value and b > 0:
                        statistics(k - 1, b - 1)
                if weigh:
                    router(k - 2)
                if query:
                    gate_of(k)

            add_squares(0, 0)
            stage3(0, value=False, weigh=False)
            stage3(1, weigh=False)
            with dve.Fori(2, STEPS - 1) as k:
                stage3(k)
            stage3(STEPS - 1, ahead=False)
            stage3(STEPS, query=False)
            stage3(STEPS + 1, query=False, value=False)

            count = [0]

            def link(*ins):
                count[0] += 1
                ins[-1].then_inc(s4_step, 1)
                dve.wait_ge(s4_step, count[0])

            totals = [0]

            def total(width):
                totals[0] += 1
                dve.wait_ge(s4_tot, totals[0])
                return ps[:, 0, 0:width]

            dve.wait_ge(s3_rows, STEPS)
            sign, target, wstar, need = (sc4[:, i:i + 1] for i in range(4))
            link(dve.tensor_scalar(u_w, w_all[:, :], 0.0, 0.0, ALU.is_ge, ALU.add, accum_out=cnt_f[:, 0:1]))
            dve.tensor_copy(cnt_b[:, 0:1], cnt_f[:, 0:1]).then_inc(s4_cnt, 1)
            link(dve.tensor_scalar(sc4[:, 4:5], total(1), float(KEEP), None, ALU.is_ge))
            link(dve.tensor_scalar(sign, sc4[:, 4:5], 2.0, -1.0, ALU.mult, ALU.add))
            link(dve.tensor_scalar(target, sc4[:, 4:5], float(2 * KEEP - PIX - 1), float(PIX - KEEP + 1), ALU.mult, ALU.add))
            link(dve.tensor_scalar(u_w, w_all[:, :], sign, None, ALU.mult))
            link(dve.tensor_copy(cand[0], ci[:, 0, :]))
            for r in range(len(SHIFTS)):
                c = cand[r % 2].bitcast(f32)
                link(dve.tensor_tensor(cmp_t, u_w.rearrange("p (a t) -> p a t", a=1).broadcast_to([P, CAND, TILES]),
                                       c.rearrange("p (j a) -> p j a", a=1).broadcast_to([P, CAND, TILES]), ALU.is_ge))
                with nc.allow_low_precision(reason="a partition's count is at most 72, exact in bfloat16"):
                    dve.tensor_reduce(cnt_b, cmp_t, AX.X, ALU.add).then_inc(s4_cnt, 1)
                link(dve.tensor_scalar(passed, total(CAND), target, -1.0, ALU.is_ge, ALU.mult))
                link(dve.tensor_tensor(masked, passed, cand[r % 2], ALU.bitwise_and))
                link(dve.tensor_reduce(prefix.bitcast(f32), masked.bitcast(f32), AX.X, ALU.max))
                if r + 1 < len(SHIFTS):
                    link(dve.tensor_tensor(cand[(r + 1) % 2], prefix.broadcast_to([P, CAND]), ci[:, r + 1, :], ALU.bitwise_or))
            link(dve.tensor_scalar(wstar, prefix.bitcast(f32), sign, None, ALU.mult))
            link(dve.tensor_scalar(gt_m, w_all[:, :], wstar, 0.0, ALU.is_gt, ALU.add, accum_out=cnt_f[:, 0:1]),
                 dve.tensor_scalar(eq_m, w_all[:, :], wstar, None, ALU.is_equal))
            link(dve.tensor_reduce(cnt_f[:, 1:4], eq_m.rearrange("p (b t) -> p b t", b=THIRDS), AX.X, ALU.add))
            dve.tensor_copy(cnt_b[:, 0:4], cnt_f[:, 0:4]).then_inc(s4_cnt, 1)
            tot = total(8)
            link(dve.tensor_copy(cnt_f[:, 0:8], tot))
            link(dve.tensor_scalar(need, cnt_f[:, 0:1], -1.0, float(KEEP), ALU.mult, ALU.add),
                 dve.tensor_tensor(cnt_f[:, 6:7], cnt_f[:, 6:7], cnt_f[:, 1:2], ALU.add),
                 dve.tensor_tensor(cnt_f[:, 7:8], cnt_f[:, 7:8], cnt_f[:, 1:2], ALU.add))
            link(dve.tensor_tensor(cnt_f[:, 7:8], cnt_f[:, 7:8], cnt_f[:, 2:3], ALU.add))
            thirds_of = [slice(b * COLS, (b + 1) * COLS) for b in range(THIRDS)]
            link(*[dve.tensor_tensor_scan(rank_t[:, s], ones_t[:, s], eq_m[:, s], cnt_f[:, 5 + b:6 + b], ALU.mult, ALU.add)
                   for b, s in enumerate(thirds_of)])
            link(dve.scalar_tensor_tensor(tmp_t, rank_t, need, eq_m, ALU.is_le, ALU.mult))
            link(dve.tensor_tensor(sel_t, tmp_t, gt_m, ALU.add))
            link(dve.tensor_reduce(cnt_f[:, 0:1], sel_t, AX.X, ALU.add))
            dve.tensor_copy(cnt_b[:, 0:1], cnt_f[:, 0:1]).then_inc(s4_cnt, 1)
            tot = total(8)
            link(dve.tensor_copy(cnt_f[:, 0:8], tot))
            link(dve.tensor_tensor_scan(rank_t, ones_t, sel_t, cnt_f[:, 4:5], ALU.mult, ALU.add))
            link(dve.tensor_tensor(rank_t, rank_t, sel_t, ALU.mult),
                 dve.tensor_scalar(tmp_t, sel_t, float(-NOSLOT - 1), float(NOSLOT), ALU.mult, ALU.add))
            link(dve.tensor_tensor(slot_i, rank_t, tmp_t, ALU.add))
            dve.tensor_single_scalar(hi_i, slot_i, 7, ALU.arith_shift_right)
            link(dve.tensor_single_scalar(lo_i, slot_i, P - 1, ALU.bitwise_and))
            dve.tensor_copy(hi_b, hi_i)
            link(dve.tensor_copy(lo_f, lo_i))
            dve.tensor_tensor(oh_hi, constb("iota")[:, 0:FT].rearrange("p (a s) -> p a s", a=1).broadcast_to([P, TILES, FT]), by_tile(hi_b),
                              ALU.is_equal).then_inc(s4_hi, 1)
            dve.wait_ge(s4_hi, 1)
            dve.tensor_scalar(oh_id[:, :, FT:2 * FT], oh_hi, const("part"), None, ALU.mult)
            for t in range(TILES):
                ins = dve.tensor_scalar(oh_lo[:, t, :], constb("iota"), lo_f[:, t:t + 1], None, ALU.is_equal)
                if t % TPS == TPS - 1:
                    ins.then_inc(s4_hot, 1)
            dve.wait_ge(s4_ids, 1)
            dve.tensor_copy(id_t, ps[:, 1, 0:FT])
            link(dve.tensor_copy(id_p, ps[:, 1, FT:2 * FT]))
            thirds = float(COLS * (P - 1))
            dve.tensor_scalar(id_1, id_t, float(COLS), thirds, ALU.is_ge, ALU.mult)
            dve.tensor_scalar(id_2, id_t, float(2 * COLS), thirds, ALU.is_ge, ALU.mult)
            link(dve.scalar_tensor_tensor(id_3, id_p, float(COLS), id_t, ALU.mult, ALU.add))
            link(dve.tensor_tensor(id_1, id_1, id_2, ALU.add))
            dve.tensor_tensor(idx[:, :], id_1, id_3, ALU.add).then_inc(s4_idx, 1)

            def later(f, b, n):
                return f + (b + n) // THIRDS, (b + n) % THIRDS

            def rows_in(f, b):
                c = THIRDS * f + b
                first = isinstance(c, int) and c == 0
                if b > 0:
                    dve.wait_ge(got_in[b], 16 * TPC * (f + 1))
                elif not first:
                    dve.wait_ge(got_in[b], 16 * TPC * f)
                if not isinstance(c, int) or c >= 1:
                    dve.wait_ge(s5_tr, 2 * c)
                for j in range(TPC):
                    if first:
                        dve.wait_ge(tile_in[j], 16)
                    ins = dve.tensor_scalar(ln_tok[:, j, :], got[b][:, j, 0:C], got[b][:, j, C:C + 1], got[b][:, j, C + 1:C + 2], ALU.mult, ALU.add)
                ins.then_inc(s5_ln, 1)

            def low(f, b):
                dve.wait_ge(s5_lnhi, THIRDS * f + b + 1)
                dve.tensor_tensor(lnt_lo[:, :, :], ln_tok[:, :, :], lnt_hi[:, :, :].bitcast(f32), ALU.subtract).then_inc(s5_lnlo, 1)

            def unrouted(f, b):
                c = THIRDS * f + b
                dve.wait_ge(s5_ln, THIRDS * f + b + 1)
                for j in range(TPC):
                    ins = dve.tensor_scalar(got[b][:, j, 0:C], got[b][:, j, 0:C], got[b][:, j, C + 2:C + 3], got[b][:, j, C + 1:C + 2], ALU.mult, ALU.add)
                ins.then_inc(s5_unr, 1)
                dve.wait_ge(s5_unr, c + 1)
                for j in range(TPC):
                    ins = dve.scalar_tensor_tensor(got[b][:, j, 0:C], b2_s[:, :], got[b][:, j, C + 3:C + 4], got[b][:, j, 0:C], ALU.mult, ALU.add)
                ins.then_inc(s5_base, 1)

            def channels(f, b):
                c = THIRDS * f + b
                dve.wait_ge(s5_tr, 2 * c + 1)
                dve.tensor_copy(ln_hi[b][:, :, :], ps[:, 0:2, :]).then_inc(s5_chhi, 1)

            def splits(f, b, ts):
                n0 = HT * (THIRDS * f + b)
                for t in ts:
                    dve.wait_ge(s5_gelu, n0 + t + 1)
                    dve.tensor_copy(hid_hi[b][:, t, :], act_out[:, t % 4, :]).then_inc(s5_hi, 1)
                    dve.wait_ge(s5_hi, n0 + t + 1)
                    dve.tensor_tensor(hid_lo[b][:, t, :], act_out[:, t % 4, :], hid_hi[b][:, t, :].bitcast(f32), ALU.subtract).then_inc(s5_split, 1)

            def place_idx(f, b, ahead=True):
                if not isinstance(f, int) or f >= 1:
                    dve.wait_ge(scat[b], 16 * TPC * f)
                ins = dve.tensor_copy(idx_put[:, b, :], idx[:, bass.ds(TPS * f + TPC * b, TPC)])
                if ahead:
                    ins = dve.tensor_copy(idx_get[:, b, :], idx[:, bass.ds(TPS * (f + 1) + TPC * b, TPC)])
                ins.then_inc(s5_idx, 1)

            def result(f, b, jj):
                c = THIRDS * f + b
                if jj == 0:
                    pf, pb = later(f, b, -1)
                    if not isinstance(c, int) or c >= 1:
                        dve.wait_ge(scat[pb], 16 * TPC * (pf + 1))
                dve.wait_ge(s5_base, c + 1)
                dve.wait_ge(s5_y, 2 * c + jj + 1)
                for j in (2 * jj, 2 * jj + 1):
                    ins = dve.scalar_tensor_tensor(res[:, j, :], ps[:, 4 + jj, (j % 2) * C:(j % 2 + 1) * C], got[b][:, j, C + 3:C + 4],
                                                   got[b][:, j, 0:C], ALU.mult, ALU.add)
                ins.then_inc(s5_res, 1)

            def stage5(f, b, one=True, two=True):
                if one:
                    splits(*later(f, b, 1), range(HT))
                if two:
                    rows_in(*later(f, b, 2))
                    low(*later(f, b, 2))
                place_idx(f, b, ahead=not isinstance(f, int) or f < FSTEPS - 1)
                result(f, b, 0)
                if two:
                    channels(*later(f, b, 2))
                    unrouted(*later(f, b, 2))
                result(f, b, 1)

            dve.wait_ge(s4_idx, 1)
            dve.wait_ge(table_out, 16 * NCHUNK)
            dve.wait_ge(base_out, 16 * NCHUNK)
            dve.tensor_copy(idx_get[:, :, :].rearrange("p b j -> p (b j)"), idx[:, 0:TPS]).then_inc(s5_idx, 1)
            dve.tensor_copy(ident_r[:, :], ident).then_inc(ident_in, 1)
            rows_in(0, 0)
            low(0, 0)
            channels(0, 0)
            rows_in(0, 1)
            low(0, 1)
            unrouted(0, 0)
            splits(0, 0, range(0, 6))
            channels(0, 1)
            unrouted(0, 1)
            splits(0, 0, range(6, HT))
            for b in range(THIRDS):
                stage5(0, b)
            with dve.Fori(1, FSTEPS - 1) as f:
                for b in range(THIRDS):
                    stage5(f, b)
            for b in range(THIRDS):
                stage5(FSTEPS - 1, b, one=b + 1 < THIRDS, two=b + 2 < THIRDS)

        @block.tensor
        def _(pe):
            def product(k, b, lhs, banks, w, bias, ready, done, used):
                for jj in range(2):
                    for j in (2 * jj, 2 * jj + 1):
                        o = ps[:, banks[jj], (j % 2) * C:(j % 2 + 1) * C]
                        if j % 2 == 0:
                            used(jj)
                        if bias is not None:
                            pe.matmul(o, constb("ones")[0:3, :], bias, start=True, stop=False)
                        for h in range(HALVES):
                            if jj == 0 and j == 0:
                                ready(h)
                            ins = pe.matmul(o, lhs[:, h * CHUNK + j * P:h * CHUNK + (j + 1) * P], w[:, h, :], start=bias is None and h == 0, stop=h == HALVES - 1)
                    ins.then_inc(done, 1)

            def later(k, b, n):
                return k + (b + n) // THIRDS, (b + n) % THIRDS

            def transpose1(k, b):
                pe.wait_ge(s1_vtok, THIRDS * k + b + 1)
                if not isinstance(k, int) or k >= 1:
                    pe.wait_ge(s1_vst, THIRDS * (k - 1) + b + 1)
                for h in range(HALVES):
                    for j in range(TPC):
                        ins = pe.transpose(ps[:, 2 * b + h, j * P:(j + 1) * P], v_tok[b][:, j, h * P:(h + 1) * P], ident)
                ins.then_inc(s1_tr, 1)

            def value(k, b):
                product(k, b, v_st[b], (6, 7), wv_s, None, lambda h: pe.wait_ge(s1_vst, THIRDS * k + b + 1), s1_val,
                        lambda jj: None if isinstance(k, int) and k == 0 and b == 0 else pe.wait_ge(s1_out, 2 * (THIRDS * k + b - 1) + jj + 1))

            def stage1(k):
                for b in range(THIRDS):
                    transpose1(*later(k, b, 1))
                    value(k, b)

            pe.wait_ge(first_in, 16 * 2)
            transpose1(0, 0)
            stage1(0)
            with pe.Fori(1, STEPS - 1) as k:
                stage1(k)
            transpose1(STEPS - 1, 1)
            transpose1(STEPS - 1, 2)
            value(STEPS - 1, 0)

            pe.wait_ge(s1_mm, NCHUNK + 3)
            for i, a in enumerate((a_max, a_min)):
                for h in range(HALVES):
                    n = HALVES * i + h
                    ins = pe.transpose(ps[:, 1, n * P:(n + 1) * P], a[:, h * P:(h + 1) * P], ident)
            ins.then_inc(s1_extt, 1)
            pe.wait_ge(s1_scale, 1)
            for i in range(2 * HALVES):
                ins = pe.transpose(ps[:, 0, i * P:(i + 1) * P], fin_wide[:, i, :], ident)
            ins.then_inc(s1_rows, 1)
            for b in range(1, THIRDS):
                value(STEPS - 1, b)

            def fourier(k, b, first=False, last=False):
                pe.wait_ge(s2_q, THIRDS * k + b + 1)
                for j in range(TPC):
                    ins = pe.matmul(ps[0:3 * NFUN, 5, 0:C], fwd[:, bass.ds(COLS * b + TPC * k + j, 1), :].rearrange("p k m -> p (k m)"),
                                    q_tok[b][:, j * C:(j + 1) * C], start=first and j == 0, stop=last and j == TPC - 1)
                ins.then_inc(s2_dft, 1)

            pe.wait_ge(fwd_in, 16)
            for b in range(THIRDS):
                fourier(0, b, first=b == 0)
            with pe.Fori(1, STEPS - 1) as k:
                for b in range(THIRDS):
                    fourier(k, b)
            for b in range(THIRDS):
                fourier(STEPS - 1, b, last=b == THIRDS - 1)

            pe.wait_ge(s2_sums, 1)
            for i in range(2):
                pe.matmul(ps[:, i, 0:C], const(f"sel_{i}")[0:3 * NFUN, :], sums, start=True, stop=True).then_inc(s2_coef, 1)
            pe.wait_ge(s2_done, 1)

            def invert(k, b):
                pe.wait_ge(inv_in[b], 16 * (k + 1))
                for h in range(HALVES):
                    if not (isinstance(k, int) and k == 0 and b == 0):
                        pe.wait_ge(s3_sq, HALVES * (THIRDS * k + b - 1) + h + 1)
                    cs = slice(h * P, (h + 1) * P)
                    pe.matmul(ps[:, 2 * h, :], coef[:, 0, cs], inv[b][:, 0, :], start=True, stop=False)
                    pe.matmul(ps[:, 2 * h, :], coef[R2_AT:R2_AT + R2, 1, cs], inv[b][R2_AT:R2_AT + R2, 1, :], start=False, stop=True)
                    pe.matmul(ps[:, 2 * h + 1, :], coef[0:RI, 1, cs], inv[b][0:RI, 1, :], start=True, stop=True).then_inc(s3_ri, 1)

            def query(k, b):
                c = THIRDS * k + b
                last = (c - 1, c - 3, c - 2)[b]

                def used(jj):
                    if not isinstance(k, int) or last >= 0:
                        pe.wait_ge(s3_qmax, 2 * last + jj + 1)

                product(k, b, mag[b], (6, 7) if b == 1 else (4, 5), wq_s, bq_s[:, :], lambda h: pe.wait_ge(s3_mag, HALVES * c + h + 1), s3_q, used)

            def stage3(k, ahead=True):
                for b in range(THIRDS):
                    if b + 1 < THIRDS:
                        invert(k, b + 1)
                    elif ahead:
                        invert(k + 1, 0)
                    query(k, b)

            pe.wait_ge(consts_in, 16 * 7)
            pe.wait_ge(bias_parts, 8)
            invert(0, 0)
            stage3(0)
            with pe.Fori(1, STEPS - 1) as k:
                stage3(k)
            stage3(STEPS - 1, ahead=False)

            n_rounds = len(SHIFTS)
            for i in range(n_rounds + 3):
                pe.wait_ge(s4_cnt, i + 1)
                width = 1 if i == 0 else CAND if i <= n_rounds else 4
                prefixes = i > n_rounds
                ins = pe.matmul(ps[:, 0, 0:width], constb("ones"), cnt_b[:, 0:width], start=True, stop=True)
                if prefixes:
                    ins = pe.matmul(ps[:, 0, 4:8], constb("tri"), cnt_b[:, 0:4], start=True, stop=True)
                ins.then_inc(s4_tot, 1)
            pe.wait_ge(s4_oht, 1)
            for t in range(TILES):
                if t % TPS == 0:
                    pe.wait_ge(s4_hot, t // TPS + 1)
                ins = pe.matmul(ps[:, 1, 0:2 * FT], oh_lo[:, t, :], oh_id[:, t, :], start=t == 0, stop=t == TILES - 1)
            ins.then_inc(s4_ids, 1)

            def transpose5(f, b):
                c = THIRDS * f + b
                for part_, src, ready, used, bank in ((0, lnt_hi, s5_lnhi, s5_chhi, 0), (1, lnt_lo, s5_lnlo, s5_chlo, 6)):
                    pe.wait_ge(ready, c + 1)
                    if not isinstance(c, int) or c >= 1:
                        pe.wait_ge(used, c)
                    for h in range(HALVES):
                        for j in range(TPC):
                            ins = pe.transpose(ps[:, bank + h, j * P:(j + 1) * P].bitcast(f32r), src[:, j, h * P:(h + 1) * P], ident_r[:, :])
                    ins.then_inc(s5_tr, 1)

            def hidden(f, b):
                c = THIRDS * f + b
                pe.wait_ge(s5_chhi, c + 1)
                pe.wait_ge(s5_chlo, c + 1)
                for t in range(HT):
                    n = HT * c + t
                    if not isinstance(n, int) or n >= 2:
                        pe.wait_ge(s5_gelu, n - 1)
                    o = ps[:, 2 + t % 2, :]
                    ws = slice(t * P, (t + 1) * P)
                    products = [(w, x, h) for h in range(HALVES) for w, x in ((w1_hi, ln_hi), (w1_hi, ln_lo), (w1_lo, ln_hi))]
                    for i, (w, x, h) in enumerate(products):
                        ins = pe.matmul(o, w[:, h, ws], x[b][:, h, :], start=i == 0, stop=i == len(products) - 1)
                    ins.then_inc(s5_h, 1)

            def second(f, b, jj):
                c = THIRDS * f + b
                pe.wait_ge(s5_split, HT * (c + 1))
                if not isinstance(c, int) or c >= 1:
                    pe.wait_ge(s5_res, 2 * (c - 1) + jj + 1)
                for j in (2 * jj, 2 * jj + 1):
                    o = ps[:, 4 + jj, (j % 2) * C:(j % 2 + 1) * C]
                    for t in range(HT):
                        js = slice(j * P, (j + 1) * P)
                        for x, w in ((hid_hi, w2_hi), (hid_hi, w2_lo), (hid_lo, w2_hi)):
                            last = t == HT - 1 and x is hid_lo
                            ins = pe.matmul(o, x[b][:, t, js], w[:, t, :], start=t == 0 and x is hid_hi and w is w2_hi, stop=last)
                ins.then_inc(s5_y, 1)

            def stage5(f, b, one=True, two=True):
                if one:
                    hidden(*later(f, b, 1))
                second(f, b, 0)
                if two:
                    transpose5(*later(f, b, 2))
                second(f, b, 1)

            pe.wait_ge(ident_in, 1)
            transpose5(0, 0)
            pe.wait_ge(w_parts, 2)
            hidden(0, 0)
            transpose5(0, 1)
            for b in range(THIRDS):
                stage5(0, b)
            with pe.Fori(1, FSTEPS - 1) as f:
                for b in range(THIRDS):
                    stage5(f, b)
            for b in range(THIRDS):
                stage5(FSTEPS - 1, b, one=b + 1 < THIRDS, two=b + 2 < THIRDS)


def bases():
    bf = mybir.dt.np(mybir.dt.bfloat16)
    pairs, lone = frequencies()
    pix = np.arange(PIX)
    y, x = pix // SIDE, pix % SIDE
    funs = [np.ones(PIX)]
    for u, v in pairs + lone:
        turn = 2 * np.pi * ((u * y + v * x) % SIDE) / SIDE
        funs += [np.cos(turn), np.sin(turn)]
    funs = np.stack(funs)

    def parts(a):
        out_, rest = [], a.astype(np.float64)
        for _ in range(3):
            p_ = rest.astype(bf)
            out_.append(p_)
            rest = rest - p_.astype(np.float64)
        return out_

    fp = np.stack(parts(funs))
    cube = fp.reshape(3, NFUN, THIRDS, P, COLS)
    fwd = np.ascontiguousarray(cube.transpose(3, 2, 4, 0, 1)).reshape(P, TILES * 3 * NFUN)
    flat = cube.reshape(3, NFUN, THIRDS, P, STEPS, TPC).transpose(0, 1, 2, 4, 5, 3).reshape(3, NFUN, THIRDS, STEPS, CHUNK)
    inv = np.zeros((THIRDS, STEPS, P, 2, CHUNK), bf)
    for r, (i, _, b) in enumerate(REAL_ROWS[:P]):
        inv[:, :, r, 0] = flat[b, i]
    n0 = 1 + 2 * len(pairs)
    for r, (i, _, b) in enumerate(IMAG_ROWS):
        inv[:, :, r, 1] = flat[b, n0 + i]
    const = np.zeros((P, NCF), np.float32)

    def put(name, rows_, cols, val):
        const[rows_, CF[name][0] + cols] = val

    for p_ in range(P):
        put("ident", p_, p_, 1.0)
    n = float(PIX)
    for r, (i, a, _) in enumerate(REAL_ROWS):
        name, col = ("sel_0", r) if r < P else ("sel_1", R2_AT + r - P)
        mask = "mask_0" if r < P else "mask_1"
        w = (2.0 if 0 < i < n0 else 1.0) / n
        for part_ in range(3):
            put(name, part_ * NFUN + i, col, w)
        put(mask, col, a, 1.0)
        if r >= P:
            inv[:, :, col, 1] = flat[REAL_ROWS[r][2], i]
    for r, (i, a, _) in enumerate(IMAG_ROWS):
        src, w = (i - 1, 1.0 / n) if i % 2 else (i + 1, -1.0 / n)
        for part_ in range(3):
            put("sel_1", part_ * NFUN + n0 + src, r, w)
        put("mask_1", r, a, 1.0)
    for part_ in range(3):
        put("mask_b", part_, part_, 1.0)
    const[:, CF["part"][0]] = np.arange(P)
    const[:, CF["magic"][0]] = -MAGIC
    digits = np.zeros((P, len(SHIFTS), CAND), np.int32)
    for r, s in enumerate(SHIFTS):
        digits[:, r, :] = [(j << s) if (s or j < 2) else 0 for j in range(CAND)]
    cb = np.zeros((P, NCB), np.float32)
    cb[:, 0:P] = 1.0
    cb[:, P:2 * P] = np.arange(P)[:, None] < np.arange(P)[None, :]
    cb[:, 2 * P:3 * P] = np.arange(P)[None, :]
    return fwd, inv, const, digits, cb.astype(bf)


def kernel(**inputs):
    import numpy as _np
    import concourse.bacc as _bacc
    from concourse import mybir as _mybir
    from concourse.bass_utils import run_bass_kernel_spmd as _run

    a = {k: _np.asarray(v) for k, v in inputs.items()}
    fwd, inv, const, digits, cb = bases()
    arrays = {
        "x": a["x"].reshape(C, PIX).T,
        "wq": a["L0_conv_Wq"].T,
        "wv": a["L0_conv_Wv"].T,
        "bq": _np.broadcast_to(a["L0_conv_bq"].reshape(1, C), (3, C)),
        "bv": _np.broadcast_to(a["L0_conv_bv"].reshape(1, C), (P, C)),
        "wr": _np.broadcast_to(a["L0_ffn_wr"].reshape(1, C), (P, C)),
        "b2": _np.broadcast_to(a["L0_ffn_b2"].reshape(1, C), (P, C)),
        "br": _np.broadcast_to(a["L0_ffn_br"].reshape(1, 1), (P, 1)),
        "w1": a["L0_ffn_w1"],
        "b1": a["L0_ffn_b1"].reshape(HT, P).T,
        "w2": a["L0_ffn_w2"],
        "const_f": const, "const_i": digits, "const_b": cb, "fwd_basis": fwd, "inv_basis": inv,
    }
    nc = _bacc.Bacc("TRN2", target_bir_lowering=False, num_devices=1)
    feeds, args = {}, []
    for name, arr in arrays.items():
        arr = _np.ascontiguousarray(arr)
        feeds["in_" + name] = arr
        args.append(nc.dram_tensor("in_" + name, arr.shape, _mybir.dt.from_np(arr.dtype), kind="ExternalInput").ap())
    args.append(nc.dram_tensor("out_tokens", (PIX, C), _mybir.dt.float32, kind="ExternalOutput").ap())
    layer_kernel(nc, *args)
    r = _run(nc, [feeds], core_ids=[0])
    got = r.results[0]["out_tokens"]
    return _np.ascontiguousarray(got.T).reshape(1, C, SIDE, SIDE)
```
